# Optimizing a Trainium2 kernel written in Bass

```python
import numpy as np
import jax
import jax.numpy as jnp

def _softmax(x, axis=-1):
    return jax.nn.softmax(x, axis=axis)

def _gelu(x):
    return jax.nn.gelu(x, approximate=True)

def _silu(x):
    return jax.nn.silu(x)

def _sigmoid(x):
    return jax.nn.sigmoid(x)

def _layernorm(x, axis=-1, eps=1e-05):
    m = jnp.mean(x, axis=axis, keepdims=True)
    v = jnp.var(x, axis=axis, keepdims=True)
    return (x - m) / jnp.sqrt(v + eps)

def _scatter_add(tgt, idx, src, axis=0):
    return tgt.at[idx].add(src)

def _segment_sum(src, seg, n):
    return jax.ops.segment_sum(src, seg, n)
kernel_name = 'mk_seq_postln_d2_jaxref_r8_4fcd9f'

def setup_inputs(seed: int=0):
    np.random.seed(seed)
    _w = jnp.asarray

    def _L0_attn_setup():
        import jax, jax.numpy as jnp
        import numpy as np
        B, S, H = (8, 256, 128)
        key = jax.random.key(seed)
        k1, k2, k3 = jax.random.split(key, 3)
        x = jax.random.normal(k1, (B, S, H), dtype=jnp.float32)
        W_qkv = jax.random.normal(k2, (3 * H, H), dtype=jnp.float32) / np.sqrt(H)
        W_out = jax.random.normal(k3, (H, H), dtype=jnp.float32) / np.sqrt(H)
        return {'x': x, 'W_qkv': W_qkv, 'W_out': W_out}
    _L0_attn_in = _L0_attn_setup()

    def _L0_ffn_setup():
        import jax, jax.numpy as jnp
        import numpy as np
        D_MODEL = 128
        N_EXPERTS = 8
        TOP_K = 2
        HIDDEN = 4 * D_MODEL
        key = jax.random.key(seed)
        ks = jax.random.split(key, 6)
        B, S = (2, 256)
        x = jax.random.normal(ks[0], (B, S, D_MODEL), dtype=jnp.float32)
        shared_w1 = jax.random.normal(ks[1], (HIDDEN, D_MODEL), dtype=jnp.float32) * 0.02
        shared_w2 = jax.random.normal(ks[2], (D_MODEL, HIDDEN), dtype=jnp.float32) * 0.02
        experts_w1 = jax.random.normal(ks[3], (N_EXPERTS, HIDDEN, D_MODEL), dtype=jnp.float32) * 0.02
        experts_w2 = jax.random.normal(ks[4], (N_EXPERTS, D_MODEL, HIDDEN), dtype=jnp.float32) * 0.02
        gate_w = jax.random.normal(ks[5], (N_EXPERTS, D_MODEL), dtype=jnp.float32) * 0.02
        return {'x': x, 'shared_w1': shared_w1, 'shared_w2': shared_w2, 'experts_w1': experts_w1, 'experts_w2': experts_w2, 'gate_w': gate_w}
    _L0_ffn_in = _L0_ffn_setup()

    def _L1_attn_setup():
        import jax, jax.numpy as jnp
        import numpy as np
        D_MODEL, N_STATE, E_INNER, K_CONV, DT_RANK = (128, 16, 256, 4, 64)
        EPS = 1e-06

        def _silu(x):
            return x * jax.nn.sigmoid(x)

        def _rmsnorm(x, w):
            var = jnp.mean(x * x, axis=-1, keepdims=True)
            return x * jax.lax.rsqrt(var + EPS) * w

        def _causal_dwconv(x, conv_w):
            xc = jnp.swapaxes(x, 1, 2)
            xc = jnp.pad(xc, ((0, 0), (0, 0), (K_CONV - 1, 0)))
            y = jax.lax.conv_general_dilated(xc, conv_w, window_strides=(1,), padding='VALID', dimension_numbers=('NCL', 'OIL', 'NCL'), feature_group_count=E_INNER)
            return jnp.swapaxes(y, 1, 2)

        def _selective_scan(u, delta, A, Bm, Cm, Dp):

            def step(h, inp):
                d_t, B_t, C_t, u_t = inp
                dA = jnp.exp(d_t[..., None] * A)
                h = dA * h + (d_t * u_t)[..., None] * B_t[:, None, :]
                y = jnp.einsum('ben,bn->be', h, C_t)
                return (h, y)
            h0 = jnp.zeros((u.shape[0], E_INNER, N_STATE), u.dtype)
            xs = (jnp.swapaxes(delta, 0, 1), jnp.swapaxes(Bm, 0, 1), jnp.swapaxes(Cm, 0, 1), jnp.swapaxes(u, 0, 1))
            h_last, ys = jax.lax.scan(step, h0, xs)
            return (jnp.swapaxes(ys, 0, 1) + u * Dp, h_last)

        def _reference_tuple_inner(hidden_states, norm_w, W_in, conv_w, W_x, W_dt, b_dt, A_log, D_param, W_out):
            residual = hidden_states
            x = _rmsnorm(hidden_states, norm_w)
            xz = jnp.einsum('bld,de->ble', x, W_in)
            x_in, z = jnp.split(xz, 2, axis=-1)
            x_act = _silu(_causal_dwconv(x_in, conv_w))
            x_db = jnp.einsum('ble,er->blr', x_act, W_x)
            dt_lr = x_db[..., :DT_RANK]
            Bm = x_db[..., DT_RANK:DT_RANK + N_STATE]
            Cm = x_db[..., DT_RANK + N_STATE:]
            delta = jax.nn.softplus(jnp.einsum('blr,re->ble', dt_lr, W_dt) + b_dt)
            A = -jnp.exp(A_log)
            y, h_last = _selective_scan(x_act, delta, A, Bm, Cm, D_param)
            y = y * _silu(z)
            out = jnp.einsum('ble,ed->bld', y, W_out)
            return (residual + out, h_last)
        key = jax.random.key(seed)
        ks = jax.random.split(key, 8)
        B, L = (4, 128)
        hidden_states = jax.random.normal(ks[0], (B, L, D_MODEL), jnp.float32)
        norm_w = jnp.ones((D_MODEL,), jnp.float32)
        W_in = jax.random.normal(ks[1], (D_MODEL, 2 * E_INNER), jnp.float32) * D_MODEL ** (-0.5)
        conv_w = jax.random.normal(ks[2], (E_INNER, 1, K_CONV), jnp.float32) * K_CONV ** (-0.5)
        W_x = jax.random.normal(ks[3], (E_INNER, DT_RANK + 2 * N_STATE), jnp.float32) * E_INNER ** (-0.5)
        W_dt = jax.random.normal(ks[4], (DT_RANK, E_INNER), jnp.float32) * DT_RANK ** (-0.5)
        dt = jnp.exp(jax.random.uniform(ks[5], (E_INNER,)) * (np.log(0.1) - np.log(0.001)) + np.log(0.001))
        b_dt = dt + jnp.log(-jnp.expm1(-dt))
        A_log = jnp.log(jnp.broadcast_to(jnp.arange(1, N_STATE + 1, dtype=jnp.float32), (E_INNER, N_STATE)))
        D_param = jnp.ones((E_INNER,), jnp.float32)
        W_out = jax.random.normal(ks[6], (E_INNER, D_MODEL), jnp.float32) * E_INNER ** (-0.5)
        return {'hidden_states': hidden_states, 'norm_w': norm_w, 'W_in': W_in, 'conv_w': conv_w, 'W_x': W_x, 'W_dt': W_dt, 'b_dt': b_dt, 'A_log': A_log, 'D_param': D_param, 'W_out': W_out}
    _L1_attn_in = _L1_attn_setup()

    def _L1_ffn_setup():
        import jax, jax.numpy as jnp
        import numpy as np
        B, S, D = (4, 256, 128)
        E, F, TOP_K = (8, 512, 2)
        key = jax.random.key(seed)
        ks = jax.random.split(key, 8)
        sc_d = 1.0 / np.sqrt(D)
        sc_f = 1.0 / np.sqrt(F)
        return {'hidden_states': jax.random.normal(ks[0], (B, S, D), jnp.float32), 'w_router': jax.random.normal(ks[1], (D, E), jnp.float32) * sc_d, 'w_gate': jax.random.normal(ks[2], (E, D, F), jnp.float32) * sc_d, 'w_up': jax.random.normal(ks[3], (E, D, F), jnp.float32) * sc_d, 'w_down': jax.random.normal(ks[4], (E, F, D), jnp.float32) * sc_f, 'ws_gate': jax.random.normal(ks[5], (D, F), jnp.float32) * sc_d, 'ws_up': jax.random.normal(ks[6], (D, F), jnp.float32) * sc_d, 'ws_down': jax.random.normal(ks[7], (F, D), jnp.float32) * sc_f}
    _L1_ffn_in = _L1_ffn_setup()
    _d = {'L0_attn_x': _L0_attn_in['x'], 'L0_attn_W_qkv': _L0_attn_in['W_qkv'], 'L0_attn_W_out': _L0_attn_in['W_out'], 'L0_ffn_shared_w1': _L0_ffn_in['shared_w1'], 'L0_ffn_shared_w2': _L0_ffn_in['shared_w2'], 'L0_ffn_experts_w1': _L0_ffn_in['experts_w1'], 'L0_ffn_experts_w2': _L0_ffn_in['experts_w2'], 'L0_ffn_gate_w': _L0_ffn_in['gate_w'], 'L1_attn_norm_w': _L1_attn_in['norm_w'], 'L1_attn_W_in': _L1_attn_in['W_in'], 'L1_attn_conv_w': _L1_attn_in['conv_w'], 'L1_attn_W_x': _L1_attn_in['W_x'], 'L1_attn_W_dt': _L1_attn_in['W_dt'], 'L1_attn_b_dt': _L1_attn_in['b_dt'], 'L1_attn_A_log': _L1_attn_in['A_log'], 'L1_attn_D_param': _L1_attn_in['D_param'], 'L1_attn_W_out': _L1_attn_in['W_out'], 'L1_ffn_w_router': _L1_ffn_in['w_router'], 'L1_ffn_w_gate': _L1_ffn_in['w_gate'], 'L1_ffn_w_up': _L1_ffn_in['w_up'], 'L1_ffn_w_down': _L1_ffn_in['w_down'], 'L1_ffn_ws_gate': _L1_ffn_in['ws_gate'], 'L1_ffn_ws_up': _L1_ffn_in['ws_up'], 'L1_ffn_ws_down': _L1_ffn_in['ws_down']}
    _x0 = _d['L0_attn_x']
    _d['L0_attn_x'] = jax.random.normal(jax.random.fold_in(jax.random.key(seed), 1), (4, 512, 128), dtype=_x0.dtype)
    del _x0
    return _d

def reference(L0_attn_x, L0_attn_W_qkv, L0_attn_W_out, L0_ffn_shared_w1, L0_ffn_shared_w2, L0_ffn_experts_w1, L0_ffn_experts_w2, L0_ffn_gate_w, L1_attn_norm_w, L1_attn_W_in, L1_attn_conv_w, L1_attn_W_x, L1_attn_W_dt, L1_attn_b_dt, L1_attn_A_log, L1_attn_D_param, L1_attn_W_out, L1_ffn_w_router, L1_ffn_w_gate, L1_ffn_w_up, L1_ffn_w_down, L1_ffn_ws_gate, L1_ffn_ws_up, L1_ffn_ws_down):

    def _L0_attn_ref(x, W_qkv, W_out):
        import jax, jax.numpy as jnp
        import numpy as np
        B, S, H = (8, 256, 128)
        h = x.shape[-1]
        scale = 1.0 / np.sqrt(h).astype(np.float32)
        y = jnp.einsum('bsh,oh->bso', x, W_qkv).reshape(*x.shape, 3)
        q, k, v = (y[..., 0], y[..., 1], y[..., 2])
        scores = jnp.einsum('bqh,bkh->bqk', q, k) * scale
        attn = jax.nn.softmax(scores, axis=-1)
        ctx = jnp.einsum('bqk,bkh->bqh', attn, v)
        out = jnp.einsum('bsh,oh->bso', ctx, W_out)
        return out

    def _L0_ffn_ref(x, shared_w1, shared_w2, experts_w1, experts_w2, gate_w):
        import jax, jax.numpy as jnp
        import numpy as np
        D_MODEL = 128
        N_EXPERTS = 8
        TOP_K = 2
        HIDDEN = 4 * D_MODEL
        B, S, D = x.shape
        T = B * S
        x_flat = x.reshape(T, D)
        shared = jnp.einsum('td,dh->th', x_flat, shared_w1.T)
        shared = jnp.einsum('th,hd->td', jax.nn.silu(shared), shared_w2.T)
        gate_logits = x_flat @ gate_w.T
        top_k_gates, top_k_idx = jax.lax.top_k(gate_logits, TOP_K)
        top_k_gates = jax.nn.softmax(top_k_gates, axis=1)
        gates = jnp.zeros((T, N_EXPERTS), dtype=x.dtype)
        gates = gates.at[jnp.arange(T)[:, None], top_k_idx].set(top_k_gates)
        h = jnp.einsum('td,ehd->teh', x_flat, experts_w1)
        expert_out = jnp.einsum('teh,edh->ted', jax.nn.silu(h), experts_w2)
        selected = jnp.einsum('ted,te->td', expert_out, gates)
        return (shared + selected).reshape(B, S, D)

    def _L1_attn_ref(hidden_states, norm_w, W_in, conv_w, W_x, W_dt, b_dt, A_log, D_param, W_out):
        import jax, jax.numpy as jnp
        import numpy as np
        D_MODEL, N_STATE, E_INNER, K_CONV, DT_RANK = (128, 16, 256, 4, 64)
        EPS = 1e-06

        def _silu(x):
            return x * jax.nn.sigmoid(x)

        def _rmsnorm(x, w):
            var = jnp.mean(x * x, axis=-1, keepdims=True)
            return x * jax.lax.rsqrt(var + EPS) * w

        def _causal_dwconv(x, conv_w):
            xc = jnp.swapaxes(x, 1, 2)
            xc = jnp.pad(xc, ((0, 0), (0, 0), (K_CONV - 1, 0)))
            y = jax.lax.conv_general_dilated(xc, conv_w, window_strides=(1,), padding='VALID', dimension_numbers=('NCL', 'OIL', 'NCL'), feature_group_count=E_INNER)
            return jnp.swapaxes(y, 1, 2)

        def _selective_scan(u, delta, A, Bm, Cm, Dp):

            def step(h, inp):
                d_t, B_t, C_t, u_t = inp
                dA = jnp.exp(d_t[..., None] * A)
                h = dA * h + (d_t * u_t)[..., None] * B_t[:, None, :]
                y = jnp.einsum('ben,bn->be', h, C_t)
                return (h, y)
            h0 = jnp.zeros((u.shape[0], E_INNER, N_STATE), u.dtype)
            xs = (jnp.swapaxes(delta, 0, 1), jnp.swapaxes(Bm, 0, 1), jnp.swapaxes(Cm, 0, 1), jnp.swapaxes(u, 0, 1))
            h_last, ys = jax.lax.scan(step, h0, xs)
            return (jnp.swapaxes(ys, 0, 1) + u * Dp, h_last)

        def _reference_tuple_inner(hidden_states, norm_w, W_in, conv_w, W_x, W_dt, b_dt, A_log, D_param, W_out):
            residual = hidden_states
            x = _rmsnorm(hidden_states, norm_w)
            xz = jnp.einsum('bld,de->ble', x, W_in)
            x_in, z = jnp.split(xz, 2, axis=-1)
            x_act = _silu(_causal_dwconv(x_in, conv_w))
            x_db = jnp.einsum('ble,er->blr', x_act, W_x)
            dt_lr = x_db[..., :DT_RANK]
            Bm = x_db[..., DT_RANK:DT_RANK + N_STATE]
            Cm = x_db[..., DT_RANK + N_STATE:]
            delta = jax.nn.softplus(jnp.einsum('blr,re->ble', dt_lr, W_dt) + b_dt)
            A = -jnp.exp(A_log)
            y, h_last = _selective_scan(x_act, delta, A, Bm, Cm, D_param)
            y = y * _silu(z)
            out = jnp.einsum('ble,ed->bld', y, W_out)
            return (residual + out, h_last)
        return _reference_tuple_inner(hidden_states, norm_w, W_in, conv_w, W_x, W_dt, b_dt, A_log, D_param, W_out)[0]

    def _L1_ffn_ref(hidden_states, w_router, w_gate, w_up, w_down, ws_gate, ws_up, ws_down):
        import jax, jax.numpy as jnp
        import numpy as np
        B, S, D = (4, 256, 128)
        E, F, TOP_K = (8, 512, 2)
        b, s, d = hidden_states.shape
        x = hidden_states.reshape(-1, d)
        T = x.shape[0]
        num_experts = w_gate.shape[0]
        logits = x @ w_router
        probs = jax.nn.softmax(logits, axis=-1)
        top_w, top_i = jax.lax.top_k(probs, TOP_K)
        mult = top_w / (top_w.sum(axis=-1, keepdims=True) + 1e-08)
        w_full = jnp.zeros((T, num_experts), dtype=x.dtype).at[jnp.arange(T)[:, None], top_i].set(mult)
        out = jnp.zeros_like(x)
        for e in range(num_experts):
            h = jax.nn.silu(x @ w_gate[e]) * (x @ w_up[e])
            out = out + w_full[:, e:e + 1] * (h @ w_down[e])
        hs = jax.nn.silu(x @ ws_gate) * (x @ ws_up)
        out = out + hs @ ws_down
        return out.reshape(b, s, d)
    x = L0_attn_x
    x = _layernorm(x + _L0_attn_ref(x, L0_attn_W_qkv, L0_attn_W_out), axis=-1)
    x = _layernorm(x + _L0_ffn_ref(x, L0_ffn_shared_w1, L0_ffn_shared_w2, L0_ffn_experts_w1, L0_ffn_experts_w2, L0_ffn_gate_w), axis=-1)
    x = _layernorm(x + _L1_attn_ref(x, L1_attn_norm_w, L1_attn_W_in, L1_attn_conv_w, L1_attn_W_x, L1_attn_W_dt, L1_attn_b_dt, L1_attn_A_log, L1_attn_D_param, L1_attn_W_out), axis=-1)
    x = _layernorm(x + _L1_ffn_ref(x, L1_ffn_w_router, L1_ffn_w_gate, L1_ffn_w_up, L1_ffn_w_down, L1_ffn_ws_gate, L1_ffn_ws_up, L1_ffn_ws_down), axis=-1)
    return x

_drawn_inputs = setup_inputs


def setup_inputs(seed=0):
    import zlib

    import numpy as np

    out = dict(_drawn_inputs(seed))
    spreads = {'L1_attn_norm_w': (1.0, 0.2), 'L1_attn_D_param': (1.0, 0.2)}
    factors = {}
    for name, (base, spread) in spreads.items():
        noise = np.random.default_rng([zlib.crc32(name.encode()), seed]).standard_normal(out[name].shape)
        drawn = base * np.exp(spread * noise) if base else spread * noise
        out[name] = jnp.asarray(drawn.astype(out[name].dtype))
    for name, factor in factors.items():
        out[name] = (out[name] * factor).astype(out[name].dtype)
    return out
```

```python
import numpy as np
import concourse.bass as bass
from concourse import mybir
from contextlib import ExitStack, contextmanager

F32 = mybir.dt.float32
BF16 = mybir.dt.bfloat16
I32 = mybir.dt.int32
U32 = mybir.dt.uint32
ALU = mybir.AluOpType
ACT = mybir.ActivationFunctionType
AXX = mybir.AxisListType.X
ds = bass.ds

P = 128
D = 128
NB = 4
S = 512
QT = S // P
T = NB * S
NT = T // P
NE = 8
HID = 512
HB = HID // P
ROUTED = (2 * T + NE * (P - 1)) // P
SLOTS = NT + ROUTED
ROWS = SLOTS * P
EI = 256
EH = EI // P
NS = 16
KC = 4
DTR = 64
BC = 2 * NS
LN_EPS = 1e-5
RMS_EPS = 1e-6
SCALE = float(D) ** -0.5
NEVER = -3.0e38


class Steps:

    def __init__(self, eng, sem):
        self.eng, self.sem, self.n = eng, sem, 0

    def mark(self, ins):
        ins.then_inc(self.sem, 1)
        self.n = self.n + 1

    def link(self, ins):
        self.mark(ins)
        self.eng.wait_ge(self.sem, self.n)

    @contextmanager
    def loop(self, lo, hi, per):
        base = self.n
        with self.eng.Fori(0, hi - lo) as i:
            self.n = base + i * per
            yield i + lo
        self.n = base + (hi - lo) * per


class Share:

    def __init__(self, sem, base):
        self.sem, self.base = sem, base

    def at(self, n):
        return self.sem, n + self.base


def build(nc, a, out):
    ctx = ExitStack()
    with ctx:
        def sb(name, shape, dt=F32):
            return ctx.enter_context(nc.sbuf_tensor(name, shape, dt))

        def sem(name):
            return ctx.enter_context(nc.semaphore(name))

        xs = nc.dram_tensor("xs", (ROWS, D), F32).ap()
        ys = nc.dram_tensor("ys", (ROWS, D), F32).ap()

        x_all = sb("x_all", [P, T])
        ident = sb("ident", [P, P])
        ones = sb("ones", [P, P])
        before = sb("before", [P, P])
        wq = sb("wq", [P, D]); wk = sb("wk", [P, D]); wv = sb("wv", [P, D]); woT = sb("woT", [P, D])
        wqk = sb("wqk", [P, D]); wvo = sb("wvo", [P, D])
        gate = [sb(f"gate{l}", [P, NE]) for l in range(2)]
        w1 = sb("w1", [P, (NE + 1) * HID])
        w2 = sb("w2", [P, (NE + 1) * HID])
        wg = sb("wg", [P, (NE + 1) * HID])
        wu = sb("wu", [P, (NE + 1) * HID])
        wd = sb("wd", [P, (NE + 1) * HID])
        norm_w = sb("norm_w", [P, 1])
        w_in = sb("w_in", [P, 2 * EI])
        conv = sb("conv", [P, EH, KC])
        w_dtl = sb("w_dtl", [P, EH, DTR])
        w_bc3 = sb("w_bc3", [P, EH, 3 * BC])
        w_dt = sb("w_dt", [DTR, EI])
        b_dt = sb("b_dt", [P, EH])
        a_log = sb("a_log", [P, EH * NS])
        a_neg = sb("a_neg", [P, EH * NS])
        d_par = sb("d_par", [P, EH])
        w_out = sb("w_out", [P, EH, D])
        diag = sb("diag", [P, EH * KC, P])
        sel = sb("sel", [3 * BC, BC * P], BF16)
        normed = sb("normed", [P, QT, D])
        normT = sb("normT", [P, S])
        pre = sb("pre", [P, QT, D])
        stats = sb("stats", [P, QT, 6])
        stats_n = sb("stats_n", [P, QT])
        mv = sb("mv", [P, QT, 2])
        rstd = sb("rstd", [P, QT])
        half = sb("half", [P, QT])
        eps = sb("eps", [P, 2, QT])
        logits = sb("logits", [P, NT, NE])
        rank8 = sb("rank8", [P, NE]); rank8i = sb("rank8i", [P, NE], I32)
        slot_row = sb("slot_row", [P, ROUTED]); slot_rowi = sb("slot_rowi", [P, ROUTED], I32)
        eq = sb("eq", [P, NT, NE]); sc = sb("sc", [P, NT, NE]); l2 = sb("l2", [P, NT, NE])
        oh = [sb(f"oh{k}", [P, NT, NE]) for k in range(2)]
        mm = [sb(f"mm{k}", [P, NT]) for k in range(2)]
        ms = [sb(f"ms{k}", [P, NT]) for k in range(2)]
        mask = sb("mask", [P, NT, NE])
        gap = sb("gap", [P, NT]); egap = sb("egap", [P, NT]); den = sb("den", [P, NT]); zsum = sb("zsum", [P, NT])
        gates = [sb(f"gates{k}", [P, NT]) for k in range(2)]
        carry = sb("carry", [P, NE, NT])
        tot = sb("tot", [P, NE, NT]); incl = sb("incl", [P, NE, NT])
        cnt_i = sb("cnt_i", [P, NE], I32); cnt = sb("cnt", [P, NE]); ends = sb("ends", [P, NE]); offs = sb("offs", [P, NE])
        pos = sb("pos", [P, NT, NE]); posk = sb("posk", [P, NT, NE]); posf = [sb(f"posf{k}", [P, NT]) for k in range(2)]
        rows = [sb(f"rows{k}", [P, NT], U32) for k in range(2)]
        past = sb("past", [P, ROUTED, NE]); slot_ef = sb("slot_ef", [P, ROUTED])
        slot_e = sb("slot_e", [P, SLOTS], I32)
        xin = [sb(f"xin{k}", [P, D]) for k in range(4)]
        xT = [sb(f"xT{k}", [P, P]) for k in range(2)]
        wide = sb("wide", [P, 8 * HID])
        th, ga, hs, hT = ([wide[:, (2 * j + k) * HID:(2 * j + k + 1) * HID] for k in range(2)] for j in range(4))
        yout = [sb(f"yout{k}", [P, D]) for k in range(4)]
        work = sb("work", [P, 12 * 1024])

        def area(at, *shape):
            n = int(np.prod(shape))
            v = work[:, at:at + n]
            if len(shape) == 2:
                v = v.rearrange("p (a b) -> p a b", a=shape[0])
            return v

        xb = area(0, QT, D)
        xbT = area(512, S)
        qmT = area(1024, S)
        v_all = area(1536, T)
        probs = area(3584, QT, S)
        pT = [area(5632 + 512 * k, S) for k in range(2)]
        mx = area(6656, QT); nmx = area(6660, QT); rs = area(6664, QT); rinv = area(6668, QT)
        zero = area(6720, ROUTED * D)
        shared = area(0, T)
        y_k = [[area(2048 + 1024 * k + 128 * q, D) for q in range(8)] for k in range(2)]
        srt = area(4096, QT)
        xn = area(0, QT, D); xnT = area(512, S)
        xi = area(1024, EH, S + KC - 1)
        xa = area(2304, EH, S); zs = area(3328, EH, S)
        u1 = area(4352, EH, S); u2 = area(5376, EH, S); u3 = area(6400, EH, S)
        delta = area(7424, EH, S); du = area(8448, EH, S)
        dts = xnT
        res = area(9472, S)
        ssq = area(12032, QT); rms = area(12036, QT)
        dA = [area(9984 + 1024 * k, EH, S) for k in range(2)]
        st, hc = ([wide[:, (2 * j + k) * EH * S:(2 * j + k + 1) * EH * S].rearrange("p (h t) -> p h t", h=EH)
                   for k in range(2)] for j in range(2))
        cc = [res, dts]
        hi = sb("hi", [3 * BC, S], BF16); mid = sb("mid", [3 * BC, S], BF16)
        parts = sb("parts", [3 * BC, S], BF16)
        sq = area(0, D)

        ps = ctx.enter_context(nc.psum_tensor("ps", [P, 8, 512], F32))

        def bank(k, n=512):
            return ps[:, k, 0:n]

        def tile_of(ap, t):
            return ap[:, ds(t * D, D)]

        def tiles(ap):
            return ap.rearrange("p (q d) -> p q d", d=D)

        def layers(name, per_layer):
            s = sem(name)
            return [Share(s, l * per_layer) for l in range(2)]

        def fills(k):
            return (SLOTS - k + 3) // 4

        ld_x = sem("ld_x"); ld_gate = sem("ld_gate"); ld_att = sem("ld_att"); ld_f0 = sem("ld_f0"); ld_f1 = sem("ld_f1"); ld_ss = sem("ld_ss")
        zero_set = sem("zero_set"); xs_zeroed = sem("xs_zeroed")
        consts = sem("consts"); diag_set = sem("diag_set")
        w_ps = sem("w_ps"); w_set = sem("w_set")
        pool_step = sem("pool_step"); dve_step = sem("dve_step"); act_step = sem("act_step")
        xb_loaded = sem("xb_loaded"); xbT_ps = sem("xbT_ps"); xbT_set = sem("xbT_set")
        qm_ps = sem("qm_ps"); qmT_set = sem("qmT_set"); v_ps = sem("v_ps"); v_set = sem("v_set")
        scores_ps = sem("scores_ps"); nmax_set = sem("nmax_set"); probs_set = sem("probs_set")
        pT_ps = sem("pT_ps"); pT_set = sem("pT_set"); ctx_ps = sem("ctx_ps"); ctx_added = sem("ctx_added")
        stats_set = layers("stats_set", NB); rstd_set = layers("rstd_set", NB)
        normed_set = layers("normed_set", NB); kept = layers("kept", NB)
        xs_stored = layers("xs_stored", 16 * NB)
        nT_ps = layers("nT_ps", NB); nT_set = layers("nT_set", NB)
        logit_ps = layers("logit_ps", NB); logits_set = layers("logits_set", NB)
        mask_set = layers("mask_set", 1); count_ps = layers("count_ps", 1)
        counts_taken = layers("counts_taken", 1)
        gap_set = layers("gap_set", 1); egap_set = layers("egap_set", 1)
        rows_set = layers("rows_set", 2); scattered = layers("scattered", 16 * 2 * NT)
        xin_loaded_ = [layers(f"xin_loaded{k}", 16 * fills(k)) for k in range(4)]
        xin_loaded = [[r[l] for r in xin_loaded_] for l in range(2)]
        x_ps = layers("x_ps", SLOTS); xT_set = layers("xT_set", SLOTS)
        h_ps = layers("h_ps", SLOTS); th_set = layers("th_set", SLOTS)
        hs_set = layers("hs_set", SLOTS); hT_ps = layers("hT_ps", SLOTS)
        hT_set = layers("hT_set", SLOTS); y_ps = layers("y_ps", SLOTS)
        yout_set = layers("yout_set", SLOTS)
        ys_stored_ = [layers(f"ys_stored{k}", 16 * fills(k)) for k in range(4)]
        ys_stored = [[r[l] for r in ys_stored_] for l in range(2)]
        shared_loaded = layers("shared_loaded", 16)
        gathered_ = [layers(f"gathered{k}", 64) for k in range(8)]
        gathered = [[r[l] for r in gathered_] for l in range(2)]
        rms_mid = sem("rms_mid"); fix_mid = sem("fix_mid")
        combined = layers("combined", NB); var_set = layers("var_set", NB)
        std_set = layers("std_set", NB); layer_out = layers("layer_out", NB)
        out_stored = sem("out_stored")
        a_set = sem("a_set"); ssq_set = sem("ssq_set"); rms_set = sem("rms_set"); xn_set = sem("xn_set")
        xn_ps = sem("xn_ps"); xnT_set = sem("xnT_set"); xi_ps = sem("xi_ps"); z_ps = sem("z_ps"); xi_set = sem("xi_set")
        conv_ps = sem("conv_ps"); conv_th = sem("conv_th"); z_th = sem("z_th"); xa_set = sem("xa_set")
        zs_set = sem("zs_set"); dtl_ps = sem("dtl_ps"); bc_ps = sem("bc_ps"); dts_set = sem("dts_set"); hi_set = sem("hi_set")
        parts_set = sem("parts_set"); dl_ps = sem("dl_ps"); soft_abs = sem("soft_abs"); soft_exp = sem("soft_exp")
        soft_ln = sem("soft_ln"); soft_fix = sem("soft_fix"); du_set = sem("du_set"); delta_set = sem("delta_set")
        b_ps = sem("b_ps"); c_ps = sem("c_ps"); dA_set = sem("dA_set"); cc_set = sem("cc_set")
        dbu_set = sem("dbu_set"); st_set = sem("st_set"); hc_set = sem("hc_set"); y_sum = sem("y_sum")
        yg_set = sem("yg_set"); o_ps = sem("o_ps"); o_added = sem("o_added")

        block = ctx.enter_context(nc.Block())

        LOOP_LO = 9
        LOOP_TRIPS = (SLOTS - 2 - LOOP_LO) // 4
        COUNT_STEP, EGAP_STEP = -1, 1

        def slot_steps(loop, step):
            for i in range(-2, LOOP_LO):
                step(0, i)
            with loop as m:
                for k in range(4):
                    step(m, LOOP_LO + k)
            for i in range(LOOP_LO + 4 * LOOP_TRIPS, SLOTS + 1):
                step(0, i)

        before_ps, tiles_ps = (ps[:, 0, P + k * NT * NE:P + (k + 1) * NT * NE] for k in range(2))

        def valid(i, n=SLOTS):
            return not isinstance(i, int) or 0 <= i < n

        def wait_pos(eng, s, value):
            if isinstance(value, int) and value <= 0:
                return
            eng.wait_ge(*s.at(value))

        @block.sync
        def _(sp):
            def load_seq(b):
                if not isinstance(b, int):
                    sp.wait_ge(xbT_ps, b)
                sp.dma_start(xb, a["x"][ds(b * S, S), :].rearrange("(q p) d -> p q d", p=P)).then_inc(xb_loaded, 16)

            def load_weights(done, *pairs):
                for dst, name in pairs:
                    sp.dma_start(dst[:], a[name]).then_inc(done, 16)

            load_seq(0)
            load_weights(ld_att, (wq, "wq"), (wk, "wk"), (wv, "wv"), (woT, "woT"))
            load_weights(ld_gate, (gate[0], "gate0"), (gate[1], "gate1"))
            sp.dma_start(x_all[:].rearrange("p (t d) -> p t d", d=D),
                         a["x"].rearrange("(t p) d -> p t d", p=P)).then_inc(ld_x, 16)
            with sp.Fori(1, NB) as b:
                load_seq(b)
            load_weights(ld_ss, (norm_w, "norm_w"), (w_in, "w_in"), (conv, "conv"), (w_dtl, "w_dtl"), (w_bc3, "w_bc3"),
                         (w_dt, "w_dt"), (b_dt, "b_dt"), (a_log, "a_log"), (d_par, "d_par"), (w_out, "w_out"))

            def moe(l):
                def keep_rows(b):
                    sp.wait_ge(*normed_set[l].at(b + 1))
                    sp.dma_start(xs[ds(b * S, S), :].rearrange("(q p) d -> p q d", p=P),
                                 normed[:, :, :]).then_inc(xs_stored[l].sem, 16)

                def load(i, k):
                    if not isinstance(i, int) or i >= 4:
                        sp.wait_ge(*x_ps[l].at(i - 3))
                    sp.dma_start(xin[k % 4][:, :], xs[ds(i * P, P), :]).then_inc(xin_loaded[l][k % 4].sem, 16)

                with sp.Fori(0, NB - 1) as b:
                    keep_rows(b)
                sp.wait_ge(*xs_stored[l].at(16 * (NB - 1)))
                for i in range(4):
                    load(i, i)
                keep_rows(NB - 1)
                sp.wait_ge(*xs_stored[l].at(16 * NB))
                with sp.Fori(0, (NT - 4) // 4) as m:
                    for k in range(4):
                        load(m * 4 + (k + 4), k)
                sp.wait_ge(*scattered[l].at(16 * 2 * NT))
                trips = ROUTED // 4
                with sp.Fori(0, trips) as m:
                    for k in range(4):
                        load(m * 4 + (NT + k), k)
                for i in range(NT + 4 * trips, SLOTS):
                    load(i, i)
                if l == 0:
                    load_weights(ld_f1, (wg, "wg"), (wu, "wu"), (wd, "wd"))
                for k in range(4):
                    sp.wait_ge(*ys_stored[l][k].at(16 * fills(k)))
                sp.dma_start(tiles(shared), ys[0:T, :].rearrange("(t p) d -> p t d", p=P)).then_inc(shared_loaded[l].sem, 16)

            moe(0)
            moe(1)
            with sp.Fori(0, NB) as b:
                sp.wait_ge(*layer_out[1].at(b + 1))
                sp.dma_start(out[ds(b * S, S), :].rearrange("(q p) d -> p q d", p=P),
                             tiles(x_all[:, ds(b * S, S)])).then_inc(out_stored, 16)
            sp.wait_ge(out_stored, 16 * NB)

        @block.tensor
        def _(pe):
            mm_ = nc.tensor.matmul
            tr = nc.tensor.transpose
            pe.wait_ge(ld_att, 64)
            mm_(bank(5, P), wq[:, :], wk[:, :], start=True, stop=True).then_inc(w_ps, 1)
            mm_(bank(6, P), wv[:, :], woT[:, :], start=True, stop=True).then_inc(w_ps, 1)
            pe.wait_ge(consts, 4)
            pe.wait_ge(w_set, 2)

            def project(b):
                pe.wait_ge(xb_loaded, b * 16 + 16)
                for q in range(QT):
                    last = tr(ps[:, 6, q * P:(q + 1) * P], xb[:, q, :], ident[:, :])
                last.then_inc(xbT_ps, 1)
                pe.wait_ge(xbT_set, b + 1)
                mm_(bank(5), wqk[:, :], xbT, start=True, stop=True).then_inc(qm_ps, 1)
                for q in range(QT):
                    last = mm_(ps[:, 6, q * P:(q + 1) * P], xbT[:, q * P:(q + 1) * P], wvo[:, :], start=True, stop=True)
                last.then_inc(v_ps, 1)

            def router(l, b):
                pe.wait_ge(*normed_set[l].at(b + 1))
                for q in range(QT):
                    last = tr(ps[:, 5, q * P:(q + 1) * P], normed[:, q, :], ident[:, :])
                last.then_inc(nT_ps[l].sem, 1)
                pe.wait_ge(*nT_set[l].at(b + 1))
                for q in range(QT):
                    last = mm_(ps[:, 6, q * NE:(q + 1) * NE], normT[:, q * P:(q + 1) * P], gate[l][:, :],
                               start=True, stop=True)
                last.then_inc(logit_ps[l].sem, 1)
                pe.wait_ge(*logits_set[l].at(b + 1))

            def attend(b, first, final):
                pe.wait_ge(qmT_set, b + 1)
                for q in range(QT):
                    mm_(bank(q), qmT[:, q * P:(q + 1) * P], xbT, start=True, stop=True).then_inc(scores_ps, 1)
                pe.wait_ge(v_set, b + 1)
                if not final:
                    project(b + 1)

                def turn(q):
                    pe.wait_ge(probs_set, b * QT + (q + 1))
                    if q > 0 or not first:
                        pe.wait_ge(pT_set, b * QT + q)
                    for k in range(QT):
                        last = tr(ps[:, 7, k * P:(k + 1) * P], probs[:, q, k * P:(k + 1) * P], ident[:, :])
                    last.then_inc(pT_ps, 1)

                def context(q):
                    pe.wait_ge(pT_set, b * QT + (q + 1))
                    if q == 0 and not first:
                        pe.wait_ge(ctx_added, b)
                    for k in range(QT):
                        last = mm_(ps[:, 4, q * P:(q + 1) * P], pT[q % 2][:, k * P:(k + 1) * P],
                                   tile_of(v_all, b * QT + k), start=(k == 0), stop=(k == QT - 1))
                    last.then_inc(ctx_ps, 1)

                turn(0)
                for q in range(QT):
                    if q + 1 < QT:
                        turn(q + 1)
                    context(q)
                if not first:
                    router(0, b - 1)

            project(0)
            attend(0, True, False)
            pe.wait_ge(ld_gate, 32)
            with pe.Fori(1, NB - 1) as b:
                attend(b, False, False)
            attend(NB - 1, False, True)
            router(0, NB - 1)

            def moe(l):
                wa, wb, wc = ((w1, None, w2), (wg, wu, wd))[l]
                hbank = (4, 6)
                pe.wait_ge(*((ld_f0, 32), (ld_f1, 48))[l])

                def counts():
                    pe.wait_ge(*mask_set[l].at(1))
                    pe.wait_ge(*xT_set[l].at(COUNT_STEP + 2))
                    flat = mask[:, :, :].rearrange("p t e -> p (t e)")
                    mm_(before_ps, before[:, :], flat, start=True, stop=True)
                    mm_(tiles_ps, ones[:, :], flat, start=True, stop=True).then_inc(count_ps[l].sem, 1)
                    pe.wait_ge(*counts_taken[l].at(1))

                expert = {}

                def expert_of(i, k):
                    if isinstance(i, int):
                        expert.clear()
                        if i < NT:
                            return NE * HID
                        return pe.value_load(slot_e[0:1, i:i + 1], min_val=0, max_val=NE * HID)
                    if k not in expert:
                        expert[k] = pe.value_load(slot_e[0:1, ds(i, 1)], min_val=0, max_val=NE * HID)
                    return expert[k]

                def step(m, k):
                    i = m * 4 + k
                    x, h, t, y = i + 2, i + 1, i, i - 1
                    if isinstance(m, int) and i == COUNT_STEP:
                        counts()
                    if isinstance(m, int) and i == LOOP_LO - 1:
                        pe.wait_ge(*rows_set[l].at(2))
                    if valid(x):
                        q = (k + 2) % 4
                        pe.wait_ge(*xin_loaded[l][q].at((m + (k + 2) // 4 + 1) * 16))
                        wait_pos(pe, xT_set[l], x)
                        tr(bank(0, P), xin[q][:, :], ident[:, :]).then_inc(x_ps[l].sem, 1)
                    if valid(h):
                        p = (k + 1) % 2
                        e = expert_of(h, k + 1)
                        pe.wait_ge(*xT_set[l].at(h + 1))
                        wait_pos(pe, hs_set[l], h - 1)
                        last = mm_(bank(hbank[0] + p), xT[p][:, :], wa[:, ds(e, HID)], start=True, stop=True)
                        if wb is not None:
                            last = mm_(bank(hbank[1] + p), xT[p][:, :], wb[:, ds(e, HID)], start=True, stop=True)
                        last.then_inc(h_ps[l].sem, 1)
                        if not isinstance(h, int) and k < LOOP_LO + 3:
                            expert_of(h + 1, k + 2)
                    if valid(t):
                        p = k % 2
                        pe.wait_ge(*hs_set[l].at(t + 1))
                        wait_pos(pe, hT_set[l], t - 1)
                        for j in range(HB):
                            last = tr(ps[:, 2 + p, j * P:(j + 1) * P], hs[p][:, j * P:(j + 1) * P], ident[:, :])
                        last.then_inc(hT_ps[l].sem, 1)
                    if valid(y):
                        p = (k - 1) % 2
                        e = expert_of(y, k - 1)
                        pe.wait_ge(*hT_set[l].at(y + 1))
                        wait_pos(pe, yout_set[l], y)
                        for j in range(HB):
                            last = mm_(bank(1, D), hT[p][:, j * P:(j + 1) * P], wc[:, ds(e + j * D, D)],
                                       start=(j == 0), stop=(j == HB - 1))
                        last.then_inc(y_ps[l].sem, 1)

                slot_steps(pe.Fori(0, LOOP_TRIPS), step)

            moe(0)

            pe.wait_ge(ld_ss, 160)
            pe.wait_ge(diag_set, EH * KC)
            pe.wait_ge(consts, 5)

            def ss(b, first):
                pe.wait_ge(xn_set, b + 1)
                for q in range(QT):
                    last = tr(ps[:, 0, q * P:(q + 1) * P], xn[:, q, :], ident[:, :])
                last.then_inc(xn_ps, 1)
                pe.wait_ge(xnT_set, b + 1)
                for h in range(EH):
                    mm_(bank(1 + h), w_in[:, h * P:(h + 1) * P], xnT, start=True, stop=True).then_inc(xi_ps, 1)
                for h in range(EH):
                    mm_(bank(3 + h), w_in[:, EI + h * P:EI + (h + 1) * P], xnT, start=True, stop=True).then_inc(z_ps, 1)
                for h in range(EH):
                    pe.wait_ge(xi_set, b * EH + (h + 1))
                    for k in range(KC):
                        last = mm_(bank(1 + h), diag[:, h * KC + k, :], xi[:, h, k:k + S], start=(k == 0), stop=(k == KC - 1))
                    last.then_inc(conv_ps, 1)
                pe.wait_ge(xa_set, b * EH + EH)
                for h in range(EH):
                    last = mm_(ps[0:3 * BC, 5, :], w_bc3[:, h, :], xa[:, h, :], start=(h == 0), stop=(h == EH - 1))
                last.then_inc(bc_ps, 1)
                for h in range(EH):
                    last = mm_(ps[0:DTR, 0, :], w_dtl[:, h, :], xa[:, h, :], start=(h == 0), stop=(h == EH - 1))
                last.then_inc(dtl_ps, 1)
                pe.wait_ge(dts_set, b + 1)
                for h in range(EH):
                    last = mm_(bank(6 + h), w_dt[:, h * P:(h + 1) * P], dts[0:DTR, :], start=True, stop=True)
                last.then_inc(dl_ps, 1)
                pe.wait_ge(parts_set, b + 1)
                pe.wait_ge(zs_set, b * EH + EH)
                pe.wait_ge(soft_abs, b + 1)

                def spread(n, j, p, free):
                    if free:
                        pe.wait_ge(dbu_set, n - 1)
                    mm_(bank(p), sel[:, ds(j * P, P)], parts[:, :], start=True, stop=True).then_inc(b_ps, 1)
                    if free:
                        pe.wait_ge(cc_set, n - 1)
                    mm_(bank(2 + p), sel[:, ds((j + NS) * P, P)], parts[:, :], start=True, stop=True).then_inc(c_ps, 1)

                def add_up(n, p, start, stop):
                    pe.wait_ge(hc_set, n + 1)
                    for h in range(EH):
                        last = mm_(bank(6 + h), ident[:, :], hc[p][:, h, :], start=start, stop=stop)
                    last.then_inc(y_sum, 1)

                def pair(m, spreads, adds, start, stop):
                    for p in range(2):
                        if spreads:
                            spread(b * NS + m * 2 + p, m * 2 + p, p, not (first and isinstance(m, int) and m == 0))
                    for p in range(2):
                        if adds:
                            add_up(b * NS + m * 2 + (p - 2), p, start and p == 0, stop and p == 1)

                pair(0, True, False, False, False)
                pair(1, True, True, True, False)
                with pe.Fori(2, NS // 2) as m:
                    pair(m, True, True, False, False)
                pair(NS // 2, False, True, False, True)
                pe.wait_ge(yg_set, b + 1)
                for q in range(QT):
                    for h in range(EH):
                        last = mm_(ps[:, 3, q * P:(q + 1) * P], yg_[h][:, q * P:(q + 1) * P], w_out[:, h, :],
                                   start=(h == 0), stop=(h == EH - 1))
                last.then_inc(o_ps, 1)
                router(1, b)

            yg_ = [u1[:, h, :] for h in range(EH)]
            ss(0, True)
            with pe.Fori(1, NB) as b:
                ss(b, False)
            moe(1)

        @block.scalar
        def _(act):
            A = nc.scalar.activation
            steps = Steps(act, act_step)

            def cp(dst, src, **kw):
                return A(dst, src, ACT.Copy, **kw)

            act.wait_ge(w_ps, 1)
            cp(wqk[:, :], bank(5, P)).then_inc(w_set, 1)
            act.wait_ge(w_ps, 2)
            cp(wvo[:, :], bank(6, P)).then_inc(w_set, 1)

            def project(b):
                act.wait_ge(xbT_ps, b + 1)
                cp(xbT, bank(6)).then_inc(xbT_set, 1)

            def values(b):
                act.wait_ge(v_ps, b + 1)
                cp(v_all[:, ds(b * S, S)], bank(6)).then_inc(v_set, 1)

            def router(l, b):
                act.wait_ge(*nT_ps[l].at(b + 1))
                cp(normT[:, :], bank(5)).then_inc(nT_set[l].sem, 1)

            def attend(b, first, final):
                def soften(q):
                    act.wait_ge(nmax_set, b * QT + (q + 1))
                    A(probs[:, q, :], bank(q), ACT.Exp, bias=nmx[:, q:q + 1], scale=SCALE,
                      accum_out=rs[:, q:q + 1]).then_inc(probs_set, 1)

                for q in range(QT - 1):
                    soften(q)
                if not final:
                    project(b + 1)
                soften(QT - 1)
                if not final:
                    values(b + 1)
                for q in range(QT):
                    act.wait_ge(pT_ps, b * QT + (q + 1))
                    cp(pT[q % 2], bank(7)).then_inc(pT_set, 1)
                if not first:
                    router(0, b - 1)

            project(0)
            values(0)
            attend(0, True, False)
            act.dma_start(w1[:], a["w1"]).then_inc(ld_f0, 16)
            with act.Fori(1, NB - 1) as b:
                attend(b, False, False)
            act.dma_start(w2[:], a["w2"]).then_inc(ld_f0, 16)
            attend(NB - 1, False, True)
            router(0, NB - 1)

            def moe(l):
                def exp_gaps():
                    act.wait_ge(*gap_set[l].at(1))
                    A(egap[:, :], gap[:, :], ACT.Exp).then_inc(egap_set[l].sem, 1)
                    if l:
                        act.wait_ge(*gap_set[l].at(2))
                        A(sc[:, :, :], l2[:, :, :], ACT.Exp).then_inc(egap_set[l].sem, 1)

                def step(m, k):
                    i = m * 4 + k
                    h, t, y = i + 1, i, i - 1
                    if isinstance(m, int) and i == EGAP_STEP:
                        exp_gaps()
                    if valid(h):
                        p = (k + 1) % 2
                        act.wait_ge(*h_ps[l].at(h + 1))
                        wait_pos(act, hs_set[l], h - 1)
                        A(th[p], bank(4 + p), ACT.Tanh, scale=0.5).then_inc(th_set[l].sem, 1)
                    if valid(t):
                        p = k % 2
                        act.wait_ge(*hT_ps[l].at(t + 1))
                        wait_pos(act, y_ps[l], t - 1)
                        cp(hT[p], bank(2 + p)).then_inc(hT_set[l].sem, 1)
                    if valid(y):
                        q = (k - 1) % 4
                        act.wait_ge(*y_ps[l].at(y + 1))
                        wait_pos(act, ys_stored[l][q], (m + (k - 1) // 4) * 16)
                        A(yout[q][:, :], bank(1, D), ACT.Copy, scale=0.5).then_inc(yout_set[l].sem, 1)
                        act.wait_ge(*yout_set[l].at(y + 1))
                        act.dma_start(ys[ds(y * P, P), :], yout[q][:, :]).then_inc(ys_stored[l][q].sem, 16)

                slot_steps(act.Fori(0, LOOP_TRIPS), step)

                with act.Fori(0, NB) as b:
                    act.wait_ge(*var_set[l].at(b + 1))
                    A(srt, mv[:, :, 1], ACT.Sqrt).then_inc(std_set[l].sem, 1)

            moe(0)

            act.wait_ge(ld_ss, 160)
            A(a_neg[:, :], a_log[:, :], ACT.Exp).then_inc(a_set, 1)

            def ss(b):
                act.wait_ge(*layer_out[0].at(NB))
                for q in range(QT):
                    last = A(sq, tile_of(x_all, b * QT + q), ACT.Square, scale=D ** -0.5, accum_out=ssq[:, q:q + 1])
                    if q + 1 < QT:
                        steps.link(last)
                last.then_inc(ssq_set, 1)
                act.wait_ge(xn_ps, b + 1)
                A(xnT, bank(0), ACT.Copy, scale=norm_w[:, 0:1]).then_inc(xnT_set, 1)
                for h in range(EH):
                    act.wait_ge(xi_ps, b * EH + (h + 1))
                    cp(xi[:, h, KC - 1:KC - 1 + S], bank(1 + h)).then_inc(xi_set, 1)
                for h in range(EH):
                    act.wait_ge(z_ps, b * EH + (h + 1))
                    A(u2[:, h, :], bank(3 + h), ACT.Tanh, scale=0.5).then_inc(z_th, 1)
                for h in range(EH):
                    act.wait_ge(conv_ps, b * EH + (h + 1))
                    A(u1[:, h, :], bank(1 + h), ACT.Tanh).then_inc(conv_th, 1)
                act.wait_ge(bc_ps, b + 1)
                cp(hi[:, :], ps[0:3 * BC, 5, :]).then_inc(hi_set, 1)
                act.wait_ge(dtl_ps, b + 1)
                cp(dts[0:DTR, :], ps[0:DTR, 0, :]).then_inc(dts_set, 1)
                act.wait_ge(dl_ps, b + 1)
                act.wait_ge(xa_set, b * EH + EH)
                act.wait_ge(zs_set, b * EH + EH)
                for h in range(EH):
                    steps.mark(A(u1[:, h, :], bank(6 + h), ACT.Abs, bias=b_dt[:, h:h + 1]))
                for h in range(EH):
                    last = A(u3[:, h, :], bank(6 + h), ACT.Relu, bias=b_dt[:, h:h + 1])
                last.then_inc(soft_abs, 1)
                act.wait_ge(act_step, steps.n)
                A(u2, u1, ACT.Exp, scale=-1.0).then_inc(soft_exp, 1)
                act.wait_ge(soft_exp, b + 1)
                A(u1, u2, ACT.Ln, bias=1.0).then_inc(soft_ln, 1)
                act.wait_ge(delta_set, b + 1)

                def state(n, j, p, fresh):
                    if not fresh:
                        act.wait_ge(st_set, n - 1)
                    for h in range(EH):
                        lo = 1 if h else 0
                        last = A(dA[p][:, h, lo:S], delta[:, h, lo:S], ACT.Exp, scale=a_neg[:, ds(j + h * NS, 1)])
                    last.then_inc(dA_set, 1)
                    act.wait_ge(c_ps, n + 1)
                    if not fresh:
                        act.wait_ge(hc_set, n - 1)
                    cp(cc[p], bank(2 + p)).then_inc(cc_set, 1)

                for m in range(1):
                    for p in range(2):
                        state(b * NS + p, p, p, isinstance(b, int) and b == 0)
                with act.Fori(1, NS // 2) as m:
                    for p in range(2):
                        state(b * NS + m * 2 + p, m * 2 + p, p, False)
                router(1, b)

            ss(0)
            with steps.loop(1, NB, QT - 1 + EH) as b:
                ss(b)
            moe(1)

        @block.vector
        def _(dve):
            V = nc.vector
            steps = Steps(dve, dve_step)
            link = steps.link

            def take_qm(b):
                dve.wait_ge(qm_ps, b + 1)
                V.tensor_copy(qmT, bank(5)).then_inc(qmT_set, 1)

            def take_logits(l, b):
                dve.wait_ge(*logit_ps[l].at(b + 1))
                V.tensor_copy(logits[:].rearrange("p t e -> p (t e)")[:, ds(b * QT * NE, QT * NE)],
                              ps[:, 6, 0:QT * NE]).then_inc(logits_set[l].sem, 1)

            def norm_stats(done):
                for q in range(QT):
                    steps.mark(V.bn_stats(stats[:, q, :], pre[:, q, :]))
                dve.wait_ge(dve_step, steps.n)
                V.tensor_copy(stats_n[:, :], stats[:, :, 0])
                for q in range(QT - 1):
                    V.bn_aggr(mv[:, q, :], stats[:, q, :])
                done(V.bn_aggr(mv[:, QT - 1, :], stats[:, QT - 1, :]))

            NORM_STEPS = QT
            COMBINE_STEPS = 3 * QT - 1 + NORM_STEPS + 2

            def norm_apply(l, b):
                dve.wait_ge(*rstd_set[l].at(b + 1))
                for q in range(QT):
                    last = V.tensor_scalar(normed[:, q, :], pre[:, q, :], mv[:, q, 0:1], rstd[:, q:q + 1],
                                           ALU.subtract, ALU.mult)
                last.then_inc(normed_set[l].sem, 1)

            def reuse(l, b):
                dve.wait_ge(*xs_stored[l].at(b * 16 + 16))
                dve.wait_ge(*kept[l].at(b + 1))

            def attend_norm(b):
                dve.wait_ge(ctx_ps, b * QT + QT)
                for q in range(QT):
                    last = V.scalar_tensor_tensor(out=pre[:, q, :], in0=ps[:, 4, q * P:(q + 1) * P],
                                                  scalar=rinv[:, q:q + 1], in1=tile_of(x_all, b * QT + q),
                                                  op0=ALU.mult, op1=ALU.add)
                last.then_inc(ctx_added, 1)
                dve.wait_ge(ctx_added, b + 1)
                norm_stats(lambda ins: ins.then_inc(stats_set[0].sem, 1))
                norm_apply(0, b)

            ATT_NORM = NORM_STEPS

            def attend(b, first, final):
                for q in range(QT):
                    dve.wait_ge(scores_ps, b * QT + (q + 1))
                    link(V.reduce_max(mx[:, q:q + 1], bank(q), AXX))
                    V.tensor_scalar(nmx[:, q:q + 1], mx[:, q:q + 1], -SCALE, None, ALU.mult).then_inc(nmax_set, 1)
                if not final:
                    take_qm(b + 1)
                if not first:
                    attend_norm(b - 1)
                    take_logits(0, b - 1)
                    reuse(0, b - 1)
                dve.wait_ge(probs_set, b * QT + QT)
                link(V.reciprocal(rinv, rs))

            take_qm(0)
            dve.wait_ge(ld_x, 16)
            attend(0, True, False)
            with steps.loop(1, NB - 1, QT + 1 + ATT_NORM) as b:
                attend(b, False, False)
            attend(NB - 1, False, True)
            attend_norm(NB - 1)
            take_logits(0, NB - 1)

            dve.wait_ge(consts, 7)
            link(V.tensor_copy(rank8[:, :], rank8i[:, :]))
            link(V.tensor_copy(slot_row[:, :], slot_rowi[:, :]))
            link(V.memset(carry[:, :, :], 1.0))
            link(V.memset(carry[:, :, 0:1], 0.0))
            link(V.memset(slot_e[:, 0:NT], NE * HID))

            def moe(l):
                tok_exp = [P, NT, NE]

                def over_e(ap):
                    return ap.unsqueeze(2).to_broadcast(tok_exp)

                def over_t(ap):
                    return ap.unsqueeze(1).to_broadcast(tok_exp)

                def routing():
                    dve.wait_ge(*logits_set[l].at(NB))
                    src = logits
                    for k in range(2):
                        link(V.reduce_max(mm[k][:, :], src[:, :, :], AXX))
                        link(V.tensor_tensor(eq[:, :, :], src[:, :, :], over_e(mm[k][:, :]), ALU.is_equal))
                        link(V.tensor_tensor(sc[:, :, :], eq[:, :, :], over_t(rank8[:, :]), ALU.mult))
                        link(V.reduce_max(ms[k][:, :], sc[:, :, :], AXX))
                        link(V.tensor_tensor(oh[k][:, :, :], sc[:, :, :], over_e(ms[k][:, :]), ALU.is_equal))
                        if k == 0:
                            link(V.scalar_tensor_tensor(out=l2[:, :, :].rearrange("p t e -> p (t e)"),
                                                        in0=oh[0][:, :, :].rearrange("p t e -> p (t e)"), scalar=NEVER,
                                                        in1=logits[:, :, :].rearrange("p t e -> p (t e)"),
                                                        op0=ALU.mult, op1=ALU.add))
                            src = l2
                        yield
                    V.tensor_tensor(mask[:, :, :], oh[0][:, :, :], oh[1][:, :, :], ALU.add).then_inc(mask_set[l].sem, 1)
                    V.tensor_tensor(gap[:, :], mm[1][:, :], mm[0][:, :], ALU.subtract).then_inc(gap_set[l].sem, 1)
                    if l:
                        V.tensor_tensor(l2[:, :, :], logits[:, :, :], over_e(mm[0][:, :]),
                                        ALU.subtract).then_inc(gap_set[l].sem, 1)
                    yield
                    dve.wait_ge(*count_ps[l].at(1))
                    link(V.tensor_copy(tot[:, :, :], tiles_ps.rearrange("p (t e) -> p e t", e=NE)))
                    V.tensor_copy(pos[:, :, :].rearrange("p t e -> p (t e)"), before_ps).then_inc(counts_taken[l].sem, 1)
                    yield
                    dve.wait_ge(*counts_taken[l].at(1))
                    flat = "p e t -> p (e t)"
                    link(V.tensor_tensor_scan(incl[:, :, :].rearrange(flat), carry[:, :, :].rearrange(flat),
                                              tot[:, :, :].rearrange(flat), 0.0, ALU.mult, ALU.add))
                    link(V.tensor_scalar(cnt_i[:, :], incl[:, :, NT - 1], float(P - 1), None, ALU.add))
                    link(V.tensor_scalar(cnt_i[:, :], cnt_i[:, :], 7, None, ALU.arith_shift_right))
                    yield
                    link(V.tensor_scalar(cnt[:, :], cnt_i[:, :], float(P), None, ALU.mult))
                    link(V.tensor_tensor_scan(ends[:, :], ones[:, 0:NE], cnt[:, :], float(T), ALU.mult, ALU.add))
                    link(V.tensor_tensor(offs[:, :], ends[:, :], cnt[:, :], ALU.subtract))
                    link(V.tensor_tensor(incl[:, :, :], incl[:, :, :], tot[:, :, :], ALU.subtract))
                    link(V.tensor_tensor(pos[:, :, :], incl[:, :, :].rearrange("p e t -> p t e"),
                                         pos[:, :, :], ALU.add))
                    yield
                    link(V.tensor_tensor(pos[:, :, :], pos[:, :, :], over_t(offs[:, :]), ALU.add))
                    for k in range(2):
                        link(V.tensor_tensor(posk[:, :, :], pos[:, :, :], oh[k][:, :, :], ALU.mult))
                        link(V.reduce_sum(posf[k][:, :], posk[:, :, :], AXX))
                        last = V.tensor_copy(rows[k][:, :], posf[k][:, :])
                        if k == 0:
                            link(last)
                    last.then_inc(rows_set[l].sem, 1)
                    yield
                    shp = [P, ROUTED, NE]
                    link(V.tensor_tensor(past[:, :, :], slot_row[:, :].unsqueeze(2).to_broadcast(shp),
                                         ends[:, :].unsqueeze(1).to_broadcast(shp), ALU.is_ge))
                    link(V.reduce_sum(slot_ef[:, :], past[:, :, :], AXX))
                    V.tensor_scalar(slot_e[:, NT:SLOTS], slot_ef[:, :], float(NE - 1), float(HID),
                                    ALU.min, ALU.mult).then_inc(rows_set[l].sem, 1)
                    yield
                    dve.wait_ge(*egap_set[l].at(1))
                    if l:
                        dve.wait_ge(*egap_set[l].at(2))
                        link(V.reduce_sum(zsum[:, :], sc[:, :, :], AXX))
                        link(V.tensor_scalar(zsum[:, :], zsum[:, :], 1e-8, 1.0, ALU.mult, ALU.add))
                        link(V.tensor_tensor(den[:, :], zsum[:, :], egap[:, :], ALU.add))
                    else:
                        link(V.tensor_scalar(den[:, :], egap[:, :], 1.0, None, ALU.add))
                    link(V.reciprocal(gates[0][:, :], den[:, :]))
                    link(V.tensor_tensor(gates[1][:, :], gates[0][:, :], egap[:, :], ALU.mult))
                    yield

                route = routing()

                def step(m, k):
                    i = m * 4 + k
                    x, h = i + 2, i + 1
                    if isinstance(m, int):
                        for _ in range({-2: 3, -1: 1, 0: 3}.get(i, 1)):
                            next(route, None)
                    if valid(x):
                        p = k % 2
                        dve.wait_ge(*x_ps[l].at(x + 1))
                        wait_pos(dve, h_ps[l], x - 1)
                        V.tensor_copy(xT[p][:, :], bank(0, P)).then_inc(xT_set[l].sem, 1)
                    if valid(h):
                        p = (k + 1) % 2
                        dve.wait_ge(*th_set[l].at(h + 1))
                        wait_pos(dve, hT_ps[l], h - 1)
                        if l:
                            link(V.scalar_tensor_tensor(out=ga[p], in0=th[p], scalar=1.0, in1=bank(4 + p),
                                                        op0=ALU.add, op1=ALU.mult))
                            V.tensor_tensor(hs[p], ga[p], bank(6 + p), ALU.mult).then_inc(hs_set[l].sem, 1)
                        else:
                            V.scalar_tensor_tensor(out=hs[p], in0=th[p], scalar=1.0, in1=bank(4 + p),
                                                   op0=ALU.add, op1=ALU.mult).then_inc(hs_set[l].sem, 1)

                slot_steps(steps.loop(0, LOOP_TRIPS, 4 * l), step)

                dve.wait_ge(*shared_loaded[l].at(16))
                with steps.loop(0, NB // 2, 2 * COMBINE_STEPS) as m:
                    for g in range(2):
                        b = m * 2 + g
                        for q in range(QT):
                            t = b * QT + q
                            y = g * QT + q
                            link(V.tensor_tensor(pre[:, q, :], tile_of(x_all, t), tile_of(shared, t), ALU.add))
                            dve.wait_ge(*gathered[l][y].at(m * 32 + 32))
                            link(V.scalar_tensor_tensor(out=pre[:, q, :], in0=y_k[0][y], scalar=gates[0][:, ds(t, 1)],
                                                        in1=pre[:, q, :], op0=ALU.mult, op1=ALU.add))
                            last = V.scalar_tensor_tensor(out=pre[:, q, :], in0=y_k[1][y], scalar=gates[1][:, ds(t, 1)],
                                                          in1=pre[:, q, :], op0=ALU.mult, op1=ALU.add)
                            if q + 1 < QT:
                                steps.mark(last)
                        last.then_inc(combined[l].sem, 1)
                        dve.wait_ge(*combined[l].at(b + 1))
                        norm_stats(link)
                        V.tensor_scalar(mv[:, :, 1], mv[:, :, 1], LN_EPS, None, ALU.add).then_inc(var_set[l].sem, 1)
                        dve.wait_ge(*std_set[l].at(b + 1))
                        link(V.reciprocal(rstd[:, :], srt))
                        for q in range(QT):
                            last = V.tensor_scalar(tile_of(x_all, b * QT + q), pre[:, q, :], mv[:, q, 0:1],
                                                   rstd[:, q:q + 1], ALU.subtract, ALU.mult)
                        last.then_inc(layer_out[l].sem, 1)
                        dve.wait_ge(*layer_out[l].at(b + 1))

            moe(0)
            reuse(0, NB - 1)

            dve.wait_ge(*layer_out[0].at(NB))
            dve.wait_ge(a_set, 1)
            link(V.tensor_scalar(a_neg[:, :], a_neg[:, :], -1.0, None, ALU.mult))
            link(V.memset(xi[:, :, 0:KC - 1], 0.0))
            for k in range(2):
                link(V.memset(dA[k][:, 1, 0:1], 0.0))

            def ss(b, first):
                dve.wait_ge(rms_set, b + 1)
                for q in range(QT):
                    last = V.tensor_scalar(xn[:, q, :], tile_of(x_all, b * QT + q), rms[:, q:q + 1], None, ALU.mult)
                last.then_inc(xn_set, 1)
                for h in range(EH):
                    dve.wait_ge(z_th, b * EH + (h + 1))
                    V.scalar_tensor_tensor(out=zs[:, h, :], in0=u2[:, h, :], scalar=1.0, in1=bank(3 + h),
                                           op0=ALU.add, op1=ALU.mult).then_inc(zs_set, 1)
                for h in range(EH):
                    dve.wait_ge(conv_th, b * EH + (h + 1))
                    V.scalar_tensor_tensor(out=xa[:, h, :], in0=u1[:, h, :], scalar=1.0, in1=bank(1 + h),
                                           op0=ALU.add, op1=ALU.mult).then_inc(xa_set, 1)
                dve.wait_ge(hi_set, b + 1)
                r = res[0:3 * BC, :]
                link(V.tensor_tensor(r, ps[0:3 * BC, 5, :], hi[:, :], ALU.subtract))
                link(V.tensor_copy(mid[:, :], r))
                link(V.tensor_copy(parts[0:BC, :], hi[0:BC, :]))
                link(V.tensor_copy(parts[BC:2 * BC, :], mid[BC:2 * BC, :]))
                V.tensor_tensor(parts[2 * BC:3 * BC, :], res[2 * BC:3 * BC, :], mid[2 * BC:3 * BC, :],
                                ALU.subtract).then_inc(parts_set, 1)
                dve.wait_ge(soft_exp, b + 1)
                V.tensor_scalar(du, u2, 1.0, -1.0, ALU.add, ALU.add).then_inc(fix_mid, 1)
                dve.wait_ge(soft_ln, b + 1)
                link(V.tensor_tensor(u3, u3, u1, ALU.add))
                dve.wait_ge(soft_fix, b + 1)
                V.tensor_tensor(delta, u3, u2, ALU.add).then_inc(delta_set, 1)
                dve.wait_ge(delta_set, b + 1)
                link(V.tensor_tensor(du, delta, xa, ALU.mult))
                scan_in = ps[:, 4:6, :].rearrange("p h t -> p (h t)")

                def state(n, p, free):
                    dve.wait_ge(b_ps, n + 1)
                    if not isinstance(n, int) or n > 0:
                        dve.wait_ge(st_set, n)
                    V.tensor_tensor(ps[:, 4:6, :], du, bank(p).unsqueeze(1).to_broadcast([P, EH, S]), ALU.mult)\
                        .then_inc(dbu_set, 1)
                    dve.wait_ge(dbu_set, n + 1)
                    dve.wait_ge(dA_set, n + 1)
                    if free:
                        dve.wait_ge(hc_set, n - 1)
                    V.tensor_tensor_scan(st[p].rearrange("p h t -> p (h t)"),
                                         dA[p].rearrange("p h t -> p (h t)"), scan_in, 0.0,
                                         ALU.mult, ALU.add).then_inc(st_set, 1)

                for p in range(2):
                    state(b * NS + p, p, not first)
                with dve.Fori(1, NS // 2) as m:
                    for p in range(2):
                        state(b * NS + m * 2 + p, p, True)
                dve.wait_ge(y_sum, b * NS + NS)
                for h in range(EH):
                    link(V.scalar_tensor_tensor(out=u2[:, h, :], in0=xa[:, h, :], scalar=d_par[:, h:h + 1],
                                                in1=bank(6 + h), op0=ALU.mult, op1=ALU.add))
                V.scalar_tensor_tensor(out=u1, in0=u2, scalar=0.5, in1=zs, op0=ALU.mult, op1=ALU.mult).then_inc(yg_set, 1)
                dve.wait_ge(o_ps, b + 1)
                V.scalar_tensor_tensor(out=pre[:].rearrange("p q d -> p (q d)"), in0=x_all[:, ds(b * S, S)], scalar=2.0,
                                       in1=bank(3), op0=ALU.mult, op1=ALU.add).then_inc(o_added, 1)
                dve.wait_ge(o_added, b + 1)
                norm_stats(lambda ins: ins.then_inc(stats_set[1].sem, 1))
                norm_apply(1, b)
                take_logits(1, b)
                reuse(1, b)

            SS_STEPS = 4 + 1 + 1 + EH + NORM_STEPS
            ss(0, True)
            with steps.loop(1, NB, SS_STEPS) as b:
                ss(b, False)
            moe(1)

        @block.gpsimd
        def _(pool):
            G = nc.gpsimd
            steps = Steps(pool, pool_step)
            link = steps.link

            link(G.memset(ident[:, :], 0.0))
            G.affine_select(out=ident[:, :], in_=ident[:, :], compare_op=ALU.not_equal, fill=1.0, base=0,
                            pattern=[[-1, P]], channel_multiplier=1).then_inc(consts, 1)
            G.memset(ones[:, :], 1.0).then_inc(consts, 1)
            pool.wait_ge(consts, 2)
            G.affine_select(out=before[:, :], in_=ones[:, :], compare_op=ALU.is_gt, fill=0.0, base=0,
                            pattern=[[1, P]], channel_multiplier=-1).then_inc(consts, 1)
            link(G.memset(half[:, :], -0.5))
            link(G.memset(eps[:, 0, :], LN_EPS))
            G.memset(eps[:, 1, :], RMS_EPS).then_inc(consts, 1)
            G.memset(zero, 0.0).then_inc(zero_set, 1)
            sel3 = sel[:].rearrange("r (j m) -> r j m", m=P)
            link(G.memset(sel[:], 0.0))
            for g in range(2):
                link(G.affine_select(out=sel3, in_=sel3, compare_op=ALU.not_equal, fill=1.0,
                                     base=-g * BC, pattern=[[-1, BC], [0, P]], channel_multiplier=1))
            G.affine_select(out=sel3, in_=sel3, compare_op=ALU.not_equal, fill=1.0,
                            base=-2 * BC, pattern=[[-1, BC], [0, P]], channel_multiplier=1).then_inc(consts, 1)
            G.iota(rank8i[:, :], pattern=[[-1, NE]], base=NE, channel_multiplier=0).then_inc(consts, 1)
            G.iota(slot_rowi[:, :], pattern=[[P, ROUTED]], base=T, channel_multiplier=0).then_inc(consts, 1)
            def diagonals():
                pool.wait_ge(ld_ss, 160)
                link(G.tensor_scalar(conv[:, :, :], conv[:, :, :], 0.5, None, ALU.mult))
                for h in range(EH):
                    for k in range(KC):
                        G.tensor_scalar(diag[:, h * KC + k, :], ident[:, :], conv[:, h, k:k + 1], None, ALU.mult)\
                            .then_inc(diag_set, 1)

            def norm(l):
                def one(b):
                    if l:
                        ss(b)
                    pool.wait_ge(*stats_set[l].at(b + 1))
                    link(G.tensor_tensor(mv[:, :, 1], mv[:, :, 1], eps[:, 0, :], ALU.add))
                    G.tensor_tensor(rstd[:, :], mv[:, :, 1], half[:, :], ALU.pow).then_inc(rstd_set[l].sem, 1)
                    pool.wait_ge(*normed_set[l].at(b + 1))
                    G.tensor_copy(x_all[:, ds(b * S, S)], normed[:].rearrange("p q d -> p (q d)")).then_inc(kept[l].sem, 1)

                one(0)
                if l == 0:
                    pool.wait_ge(zero_set, 1)
                    pool.dma_start(xs[NT * P:ROWS, :].rearrange("(p c) d -> p (c d)", p=P), zero).then_inc(xs_zeroed, 16)
                with steps.loop(1, NB, 1) as b:
                    one(b)

            def ss(b):
                pool.wait_ge(ssq_set, b + 1)
                G.tensor_tensor(ssq, ssq, eps[:, 1, :], ALU.add).then_inc(rms_mid, 1)
                pool.wait_ge(rms_mid, b + 1)
                G.tensor_tensor(rms, ssq, half[:, :], ALU.pow).then_inc(rms_set, 1)
                pool.wait_ge(soft_exp, b + 1)
                pool.wait_ge(fix_mid, b + 1)
                pool.wait_ge(soft_ln, b + 1)
                G.tensor_tensor(u2, u2, du, ALU.subtract).then_inc(soft_fix, 1)

                def weigh(n, p, fresh):
                    pool.wait_ge(st_set, n + 1)
                    pool.wait_ge(cc_set, n + 1)
                    if not fresh:
                        pool.wait_ge(y_sum, n - 1)
                    G.tensor_tensor(hc[p], st[p],
                                    cc[p].unsqueeze(1).to_broadcast([P, EH, S]), ALU.mult).then_inc(hc_set, 1)

                for p in range(2):
                    weigh(b * NS + p, p, isinstance(b, int))
                with pool.Fori(1, NS // 2) as m:
                    for p in range(2):
                        weigh(b * NS + m * 2 + p, p, False)

            def moe(l):
                pool.wait_ge(*rows_set[l].at(1))
                pool.wait_ge(*kept[l].at(NB))
                pool.wait_ge(xs_zeroed, 16)
                for t in range(NT):
                    for k in range(2):
                        G.indirect_dma_start(out=xs, out_offset=bass.IndirectOffsetOnAxis(ap=rows[k][:, t:t + 1], axis=0),
                                             in_=x_all[:, t * D:(t + 1) * D], in_offset=None).then_inc(scattered[l].sem, 16)
                if l == 0:
                    diagonals()
                for k in range(4):
                    pool.wait_ge(*ys_stored[l][k].at(16 * fills(k)))
                for t in range(NT):
                    if t >= 8:
                        pool.wait_ge(*combined[l].at(t // 4 - 1))
                    for k in range(2):
                        G.indirect_dma_start(out=y_k[k][t % 8], out_offset=None, in_=ys,
                                             in_offset=bass.IndirectOffsetOnAxis(ap=rows[k][:, t:t + 1], axis=0))\
                            .then_inc(gathered[l][t % 8].sem, 16)

            norm(0)
            moe(0)
            norm(1)
            moe(1)


def kernel(**inputs):
    import concourse.bacc as bacc
    from concourse.bass_utils import run_bass_kernel_spmd

    a = {k: np.asarray(v) for k, v in inputs.items()}
    put = {"x": a["L0_attn_x"].reshape(T, D)}
    qkv = a["L0_attn_W_qkv"].reshape(D, 3, D)
    put["wq"], put["wk"], put["wv"] = qkv[:, 0], qkv[:, 1], qkv[:, 2]
    put["woT"] = a["L0_attn_W_out"].T
    up = lambda w, shared: np.concatenate([w, shared[None]]).transpose(1, 0, 2).reshape(D, -1)
    down = lambda w, shared: (np.concatenate([w, shared[None]]).reshape(NE + 1, HB, P, D)
                              .transpose(2, 0, 1, 3).reshape(P, -1))
    put["gate0"] = a["L0_ffn_gate_w"].T
    put["w1"] = up(a["L0_ffn_experts_w1"].transpose(0, 2, 1), a["L0_ffn_shared_w1"].T)
    put["w2"] = down(a["L0_ffn_experts_w2"].transpose(0, 2, 1), a["L0_ffn_shared_w2"].T)
    put["gate1"] = a["L1_ffn_w_router"]
    put["wg"] = up(a["L1_ffn_w_gate"], a["L1_ffn_ws_gate"])
    put["wu"] = up(a["L1_ffn_w_up"], a["L1_ffn_ws_up"])
    put["wd"] = down(a["L1_ffn_w_down"], a["L1_ffn_ws_down"])
    halves = lambda w: w.reshape(EH, P, -1).transpose(1, 0, 2)
    put["norm_w"] = a["L1_attn_norm_w"].reshape(P, 1)
    put["w_in"] = a["L1_attn_W_in"]
    put["conv"] = halves(a["L1_attn_conv_w"])
    w_x = halves(a["L1_attn_W_x"])
    put["w_dtl"] = w_x[:, :, :DTR]
    put["w_bc3"] = np.concatenate([w_x[:, :, DTR:]] * 3, axis=2)
    put["w_dt"] = a["L1_attn_W_dt"]
    put["b_dt"] = halves(a["L1_attn_b_dt"]).reshape(P, EH)
    put["a_log"] = halves(a["L1_attn_A_log"]).reshape(P, EH * NS)
    put["d_par"] = halves(a["L1_attn_D_param"]).reshape(P, EH)
    put["w_out"] = halves(a["L1_attn_W_out"])
    put = {k: np.ascontiguousarray(v) for k, v in put.items()}

    nc = bacc.Bacc("TRN2", target_bir_lowering=False, num_devices=1)
    args = {k: nc.dram_tensor(f"in_{k}", v.shape, mybir.dt.from_np(v.dtype), kind="ExternalInput").ap()
            for k, v in put.items()}
    out = nc.dram_tensor("out", (T, D), F32, kind="ExternalOutput").ap()
    build(nc, args, out)
    r = run_bass_kernel_spmd(nc, [{f"in_{k}": v for k, v in put.items()}], core_ids=[0])
    return r.results[0]["out"].reshape(NB, S, D)
```

```python
import numpy as np
import concourse.bass as bass
from concourse import mybir
from contextlib import ExitStack, contextmanager

F32 = mybir.dt.float32
BF16 = mybir.dt.bfloat16
I32 = mybir.dt.int32
U32 = mybir.dt.uint32
ALU = mybir.AluOpType
ACT = mybir.ActivationFunctionType
AXX = mybir.AxisListType.X
ds = bass.ds

P = 128
D = 128
NB = 4
S = 512
QT = S // P
T = NB * S
NT = T // P
NE = 8
HID = 512
HB = HID // P
ROUTED = (2 * T + NE * (P - 1)) // P
SLOTS = NT + ROUTED
ROWS = SLOTS * P
EI = 256
EH = EI // P
NS = 16
KC = 4
DTR = 64
BC = 2 * NS
LN_EPS = 1e-5
RMS_EPS = 1e-6
SCALE = float(D) ** -0.5
NEVER = -3.0e38


class Steps:

    def __init__(self, eng, sem):
        self.eng, self.sem, self.n, self.marks = eng, sem, 0, 0

    def mark(self, ins):
        ins.then_inc(self.sem, 1)
        self.n = self.n + 1
        self.marks += 1

    def link(self, ins):
        self.mark(ins)
        self.eng.wait_ge(self.sem, self.n)

    @contextmanager
    def loop(self, lo, hi, per):
        base, before = self.n, self.marks
        with self.eng.Fori(0, hi - lo) as i:
            self.n = base + i * per
            yield i + lo
            assert self.marks - before == per, (self.marks - before, per)
        self.n = base + (hi - lo) * per


class Share:

    def __init__(self, sem, base):
        self.sem, self.base = sem, base

    def at(self, n):
        return self.sem, n + self.base


def build(nc, a, out):
    ctx = ExitStack()
    with ctx:
        def sb(name, shape, dt=F32):
            return ctx.enter_context(nc.sbuf_tensor(name, shape, dt))

        def sem(name):
            return ctx.enter_context(nc.semaphore(name))

        xs = nc.dram_tensor("xs", (ROWS, D), F32).ap()
        ys = nc.dram_tensor("ys", (ROWS, D), F32).ap()

        x_all = sb("x_all", [P, T])
        ident = sb("ident", [P, P])
        ones = sb("ones", [P, P])
        before = sb("before", [P, P])
        wq = sb("wq", [P, D]); wk = sb("wk", [P, D]); wv = sb("wv", [P, D]); woT = sb("woT", [P, D])
        wqk = sb("wqk", [P, D]); wvo = sb("wvo", [P, D])
        gate = [sb(f"gate{l}", [P, NE]) for l in range(2)]
        w1 = sb("w1", [P, (NE + 1) * HID])
        w2 = sb("w2", [P, (NE + 1) * HID])
        wg = sb("wg", [P, (NE + 1) * HID])
        wu = sb("wu", [P, (NE + 1) * HID])
        wd = sb("wd", [P, (NE + 1) * HID])
        norm_w = sb("norm_w", [P, 1])
        w_in = sb("w_in", [P, 2 * EI])
        conv = sb("conv", [P, EH, KC])
        w_dtl = sb("w_dtl", [P, EH, DTR])
        w_bc3 = sb("w_bc3", [P, EH, 3 * BC])
        w_dt = sb("w_dt", [DTR, EI])
        b_dt = sb("b_dt", [P, EH])
        a_log = sb("a_log", [P, EH * NS])
        a_neg = sb("a_neg", [P, EH * NS])
        d_par = sb("d_par", [P, EH])
        w_out = sb("w_out", [P, EH, D])
        diag = sb("diag", [P, EH * KC, P])
        sel = sb("sel", [3 * BC, BC * P], BF16)
        normed = sb("normed", [P, QT, D])
        normT = sb("normT", [P, S])
        pre = sb("pre", [P, QT, D])
        stats = sb("stats", [P, QT, 6])
        stats_n = sb("stats_n", [P, QT])
        mv = sb("mv", [P, QT, 2])
        rstd = sb("rstd", [P, QT])
        half = sb("half", [P, NT])
        eps = sb("eps", [P, 2, NT])
        logits = sb("logits", [P, NT, NE])
        rank8 = sb("rank8", [P, NE]); rank8i = sb("rank8i", [P, NE], I32)
        slot_row = sb("slot_row", [P, ROUTED]); slot_rowi = sb("slot_rowi", [P, ROUTED], I32)
        eq = sb("eq", [P, NT, NE]); sc = sb("sc", [P, NT, NE]); l2 = sb("l2", [P, NT, NE])
        oh = [sb(f"oh{k}", [P, NT, NE]) for k in range(2)]
        mm = [sb(f"mm{k}", [P, NT]) for k in range(2)]
        ms = [sb(f"ms{k}", [P, NT]) for k in range(2)]
        mask = sb("mask", [P, NT, NE])
        gap = sb("gap", [P, NT]); egap = sb("egap", [P, NT]); den = sb("den", [P, NT]); zsum = sb("zsum", [P, NT])
        gates = [sb(f"gates{k}", [P, NT]) for k in range(2)]
        carry = sb("carry", [P, NE, NT])
        tot = sb("tot", [P, NE, NT]); incl = sb("incl", [P, NE, NT])
        cnt_i = sb("cnt_i", [P, NE], I32); cnt = sb("cnt", [P, NE]); ends = sb("ends", [P, NE]); offs = sb("offs", [P, NE])
        pos = sb("pos", [P, NT, NE]); posk = sb("posk", [P, NT, NE]); posf = [sb(f"posf{k}", [P, NT]) for k in range(2)]
        rows = [sb(f"rows{k}", [P, NT], U32) for k in range(2)]
        past = sb("past", [P, ROUTED, NE]); slot_ef = sb("slot_ef", [P, ROUTED])
        slot_e = sb("slot_e", [P, SLOTS], I32)
        xin = [sb(f"xin{k}", [P, D]) for k in range(4)]
        xT = [sb(f"xT{k}", [P, P]) for k in range(2)]
        wide = sb("wide", [P, 8 * HID])
        th, ga, hs, hT = ([wide[:, (2 * j + k) * HID:(2 * j + k + 1) * HID] for k in range(2)] for j in range(4))
        yout = [sb(f"yout{k}", [P, D]) for k in range(4)]
        work = sb("work", [P, 12 * 1024])

        def area(at, *shape):
            n = int(np.prod(shape))
            v = work[:, at:at + n]
            if len(shape) == 2:
                v = v.rearrange("p (a b) -> p a b", a=shape[0])
            return v

        xb = area(0, QT, D)
        xbT = area(512, S)
        qmT = area(1024, S)
        v_all = area(1536, T)
        probs = area(3584, QT, S)
        pT = [area(5632 + 512 * k, S) for k in range(2)]
        mx = area(6656, QT); nmx = area(6660, QT); rs = area(6664, QT); rinv = area(6668, QT)
        zero = area(6720, ROUTED * D)
        shared = area(0, T)
        y_k = [[area(2048 + 1024 * k + 128 * q, D) for q in range(8)] for k in range(2)]
        srt = area(4096, QT)
        xn = area(0, QT, D); xnT = area(512, S)
        xi = area(1024, EH, S + KC - 1)
        xa = area(2304, EH, S); zs = area(3328, EH, S)
        u1 = area(4352, EH, S); u2 = area(5376, EH, S); u3 = area(6400, EH, S)
        delta = area(7424, EH, S); du = area(8448, EH, S)
        ssq = area(12032, NT); rms = area(12032 + NT, NT)
        res = area(9472, S)
        dA = [area(9984 + 1024 * k, EH, S) for k in range(2)]
        st, hc = ([wide[:, (2 * j + k) * EH * S:(2 * j + k + 1) * EH * S].rearrange("p (h t) -> p h t", h=EH)
                   for k in range(2)] for j in range(2))

        def halves_in(w, at):
            return w[:, at:at + EH * S].rearrange("p (h t) -> p h t", h=EH)

        dbu = [halves_in(w1, k * EH * S) for k in range(2)]
        yg = halves_in(w1, 2 * EH * S); one_w = halves_in(w1, 3 * EH * S)
        cc = [w2[:, k * S:(k + 1) * S] for k in range(2)]
        dts = w2[0:DTR, 2 * S:3 * S]
        sq = w2[:, 3 * S:4 * S]
        hc += [halves_in(w2, (4 + k * EH) * S) for k in range(2)]
        d_diag = [wq, wk]
        hi = sb("hi", [3 * BC, S], BF16); mid = sb("mid", [3 * BC, S], BF16)
        parts = sb("parts", [3 * BC, S], BF16)
        ps = ctx.enter_context(nc.psum_tensor("ps", [P, 8, 512], F32))

        def bank(k, n=512):
            return ps[:, k, 0:n]

        def tile_of(ap, t):
            return ap[:, ds(t * D, D)]

        def tiles(ap):
            return ap.rearrange("p (q d) -> p q d", d=D)

        def layers(name, per_layer):
            s = sem(name)
            return [Share(s, l * per_layer) for l in range(2)]

        def fills(k):
            return (SLOTS - k + 3) // 4

        ld_x = sem("ld_x"); ld_gate = sem("ld_gate"); ld_att = sem("ld_att"); ld_f0 = sem("ld_f0"); ld_f1 = sem("ld_f1"); ld_ss = sem("ld_ss")
        zero_set = sem("zero_set"); xs_zeroed = sem("xs_zeroed")
        consts = sem("consts"); diag_set = sem("diag_set")
        w_ps = sem("w_ps"); w_set = sem("w_set")
        pool_step = sem("pool_step"); dve_step = sem("dve_step"); act_step = sem("act_step")
        xb_loaded = sem("xb_loaded"); xbT_ps = sem("xbT_ps"); xbT_set = sem("xbT_set")
        qm_ps = sem("qm_ps"); qmT_set = sem("qmT_set"); v_ps = sem("v_ps"); v_set = sem("v_set")
        scores_ps = sem("scores_ps"); nmax_set = sem("nmax_set"); probs_set = sem("probs_set")
        pT_ps = sem("pT_ps"); pT_set = sem("pT_set"); ctx_ps = sem("ctx_ps"); ctx_added = sem("ctx_added")
        stats_set = layers("stats_set", NB); rstd_set = layers("rstd_set", NB)
        normed_set = layers("normed_set", NB); kept = layers("kept", NB)
        xs_stored = layers("xs_stored", 16 * NB)
        nT_ps = layers("nT_ps", NB); nT_set = layers("nT_set", NB)
        logit_ps = layers("logit_ps", NB); logits_set = layers("logits_set", NB)
        mask_set = layers("mask_set", 1); count_ps = layers("count_ps", 1)
        counts_taken = layers("counts_taken", 1)
        gap_set = layers("gap_set", 1); egap_set = layers("egap_set", 1)
        rows_set = layers("rows_set", 2); scattered = layers("scattered", 16 * 2 * NT)
        xin_loaded_ = [layers(f"xin_loaded{k}", 16 * fills(k)) for k in range(4)]
        xin_loaded = [[r[l] for r in xin_loaded_] for l in range(2)]
        x_ps = layers("x_ps", SLOTS); xT_set = layers("xT_set", SLOTS)
        h_ps = layers("h_ps", SLOTS); th_set = layers("th_set", SLOTS)
        hs_set = layers("hs_set", SLOTS); hT_ps = layers("hT_ps", SLOTS)
        hT_set = layers("hT_set", SLOTS); y_ps = layers("y_ps", SLOTS)
        yout_set = layers("yout_set", SLOTS)
        ys_stored_ = [layers(f"ys_stored{k}", 16 * fills(k)) for k in range(4)]
        ys_stored = [[r[l] for r in ys_stored_] for l in range(2)]
        shared_loaded = layers("shared_loaded", 16)
        gathered_ = [layers(f"gathered{k}", 64) for k in range(8)]
        gathered = [[r[l] for r in gathered_] for l in range(2)]
        rms_mid = sem("rms_mid"); fix_mid = sem("fix_mid")
        combined = layers("combined", NB); var_set = layers("var_set", NB)
        std_set = layers("std_set", NB); layer_out = layers("layer_out", NB)
        out_stored = sem("out_stored")
        a_set = sem("a_set"); ssq_set = sem("ssq_set"); rms_set = sem("rms_set"); xn_set = sem("xn_set")
        xn_ps = sem("xn_ps"); xnT_set = sem("xnT_set"); xi_ps = sem("xi_ps"); z_ps = sem("z_ps"); xi_set = sem("xi_set")
        conv_ps = sem("conv_ps"); conv_th = sem("conv_th"); z_th = sem("z_th"); xa_set = sem("xa_set")
        zs_set = sem("zs_set"); dtl_ps = sem("dtl_ps"); bc_ps = sem("bc_ps"); dts_set = sem("dts_set"); hi_set = sem("hi_set")
        parts_set = sem("parts_set"); dl_ps = sem("dl_ps"); soft_abs = sem("soft_abs"); soft_exp = sem("soft_exp")
        soft_ln = sem("soft_ln"); soft_fix = sem("soft_fix"); du_set = sem("du_set"); delta_set = sem("delta_set")
        b_ps = sem("b_ps"); c_ps = sem("c_ps"); dA_set = sem("dA_set"); cc_set = sem("cc_set")
        dbu_set = sem("dbu_set"); st_set = sem("st_set"); hc_set = sem("hc_set"); y_sum = sem("y_sum")
        yg_set = sem("yg_set"); o_ps = sem("o_ps"); o_added = sem("o_added")

        block = ctx.enter_context(nc.Block())

        LOOP_LO = 9
        LOOP_TRIPS = (SLOTS - 2 - LOOP_LO) // 4
        COUNT_STEP, EGAP_STEP = -1, 1

        def slot_steps(loop, step):
            for i in range(-2, LOOP_LO):
                step(0, i)
            with loop as m:
                for k in range(4):
                    step(m, LOOP_LO + k)
            for i in range(LOOP_LO + 4 * LOOP_TRIPS, SLOTS + 1):
                step(0, i)

        before_ps, tiles_ps = (ps[:, 0, P + k * NT * NE:P + (k + 1) * NT * NE] for k in range(2))

        def valid(i, n=SLOTS):
            return not isinstance(i, int) or 0 <= i < n

        def wait_pos(eng, s, value):
            if isinstance(value, int) and value <= 0:
                return
            eng.wait_ge(*s.at(value))

        @block.sync
        def _(sp):
            def load_seq(b):
                if not isinstance(b, int):
                    sp.wait_ge(xbT_ps, b)
                sp.dma_start(xb, a["x"][ds(b * S, S), :].rearrange("(q p) d -> p q d", p=P)).then_inc(xb_loaded, 16)

            def load_weights(done, *pairs):
                for dst, name in pairs:
                    sp.dma_start(dst[:], a[name]).then_inc(done, 16)

            load_seq(0)
            load_weights(ld_att, (wq, "wq"), (wk, "wk"), (wv, "wv"), (woT, "woT"))
            load_weights(ld_gate, (gate[0], "gate0"), (gate[1], "gate1"))
            sp.dma_start(x_all[:].rearrange("p (t d) -> p t d", d=D),
                         a["x"].rearrange("(t p) d -> p t d", p=P)).then_inc(ld_x, 16)
            with sp.Fori(1, NB) as b:
                load_seq(b)
            load_weights(ld_ss, (norm_w, "norm_w"), (w_in, "w_in"), (conv, "conv"), (w_dtl, "w_dtl"), (w_bc3, "w_bc3"),
                         (w_dt, "w_dt"), (b_dt, "b_dt"), (a_log, "a_log"), (d_par, "d_par"), (w_out, "w_out"))

            def moe(l):
                def keep_rows(b):
                    sp.wait_ge(*normed_set[l].at(b + 1))
                    sp.dma_start(xs[ds(b * S, S), :].rearrange("(q p) d -> p q d", p=P),
                                 normed[:, :, :]).then_inc(xs_stored[l].sem, 16)

                def load(i, k):
                    if not isinstance(i, int) or i >= 4:
                        sp.wait_ge(*x_ps[l].at(i - 3))
                    sp.dma_start(xin[k % 4][:, :], xs[ds(i * P, P), :]).then_inc(xin_loaded[l][k % 4].sem, 16)

                with sp.Fori(0, NB - 1) as b:
                    keep_rows(b)
                sp.wait_ge(*xs_stored[l].at(16 * (NB - 1)))
                for i in range(4):
                    load(i, i)
                keep_rows(NB - 1)
                sp.wait_ge(*xs_stored[l].at(16 * NB))
                with sp.Fori(0, (NT - 4) // 4) as m:
                    for k in range(4):
                        load(m * 4 + (k + 4), k)
                sp.wait_ge(*scattered[l].at(16 * 2 * NT))
                trips = ROUTED // 4
                with sp.Fori(0, trips) as m:
                    for k in range(4):
                        load(m * 4 + (NT + k), k)
                for i in range(NT + 4 * trips, SLOTS):
                    load(i, i)
                if l == 0:
                    load_weights(ld_f1, (wg, "wg"), (wu, "wu"), (wd, "wd"))
                for k in range(4):
                    sp.wait_ge(*ys_stored[l][k].at(16 * fills(k)))
                sp.dma_start(tiles(shared), ys[0:T, :].rearrange("(t p) d -> p t d", p=P)).then_inc(shared_loaded[l].sem, 16)

            moe(0)
            moe(1)
            with sp.Fori(0, NB) as b:
                sp.wait_ge(*layer_out[1].at(b + 1))
                sp.dma_start(out[ds(b * S, S), :].rearrange("(q p) d -> p q d", p=P),
                             tiles(x_all[:, ds(b * S, S)])).then_inc(out_stored, 16)
            sp.wait_ge(out_stored, 16 * NB)

        @block.tensor
        def _(pe):
            mm_ = nc.tensor.matmul
            tr = nc.tensor.transpose
            pe.wait_ge(ld_att, 64)
            mm_(bank(5, P), wq[:, :], wk[:, :], start=True, stop=True).then_inc(w_ps, 1)
            mm_(bank(6, P), wv[:, :], woT[:, :], start=True, stop=True).then_inc(w_ps, 1)
            pe.wait_ge(consts, 4)
            pe.wait_ge(w_set, 2)

            def project(b):
                pe.wait_ge(xb_loaded, b * 16 + 16)
                for q in range(QT):
                    last = tr(ps[:, 6, q * P:(q + 1) * P], xb[:, q, :], ident[:, :])
                last.then_inc(xbT_ps, 1)
                pe.wait_ge(xbT_set, b + 1)
                mm_(bank(5), wqk[:, :], xbT, start=True, stop=True).then_inc(qm_ps, 1)
                for q in range(QT):
                    last = mm_(ps[:, 6, q * P:(q + 1) * P], xbT[:, q * P:(q + 1) * P], wvo[:, :], start=True, stop=True)
                last.then_inc(v_ps, 1)

            def router(l, b):
                pe.wait_ge(*normed_set[l].at(b + 1))
                for q in range(QT):
                    last = tr(ps[:, 5, q * P:(q + 1) * P], normed[:, q, :], ident[:, :])
                last.then_inc(nT_ps[l].sem, 1)
                pe.wait_ge(*nT_set[l].at(b + 1))
                for q in range(QT):
                    last = mm_(ps[:, 6, q * NE:(q + 1) * NE], normT[:, q * P:(q + 1) * P], gate[l][:, :],
                               start=True, stop=True)
                last.then_inc(logit_ps[l].sem, 1)
                pe.wait_ge(*logits_set[l].at(b + 1))

            def attend(b, first, final):
                pe.wait_ge(qmT_set, b + 1)
                for q in range(QT):
                    mm_(bank(q), qmT[:, q * P:(q + 1) * P], xbT, start=True, stop=True).then_inc(scores_ps, 1)
                pe.wait_ge(v_set, b + 1)
                if not final:
                    project(b + 1)

                def turn(q):
                    pe.wait_ge(probs_set, b * QT + (q + 1))
                    if q > 0 or not first:
                        pe.wait_ge(pT_set, b * QT + q)
                    for k in range(QT):
                        last = tr(ps[:, 7, k * P:(k + 1) * P], probs[:, q, k * P:(k + 1) * P], ident[:, :])
                    last.then_inc(pT_ps, 1)

                def context(q):
                    pe.wait_ge(pT_set, b * QT + (q + 1))
                    if q == 0 and not first:
                        pe.wait_ge(ctx_added, b)
                    for k in range(QT):
                        last = mm_(ps[:, 4, q * P:(q + 1) * P], pT[q % 2][:, k * P:(k + 1) * P],
                                   tile_of(v_all, b * QT + k), start=(k == 0), stop=(k == QT - 1))
                    last.then_inc(ctx_ps, 1)

                turn(0)
                for q in range(QT):
                    if q + 1 < QT:
                        turn(q + 1)
                    context(q)
                if not first:
                    router(0, b - 1)

            project(0)
            attend(0, True, False)
            pe.wait_ge(ld_gate, 32)
            with pe.Fori(1, NB - 1) as b:
                attend(b, False, False)
            attend(NB - 1, False, True)
            router(0, NB - 1)

            def moe(l):
                wa, wb, wc = ((w1, None, w2), (wg, wu, wd))[l]
                hbank = (4, 6)
                pe.wait_ge(*((ld_f0, 32), (ld_f1, 48))[l])

                def counts():
                    pe.wait_ge(*mask_set[l].at(1))
                    pe.wait_ge(*xT_set[l].at(COUNT_STEP + 2))
                    flat = mask[:, :, :].rearrange("p t e -> p (t e)")
                    mm_(before_ps, before[:, :], flat, start=True, stop=True)
                    mm_(tiles_ps, ones[:, :], flat, start=True, stop=True).then_inc(count_ps[l].sem, 1)
                    pe.wait_ge(*counts_taken[l].at(1))

                expert = {}

                def expert_of(i, k):
                    if isinstance(i, int):
                        expert.clear()
                        if i < NT:
                            return NE * HID
                        return pe.value_load(slot_e[0:1, i:i + 1], min_val=0, max_val=NE * HID)
                    if k not in expert:
                        expert[k] = pe.value_load(slot_e[0:1, ds(i, 1)], min_val=0, max_val=NE * HID)
                    return expert[k]

                def step(m, k):
                    i = m * 4 + k
                    x, h, t, y = i + 2, i + 1, i, i - 1
                    if isinstance(m, int) and i == COUNT_STEP:
                        counts()
                    if isinstance(m, int) and i == LOOP_LO - 1:
                        pe.wait_ge(*rows_set[l].at(2))
                    if valid(x):
                        q = (k + 2) % 4
                        pe.wait_ge(*xin_loaded[l][q].at((m + (k + 2) // 4 + 1) * 16))
                        wait_pos(pe, xT_set[l], x)
                        tr(bank(0, P), xin[q][:, :], ident[:, :]).then_inc(x_ps[l].sem, 1)
                    if valid(h):
                        p = (k + 1) % 2
                        e = expert_of(h, k + 1)
                        pe.wait_ge(*xT_set[l].at(h + 1))
                        wait_pos(pe, hs_set[l], h - 1)
                        last = mm_(bank(hbank[0] + p), xT[p][:, :], wa[:, ds(e, HID)], start=True, stop=True)
                        if wb is not None:
                            last = mm_(bank(hbank[1] + p), xT[p][:, :], wb[:, ds(e, HID)], start=True, stop=True)
                        last.then_inc(h_ps[l].sem, 1)
                        if not isinstance(h, int) and k < LOOP_LO + 3:
                            expert_of(h + 1, k + 2)
                    if valid(t):
                        p = k % 2
                        pe.wait_ge(*hs_set[l].at(t + 1))
                        wait_pos(pe, hT_set[l], t - 1)
                        for j in range(HB):
                            last = tr(ps[:, 2 + p, j * P:(j + 1) * P], hs[p][:, j * P:(j + 1) * P], ident[:, :])
                        last.then_inc(hT_ps[l].sem, 1)
                    if valid(y):
                        p = (k - 1) % 2
                        e = expert_of(y, k - 1)
                        pe.wait_ge(*hT_set[l].at(y + 1))
                        wait_pos(pe, yout_set[l], y)
                        for j in range(HB):
                            last = mm_(bank(1, D), hT[p][:, j * P:(j + 1) * P], wc[:, ds(e + j * D, D)],
                                       start=(j == 0), stop=(j == HB - 1))
                        last.then_inc(y_ps[l].sem, 1)

                slot_steps(pe.Fori(0, LOOP_TRIPS), step)

            moe(0)

            pe.wait_ge(ld_ss, 160)
            pe.wait_ge(diag_set, EH * KC + EH)
            pe.wait_ge(consts, 5)
            pe.wait_ge(a_set, 2)

            def turn_xn(x):
                pe.wait_ge(xn_set, x + 1)
                for q in range(QT):
                    last = tr(ps[:, 5, q * P:(q + 1) * P], xn[:, q, :], ident[:, :])
                last.then_inc(xn_ps, 1)

            def project_x(x):
                pe.wait_ge(xnT_set, x + 1)
                for h in range(EH):
                    mm_(bank(5 - h), w_in[:, h * P:(h + 1) * P], xnT, start=True, stop=True).then_inc(xi_ps, 1)

            def convolve(x, h, taps):
                if taps[0] == 0:
                    pe.wait_ge(xi_set, x * EH + (h + 1))
                for k in taps:
                    last = mm_(bank(5 - h), diag[:, h * KC + k, :], xi[:, h, k:k + S], start=(k == 0), stop=(k == KC - 1))
                if taps[-1] == KC - 1:
                    last.then_inc(conv_ps, 1)

            def project_dt_low(x):
                pe.wait_ge(xa_set, x * EH + EH)
                for h in range(EH):
                    last = mm_(ps[0:DTR, 5, :], w_dtl[:, h, :], xa[:, h, :], start=(h == 0), stop=(h == EH - 1))
                last.then_inc(dtl_ps, 1)

            def project_dt(x):
                pe.wait_ge(dts_set, x + 1)
                for h in range(EH):
                    last = mm_(bank(4 + h), w_dt[:, h * P:(h + 1) * P], dts, start=True, stop=True)
                last.then_inc(dl_ps, 1)

            def project_bc(x):
                for h in range(EH):
                    last = mm_(ps[0:3 * BC, 3, :], w_bc3[:, h, :], xa[:, h, :], start=(h == 0), stop=(h == EH - 1))
                last.then_inc(bc_ps, 1)

            def project_z(b):
                pe.wait_ge(soft_abs, b + 1)
                for h in range(EH):
                    mm_(bank(3 + h), w_in[:, EI + h * P:EI + (h + 1) * P], xnT, start=True, stop=True).then_inc(z_ps, 1)

            def project_out(b):
                for q in range(QT):
                    for h in range(EH):
                        last = mm_(ps[:, 3, q * P:(q + 1) * P], yg[:, h, q * P:(q + 1) * P], w_out[:, h, :],
                                   start=(h == 0), stop=(h == EH - 1))
                last.then_inc(o_ps, 1)

            def turn_normed(b):
                pe.wait_ge(*normed_set[1].at(b + 1))
                for q in range(QT):
                    last = tr(ps[:, 3, q * P:(q + 1) * P], normed[:, q, :], ident[:, :])
                last.then_inc(nT_ps[1].sem, 1)

            def route_out(b):
                pe.wait_ge(*nT_set[1].at(b + 1))
                for q in range(QT):
                    last = mm_(ps[:, 3, q * NE:(q + 1) * NE], normT[:, q * P:(q + 1) * P], gate[1][:, :],
                               start=True, stop=True)
                last.then_inc(logit_ps[1].sem, 1)

            def spread_b(n, j):
                if not isinstance(n, int) or n >= 2:
                    pe.wait_ge(dbu_set, n - 1)
                mm_(bank(j % 2), sel[:, j * P:(j + 1) * P], parts[:, :], start=True, stop=True).then_inc(b_ps, 1)

            def spread_c(n, j):
                if not isinstance(n, int) or n >= 1:
                    pe.wait_ge(cc_set, n)
                mm_(bank(2), sel[:, (j + NS) * P:(j + NS + 1) * P], parts[:, :], start=True, stop=True).then_inc(c_ps, 1)

            def add_up(n, j):
                pe.wait_ge(hc_set, n + 1)
                for h in range(EH):
                    last = mm_(bank(6 + h), ident[:, :], hc[j % 4][:, h, :], start=False, stop=(j == NS - 1))
                last.then_inc(y_sum, 1)

            def states(b, after, before):
                pe.wait_ge(parts_set, b + 1)
                spread_b(b * NS, 0)
                if after:
                    add_up(b * NS - 2, NS - 2)
                for j in range(NS):
                    if j < NS - 1:
                        spread_b(b * NS + (j + 1), j + 1)
                    spread_c(b * NS + j, j)
                    if j == 0:
                        project_z(b)
                        if after:
                            add_up(b * NS - 1, NS - 1)
                    if j == 1 and before:
                        turn_xn(b + 1)
                    if j == 2:
                        if after:
                            pe.wait_ge(yg_set, b)
                        for h in range(EH):
                            mm_(bank(6 + h), d_diag[h][:, :], xa[:, h, :], start=True, stop=False)
                    if j == 3:
                        pe.wait_ge(zs_set, b * EH + EH)
                        if before:
                            project_x(b + 1)
                        if after:
                            project_out(b - 1)
                    if after:
                        if j == 8:
                            turn_normed(b - 1)
                        if j == 9:
                            route_out(b - 1)
                    if before:
                        if j in (4, 5):
                            convolve(b + 1, 0, ((0, 1), (2, 3))[j - 4])
                        if j in (6, 7):
                            convolve(b + 1, 1, ((0, 1), (2, 3))[j - 6])
                        if j == 9:
                            project_dt_low(b + 1)
                        if j == 10:
                            project_dt(b + 1)
                        if j == 11:
                            if after:
                                pe.wait_ge(*logits_set[1].at(b))
                            project_bc(b + 1)
                    if j >= 2:
                        add_up(b * NS + (j - 2), j - 2)

            turn_xn(0)
            project_x(0)
            for h in range(EH):
                convolve(0, h, range(KC))
            project_dt_low(0)
            project_dt(0)
            project_bc(0)
            states(0, False, True)
            with pe.Fori(1, NB - 1) as b:
                states(b, True, True)
            states(NB - 1, True, False)
            for k in (2, 1):
                add_up(NB * NS - k, NS - k)
            pe.wait_ge(yg_set, NB)
            project_out(NB - 1)
            turn_normed(NB - 1)
            route_out(NB - 1)
            moe(1)

        @block.scalar
        def _(act):
            A = nc.scalar.activation
            steps = Steps(act, act_step)

            def cp(dst, src, **kw):
                return A(dst, src, ACT.Copy, **kw)

            act.wait_ge(w_ps, 1)
            cp(wqk[:, :], bank(5, P)).then_inc(w_set, 1)
            act.wait_ge(w_ps, 2)
            cp(wvo[:, :], bank(6, P)).then_inc(w_set, 1)

            def project(b):
                act.wait_ge(xbT_ps, b + 1)
                cp(xbT, bank(6)).then_inc(xbT_set, 1)

            def values(b):
                act.wait_ge(v_ps, b + 1)
                cp(v_all[:, ds(b * S, S)], bank(6)).then_inc(v_set, 1)

            def router(l, b, k=5):
                act.wait_ge(*nT_ps[l].at(b + 1))
                cp(normT[:, :], bank(k)).then_inc(nT_set[l].sem, 1)

            def attend(b, first, final):
                def soften(q):
                    act.wait_ge(nmax_set, b * QT + (q + 1))
                    A(probs[:, q, :], bank(q), ACT.Exp, bias=nmx[:, q:q + 1], scale=SCALE,
                      accum_out=rs[:, q:q + 1]).then_inc(probs_set, 1)

                for q in range(QT - 1):
                    soften(q)
                if not final:
                    project(b + 1)
                soften(QT - 1)
                if not final:
                    values(b + 1)
                for q in range(QT):
                    act.wait_ge(pT_ps, b * QT + (q + 1))
                    cp(pT[q % 2], bank(7)).then_inc(pT_set, 1)
                if not first:
                    router(0, b - 1)

            project(0)
            values(0)
            attend(0, True, False)
            act.dma_start(w1[:], a["w1"]).then_inc(ld_f0, 16)
            with act.Fori(1, NB - 1) as b:
                attend(b, False, False)
            act.dma_start(w2[:], a["w2"]).then_inc(ld_f0, 16)
            attend(NB - 1, False, True)
            router(0, NB - 1)

            def moe(l):
                def exp_gaps():
                    act.wait_ge(*gap_set[l].at(1))
                    A(egap[:, :], gap[:, :], ACT.Exp).then_inc(egap_set[l].sem, 1)
                    if l:
                        act.wait_ge(*gap_set[l].at(2))
                        A(sc[:, :, :], l2[:, :, :], ACT.Exp).then_inc(egap_set[l].sem, 1)

                def step(m, k):
                    i = m * 4 + k
                    h, t, y = i + 1, i, i - 1
                    if isinstance(m, int) and i == EGAP_STEP:
                        exp_gaps()
                    if valid(h):
                        p = (k + 1) % 2
                        act.wait_ge(*h_ps[l].at(h + 1))
                        wait_pos(act, hs_set[l], h - 1)
                        A(th[p], bank(4 + p), ACT.Tanh, scale=0.5).then_inc(th_set[l].sem, 1)
                    if valid(t):
                        p = k % 2
                        act.wait_ge(*hT_ps[l].at(t + 1))
                        wait_pos(act, y_ps[l], t - 1)
                        cp(hT[p], bank(2 + p)).then_inc(hT_set[l].sem, 1)
                    if valid(y):
                        q = (k - 1) % 4
                        act.wait_ge(*y_ps[l].at(y + 1))
                        wait_pos(act, ys_stored[l][q], (m + (k - 1) // 4) * 16)
                        A(yout[q][:, :], bank(1, D), ACT.Copy, scale=0.5).then_inc(yout_set[l].sem, 1)
                        act.wait_ge(*yout_set[l].at(y + 1))
                        act.dma_start(ys[ds(y * P, P), :], yout[q][:, :]).then_inc(ys_stored[l][q].sem, 16)

                slot_steps(act.Fori(0, LOOP_TRIPS), step)

                with act.Fori(0, NB) as b:
                    act.wait_ge(*var_set[l].at(b + 1))
                    A(srt, mv[:, :, 1], ACT.Sqrt).then_inc(std_set[l].sem, 1)
                    if l == 0:
                        act.wait_ge(*layer_out[0].at(b + 1))
                        for q in range(QT):
                            last = A(sq[:, q * D:(q + 1) * D], tile_of(x_all, b * QT + q), ACT.Square, scale=D ** -0.5,
                                     accum_out=ssq[:, ds(b * QT + q, 1)])
                        last.then_inc(ssq_set, 1)

            moe(0)

            act.wait_ge(ld_ss, 160)
            A(a_neg[:, :], a_log[:, :], ACT.Exp).then_inc(a_set, 1)

            def scale_rows(x):
                for q in range(QT):
                    last = A(xn[:, q, :], tile_of(x_all, x * QT + q), ACT.Copy, scale=rms[:, ds(x * QT + q, 1)])
                last.then_inc(xn_set, 1)

            def take_xnT(x):
                act.wait_ge(xn_ps, x + 1)
                A(xnT, bank(5), ACT.Copy, scale=norm_w[:, 0:1]).then_inc(xnT_set, 1)

            def take_xi(x):
                for h in range(EH):
                    act.wait_ge(xi_ps, x * EH + (h + 1))
                    cp(xi[:, h, KC - 1:KC - 1 + S], bank(5 - h)).then_inc(xi_set, 1)

            def tanh_conv(x, h):
                act.wait_ge(conv_ps, x * EH + (h + 1))
                A(u1[:, h, :], bank(5 - h), ACT.Tanh).then_inc(conv_th, 1)

            def take_dt_low(x):
                act.wait_ge(dtl_ps, x + 1)
                cp(dts, ps[0:DTR, 5, :]).then_inc(dts_set, 1)

            def soft_parts(x):
                act.wait_ge(dl_ps, x + 1)
                act.wait_ge(xa_set, x * EH + EH)
                for h in range(EH):
                    steps.mark(A(u1[:, h, :], bank(4 + h), ACT.Abs, bias=b_dt[:, h:h + 1]))
                for h in range(EH):
                    last = A(u3[:, h, :], bank(4 + h), ACT.Relu, bias=b_dt[:, h:h + 1])
                last.then_inc(soft_abs, 1)
                act.wait_ge(act_step, steps.n)
                A(u2, u1, ACT.Exp, scale=-1.0).then_inc(soft_exp, 1)

            def take_hi(x):
                act.wait_ge(bc_ps, x + 1)
                cp(hi[:, :], ps[0:3 * BC, 3, :]).then_inc(hi_set, 1)

            def soft_log(x):
                act.wait_ge(soft_exp, x + 1)
                A(u1, u2, ACT.Ln, bias=1.0).then_inc(soft_ln, 1)

            def tanh_z(b):
                for h in range(EH):
                    act.wait_ge(z_ps, b * EH + (h + 1))
                    A(u2[:, h, :], bank(3 + h), ACT.Tanh, scale=0.5).then_inc(z_th, 1)

            def keep(b):
                act.wait_ge(*normed_set[1].at(b + 1))
                cp(x_all[:, ds(b * S, S)], normed[:].rearrange("p q d -> p (q d)")).then_inc(kept[1].sem, 1)

            def decay(n, j):
                if not isinstance(n, int) or n >= 2:
                    act.wait_ge(st_set, n - 1)
                for h in range(EH):
                    lo = 1 if h else 0
                    last = A(dA[j % 2][:, h, lo:S], delta[:, h, lo:S], ACT.Exp, scale=a_neg[:, j + h * NS:j + h * NS + 1])
                last.then_inc(dA_set, 1)

            def take_c(n, j):
                act.wait_ge(c_ps, n + 1)
                if not isinstance(n, int) or n >= 2:
                    act.wait_ge(hc_set, n - 1)
                cp(cc[j % 2], bank(2)).then_inc(cc_set, 1)

            def states(b, after, before):
                act.wait_ge(delta_set, b + 1)
                decay(b * NS, 0)
                for j in range(NS):
                    if j < NS - 1:
                        decay(b * NS + (j + 1), j + 1)
                    take_c(b * NS + j, j)
                    if j == 0 and before:
                        scale_rows(b + 1)
                    if j == 1:
                        tanh_z(b)
                    if after:
                        if j == 7:
                            keep(b - 1)
                        if j == 8:
                            router(1, b - 1, 3)
                    if before:
                        if j == 1:
                            take_xnT(b + 1)
                        if j == 3:
                            take_xi(b + 1)
                        if j == 5:
                            tanh_conv(b + 1, 0)
                        if j == 7:
                            tanh_conv(b + 1, 1)
                        if j == 9:
                            take_dt_low(b + 1)
                        if j == 10:
                            soft_parts(b + 1)
                        if j == 12:
                            take_hi(b + 1)
                        if j == 12:
                            soft_log(b + 1)

            act.wait_ge(rms_set, 1)
            scale_rows(0)
            take_xnT(0)
            take_xi(0)
            for h in range(EH):
                tanh_conv(0, h)
            take_dt_low(0)
            soft_parts(0)
            soft_log(0)
            take_hi(0)
            states(0, False, True)
            with steps.loop(1, NB - 1, EH) as b:
                states(b, True, True)
            states(NB - 1, True, False)
            router(1, NB - 1, 3)
            keep(NB - 1)
            moe(1)

        @block.vector
        def _(dve):
            V = nc.vector
            steps = Steps(dve, dve_step)
            link = steps.link

            def take_qm(b):
                dve.wait_ge(qm_ps, b + 1)
                V.tensor_copy(qmT, bank(5)).then_inc(qmT_set, 1)

            def take_logits(l, b, k=6):
                dve.wait_ge(*logit_ps[l].at(b + 1))
                V.tensor_copy(logits[:].rearrange("p t e -> p (t e)")[:, ds(b * QT * NE, QT * NE)],
                              ps[:, k, 0:QT * NE]).then_inc(logits_set[l].sem, 1)

            def norm_stats(done):
                for q in range(QT):
                    steps.mark(V.bn_stats(stats[:, q, :], pre[:, q, :]))
                dve.wait_ge(dve_step, steps.n)
                V.tensor_copy(stats_n[:, :], stats[:, :, 0])
                for q in range(QT - 1):
                    V.bn_aggr(mv[:, q, :], stats[:, q, :])
                done(V.bn_aggr(mv[:, QT - 1, :], stats[:, QT - 1, :]))

            NORM_STEPS = QT
            COMBINE_STEPS = 3 * QT - 1 + NORM_STEPS + 2

            def norm_apply(l, b):
                dve.wait_ge(*rstd_set[l].at(b + 1))
                for q in range(QT):
                    last = V.tensor_scalar(normed[:, q, :], pre[:, q, :], mv[:, q, 0:1], rstd[:, q:q + 1],
                                           ALU.subtract, ALU.mult)
                last.then_inc(normed_set[l].sem, 1)

            def reuse(l, b):
                dve.wait_ge(*xs_stored[l].at(b * 16 + 16))
                dve.wait_ge(*kept[l].at(b + 1))

            def attend_norm(b):
                dve.wait_ge(ctx_ps, b * QT + QT)
                for q in range(QT):
                    last = V.scalar_tensor_tensor(out=pre[:, q, :], in0=ps[:, 4, q * P:(q + 1) * P],
                                                  scalar=rinv[:, q:q + 1], in1=tile_of(x_all, b * QT + q),
                                                  op0=ALU.mult, op1=ALU.add)
                last.then_inc(ctx_added, 1)
                dve.wait_ge(ctx_added, b + 1)
                norm_stats(lambda ins: ins.then_inc(stats_set[0].sem, 1))
                norm_apply(0, b)

            ATT_NORM = NORM_STEPS

            def attend(b, first, final):
                for q in range(QT):
                    dve.wait_ge(scores_ps, b * QT + (q + 1))
                    link(V.reduce_max(mx[:, q:q + 1], bank(q), AXX))
                    V.tensor_scalar(nmx[:, q:q + 1], mx[:, q:q + 1], -SCALE, None, ALU.mult).then_inc(nmax_set, 1)
                if not final:
                    take_qm(b + 1)
                if not first:
                    attend_norm(b - 1)
                    take_logits(0, b - 1)
                    reuse(0, b - 1)
                dve.wait_ge(probs_set, b * QT + QT)
                link(V.reciprocal(rinv, rs))

            take_qm(0)
            dve.wait_ge(ld_x, 16)
            attend(0, True, False)
            with steps.loop(1, NB - 1, QT + 1 + ATT_NORM) as b:
                attend(b, False, False)
            attend(NB - 1, False, True)
            attend_norm(NB - 1)
            take_logits(0, NB - 1)

            dve.wait_ge(consts, 7)
            link(V.tensor_copy(rank8[:, :], rank8i[:, :]))
            link(V.tensor_copy(slot_row[:, :], slot_rowi[:, :]))
            link(V.memset(carry[:, :, :], 1.0))
            link(V.memset(carry[:, :, 0:1], 0.0))
            link(V.memset(slot_e[:, 0:NT], NE * HID))

            def moe(l):
                tok_exp = [P, NT, NE]

                def over_e(ap):
                    return ap.unsqueeze(2).to_broadcast(tok_exp)

                def over_t(ap):
                    return ap.unsqueeze(1).to_broadcast(tok_exp)

                def routing():
                    dve.wait_ge(*logits_set[l].at(NB))
                    src = logits
                    for k in range(2):
                        link(V.reduce_max(mm[k][:, :], src[:, :, :], AXX))
                        link(V.tensor_tensor(eq[:, :, :], src[:, :, :], over_e(mm[k][:, :]), ALU.is_equal))
                        link(V.tensor_tensor(sc[:, :, :], eq[:, :, :], over_t(rank8[:, :]), ALU.mult))
                        link(V.reduce_max(ms[k][:, :], sc[:, :, :], AXX))
                        link(V.tensor_tensor(oh[k][:, :, :], sc[:, :, :], over_e(ms[k][:, :]), ALU.is_equal))
                        if k == 0:
                            link(V.scalar_tensor_tensor(out=l2[:, :, :].rearrange("p t e -> p (t e)"),
                                                        in0=oh[0][:, :, :].rearrange("p t e -> p (t e)"), scalar=NEVER,
                                                        in1=logits[:, :, :].rearrange("p t e -> p (t e)"),
                                                        op0=ALU.mult, op1=ALU.add))
                            src = l2
                        yield
                    V.tensor_tensor(mask[:, :, :], oh[0][:, :, :], oh[1][:, :, :], ALU.add).then_inc(mask_set[l].sem, 1)
                    V.tensor_tensor(gap[:, :], mm[1][:, :], mm[0][:, :], ALU.subtract).then_inc(gap_set[l].sem, 1)
                    if l:
                        V.tensor_tensor(l2[:, :, :], logits[:, :, :], over_e(mm[0][:, :]),
                                        ALU.subtract).then_inc(gap_set[l].sem, 1)
                    yield
                    dve.wait_ge(*count_ps[l].at(1))
                    link(V.tensor_copy(tot[:, :, :], tiles_ps.rearrange("p (t e) -> p e t", e=NE)))
                    V.tensor_copy(pos[:, :, :].rearrange("p t e -> p (t e)"), before_ps).then_inc(counts_taken[l].sem, 1)
                    yield
                    dve.wait_ge(*counts_taken[l].at(1))
                    flat = "p e t -> p (e t)"
                    link(V.tensor_tensor_scan(incl[:, :, :].rearrange(flat), carry[:, :, :].rearrange(flat),
                                              tot[:, :, :].rearrange(flat), 0.0, ALU.mult, ALU.add))
                    link(V.tensor_scalar(cnt_i[:, :], incl[:, :, NT - 1], float(P - 1), None, ALU.add))
                    link(V.tensor_scalar(cnt_i[:, :], cnt_i[:, :], 7, None, ALU.arith_shift_right))
                    yield
                    link(V.tensor_scalar(cnt[:, :], cnt_i[:, :], float(P), None, ALU.mult))
                    link(V.tensor_tensor_scan(ends[:, :], ones[:, 0:NE], cnt[:, :], float(T), ALU.mult, ALU.add))
                    link(V.tensor_tensor(offs[:, :], ends[:, :], cnt[:, :], ALU.subtract))
                    link(V.tensor_tensor(incl[:, :, :], incl[:, :, :], tot[:, :, :], ALU.subtract))
                    link(V.tensor_tensor(pos[:, :, :], incl[:, :, :].rearrange("p e t -> p t e"),
                                         pos[:, :, :], ALU.add))
                    yield
                    link(V.tensor_tensor(pos[:, :, :], pos[:, :, :], over_t(offs[:, :]), ALU.add))
                    for k in range(2):
                        link(V.tensor_tensor(posk[:, :, :], pos[:, :, :], oh[k][:, :, :], ALU.mult))
                        link(V.reduce_sum(posf[k][:, :], posk[:, :, :], AXX))
                        last = V.tensor_copy(rows[k][:, :], posf[k][:, :])
                        if k == 0:
                            link(last)
                    last.then_inc(rows_set[l].sem, 1)
                    yield
                    shp = [P, ROUTED, NE]
                    link(V.tensor_tensor(past[:, :, :], slot_row[:, :].unsqueeze(2).to_broadcast(shp),
                                         ends[:, :].unsqueeze(1).to_broadcast(shp), ALU.is_ge))
                    link(V.reduce_sum(slot_ef[:, :], past[:, :, :], AXX))
                    V.tensor_scalar(slot_e[:, NT:SLOTS], slot_ef[:, :], float(NE - 1), float(HID),
                                    ALU.min, ALU.mult).then_inc(rows_set[l].sem, 1)
                    yield
                    dve.wait_ge(*egap_set[l].at(1))
                    if l:
                        dve.wait_ge(*egap_set[l].at(2))
                        link(V.reduce_sum(zsum[:, :], sc[:, :, :], AXX))
                        link(V.tensor_scalar(zsum[:, :], zsum[:, :], 1e-8, 1.0, ALU.mult, ALU.add))
                        link(V.tensor_tensor(den[:, :], zsum[:, :], egap[:, :], ALU.add))
                    else:
                        link(V.tensor_scalar(den[:, :], egap[:, :], 1.0, None, ALU.add))
                    link(V.reciprocal(gates[0][:, :], den[:, :]))
                    link(V.tensor_tensor(gates[1][:, :], gates[0][:, :], egap[:, :], ALU.mult))
                    yield

                route = routing()

                def step(m, k):
                    i = m * 4 + k
                    x, h = i + 2, i + 1
                    if isinstance(m, int):
                        for _ in range({-2: 3, -1: 1, 0: 3}.get(i, 1)):
                            next(route, None)
                    if valid(x):
                        p = k % 2
                        dve.wait_ge(*x_ps[l].at(x + 1))
                        wait_pos(dve, h_ps[l], x - 1)
                        V.tensor_copy(xT[p][:, :], bank(0, P)).then_inc(xT_set[l].sem, 1)
                    if valid(h):
                        p = (k + 1) % 2
                        dve.wait_ge(*th_set[l].at(h + 1))
                        wait_pos(dve, hT_ps[l], h - 1)
                        if l:
                            link(V.scalar_tensor_tensor(out=ga[p], in0=th[p], scalar=1.0, in1=bank(4 + p),
                                                        op0=ALU.add, op1=ALU.mult))
                            V.tensor_tensor(hs[p], ga[p], bank(6 + p), ALU.mult).then_inc(hs_set[l].sem, 1)
                        else:
                            V.scalar_tensor_tensor(out=hs[p], in0=th[p], scalar=1.0, in1=bank(4 + p),
                                                   op0=ALU.add, op1=ALU.mult).then_inc(hs_set[l].sem, 1)

                slot_steps(steps.loop(0, LOOP_TRIPS, 4 * l), step)

                dve.wait_ge(*shared_loaded[l].at(16))
                with steps.loop(0, NB // 2, 2 * COMBINE_STEPS) as m:
                    for g in range(2):
                        b = m * 2 + g
                        for q in range(QT):
                            t = b * QT + q
                            y = g * QT + q
                            link(V.tensor_tensor(pre[:, q, :], tile_of(x_all, t), tile_of(shared, t), ALU.add))
                            dve.wait_ge(*gathered[l][y].at(m * 32 + 32))
                            link(V.scalar_tensor_tensor(out=pre[:, q, :], in0=y_k[0][y], scalar=gates[0][:, ds(t, 1)],
                                                        in1=pre[:, q, :], op0=ALU.mult, op1=ALU.add))
                            last = V.scalar_tensor_tensor(out=pre[:, q, :], in0=y_k[1][y], scalar=gates[1][:, ds(t, 1)],
                                                          in1=pre[:, q, :], op0=ALU.mult, op1=ALU.add)
                            if q + 1 < QT:
                                steps.mark(last)
                        last.then_inc(combined[l].sem, 1)
                        dve.wait_ge(*combined[l].at(b + 1))
                        norm_stats(link)
                        V.tensor_scalar(mv[:, :, 1], mv[:, :, 1], LN_EPS, None, ALU.add).then_inc(var_set[l].sem, 1)
                        dve.wait_ge(*std_set[l].at(b + 1))
                        link(V.reciprocal(rstd[:, :], srt))
                        for q in range(QT):
                            last = V.tensor_scalar(tile_of(x_all, b * QT + q), pre[:, q, :], mv[:, q, 0:1],
                                                   rstd[:, q:q + 1], ALU.subtract, ALU.mult)
                        last.then_inc(layer_out[l].sem, 1)
                        dve.wait_ge(*layer_out[l].at(b + 1))

            moe(0)
            reuse(0, NB - 1)

            dve.wait_ge(*layer_out[0].at(NB))
            dve.wait_ge(a_set, 1)
            link(V.tensor_scalar(a_neg[:, :], a_neg[:, :], -1.0, None, ALU.mult))
            link(V.memset(xi[:, :, 0:KC - 1], 0.0))
            link(V.memset(dA[0][:, 1, 0:1], 0.0))
            V.memset(dA[1][:, 1, 0:1], 0.0).then_inc(a_set, 1)

            def activate(x, h):
                dve.wait_ge(conv_th, x * EH + (h + 1))
                V.scalar_tensor_tensor(out=xa[:, h, :], in0=u1[:, h, :], scalar=1.0, in1=bank(5 - h),
                                       op0=ALU.add, op1=ALU.mult).then_inc(xa_set, 1)

            def one_plus(x):
                dve.wait_ge(soft_exp, x + 1)
                V.tensor_scalar(one_w, u2, 1.0, -1.0, ALU.add, ALU.add).then_inc(fix_mid, 1)

            def split_bc(x):
                dve.wait_ge(hi_set, x + 1)
                link(V.tensor_tensor(res[0:3 * BC, :], ps[0:3 * BC, 3, :], hi[:, :], ALU.subtract))
                link(V.tensor_copy(mid[:, :], res[0:3 * BC, :]))

            def soft_sum(x):
                dve.wait_ge(soft_ln, x + 1)
                link(V.tensor_tensor(u3, u3, u1, ALU.add))

            def hand_over(x):
                if not isinstance(x, int) or x > 0:
                    dve.wait_ge(c_ps, x * NS)
                V.tensor_copy(parts[0:BC, :], hi[0:BC, :])
                V.tensor_copy(parts[BC:2 * BC, :], mid[BC:2 * BC, :])
                V.tensor_tensor(parts[2 * BC:3 * BC, :], res[2 * BC:3 * BC, :], mid[2 * BC:3 * BC, :],
                                ALU.subtract).then_inc(parts_set, 1)
                dve.wait_ge(soft_fix, x + 1)
                if not isinstance(x, int) or x > 0:
                    dve.wait_ge(dA_set, x * NS)
                V.tensor_tensor(delta, u3, u2, ALU.add).then_inc(delta_set, 1)

            def weigh_input(x):
                dve.wait_ge(delta_set, x + 1)
                link(V.tensor_tensor(du, delta, xa, ALU.mult))

            def activate_z(b):
                if not isinstance(b, int) or b > 0:
                    dve.wait_ge(yg_set, b)
                for h in range(EH):
                    dve.wait_ge(z_th, b * EH + (h + 1))
                    V.scalar_tensor_tensor(out=zs[:, h, :], in0=u2[:, h, :], scalar=1.0, in1=bank(3 + h),
                                           op0=ALU.add, op1=ALU.mult).then_inc(zs_set, 1)

            def gate_sum(b):
                dve.wait_ge(y_sum, b * NS + NS)
                dve.wait_ge(zs_set, b * EH + EH)
                V.scalar_tensor_tensor(out=yg, in0=ps[:, 6:8, :], scalar=0.5, in1=zs,
                                       op0=ALU.mult, op1=ALU.mult).then_inc(yg_set, 1)

            def add_residual(b):
                dve.wait_ge(o_ps, b + 1)
                V.scalar_tensor_tensor(out=pre[:].rearrange("p q d -> p (q d)"), in0=x_all[:, ds(b * S, S)], scalar=2.0,
                                       in1=bank(3), op0=ALU.mult, op1=ALU.add).then_inc(o_added, 1)
                dve.wait_ge(o_added, b + 1)
                norm_stats(lambda ins: ins.then_inc(stats_set[1].sem, 1))

            def state(n, j, between):
                dve.wait_ge(b_ps, n + 1)
                if not isinstance(n, int) or n >= 2:
                    dve.wait_ge(st_set, n - 1)
                V.tensor_tensor(dbu[j % 2], du, bank(j % 2).unsqueeze(1).to_broadcast([P, EH, S]), ALU.mult)\
                    .then_inc(dbu_set, 1)
                between()
                dve.wait_ge(dbu_set, n + 1)
                dve.wait_ge(dA_set, n + 1)
                if not isinstance(n, int) or n >= 2:
                    dve.wait_ge(hc_set, n - 1)
                V.tensor_tensor_scan(st[j % 2].rearrange("p h t -> p (h t)"),
                                     dA[j % 2].rearrange("p h t -> p (h t)"),
                                     dbu[j % 2].rearrange("p h t -> p (h t)"), 0.0,
                                     ALU.mult, ALU.add).then_inc(st_set, 1)

            def states(b, after, before):
                for j in range(NS):
                    def between():
                        if after:
                            if j == 1:
                                gate_sum(b - 1)
                            if j == 4:
                                add_residual(b - 1)
                            if j == 6:
                                if not isinstance(b, int) or b > 1:
                                    reuse(1, b - 2)
                                norm_apply(1, b - 1)
                            if j == 10:
                                take_logits(1, b - 1, 3)
                        if j == 2:
                            activate_z(b)
                        if before:
                            if j in (7, 9):
                                activate(b + 1, (j - 7) // 2)
                            if j == 12:
                                one_plus(b + 1)
                            if j == 13:
                                split_bc(b + 1)
                            if j == 14:
                                soft_sum(b + 1)
                            if j == 15:
                                hand_over(b + 1)

                    state(b * NS + j, j, between)
                if before:
                    weigh_input(b + 1)

            for h in range(EH):
                activate(0, h)
            one_plus(0)
            split_bc(0)
            soft_sum(0)
            hand_over(0)
            weigh_input(0)
            states(0, False, True)
            states(1, True, True)
            with steps.loop(2, NB - 1, NORM_STEPS + 4) as b:
                states(b, True, True)
            states(NB - 1, True, False)
            gate_sum(NB - 1)
            add_residual(NB - 1)
            reuse(1, NB - 2)
            norm_apply(1, NB - 1)
            take_logits(1, NB - 1, 3)
            moe(1)

        @block.gpsimd
        def _(pool):
            G = nc.gpsimd
            steps = Steps(pool, pool_step)
            link = steps.link

            link(G.memset(ident[:, :], 0.0))
            G.affine_select(out=ident[:, :], in_=ident[:, :], compare_op=ALU.not_equal, fill=1.0, base=0,
                            pattern=[[-1, P]], channel_multiplier=1).then_inc(consts, 1)
            G.memset(ones[:, :], 1.0).then_inc(consts, 1)
            pool.wait_ge(consts, 2)
            G.affine_select(out=before[:, :], in_=ones[:, :], compare_op=ALU.is_gt, fill=0.0, base=0,
                            pattern=[[1, P]], channel_multiplier=-1).then_inc(consts, 1)
            link(G.memset(half[:, :], -0.5))
            link(G.memset(eps[:, 0, :], LN_EPS))
            G.memset(eps[:, 1, :], RMS_EPS).then_inc(consts, 1)
            G.memset(zero, 0.0).then_inc(zero_set, 1)
            sel3 = sel[:].rearrange("r (j m) -> r j m", m=P)
            link(G.memset(sel[:], 0.0))
            for g in range(2):
                link(G.affine_select(out=sel3, in_=sel3, compare_op=ALU.not_equal, fill=1.0,
                                     base=-g * BC, pattern=[[-1, BC], [0, P]], channel_multiplier=1))
            G.affine_select(out=sel3, in_=sel3, compare_op=ALU.not_equal, fill=1.0,
                            base=-2 * BC, pattern=[[-1, BC], [0, P]], channel_multiplier=1).then_inc(consts, 1)
            G.iota(rank8i[:, :], pattern=[[-1, NE]], base=NE, channel_multiplier=0).then_inc(consts, 1)
            G.iota(slot_rowi[:, :], pattern=[[P, ROUTED]], base=T, channel_multiplier=0).then_inc(consts, 1)
            def diagonals():
                pool.wait_ge(ld_ss, 160)
                link(G.tensor_scalar(conv[:, :, :], conv[:, :, :], 0.5, None, ALU.mult))
                for h in range(EH):
                    for k in range(KC):
                        G.tensor_scalar(diag[:, h * KC + k, :], ident[:, :], conv[:, h, k:k + 1], None, ALU.mult)\
                            .then_inc(diag_set, 1)
                    G.tensor_scalar(d_diag[h][:, :], ident[:, :], d_par[:, h:h + 1], None, ALU.mult)\
                        .then_inc(diag_set, 1)

            def inverse_std(l, b):
                pool.wait_ge(*stats_set[l].at(b + 1))
                link(G.tensor_tensor(mv[:, :, 1], mv[:, :, 1], eps[:, 0, 0:QT], ALU.add))
                G.tensor_tensor(rstd[:, :], mv[:, :, 1], half[:, 0:QT], ALU.pow).then_inc(rstd_set[l].sem, 1)

            def norm_attention():
                def one(b):
                    inverse_std(0, b)
                    pool.wait_ge(*normed_set[0].at(b + 1))
                    G.tensor_copy(x_all[:, ds(b * S, S)], normed[:].rearrange("p q d -> p (q d)")).then_inc(kept[0].sem, 1)

                one(0)
                pool.wait_ge(zero_set, 1)
                pool.dma_start(xs[NT * P:ROWS, :].rearrange("(p c) d -> p (c d)", p=P), zero).then_inc(xs_zeroed, 16)
                with steps.loop(1, NB, 1) as b:
                    one(b)

            def inverse_rms():
                pool.wait_ge(ssq_set, NB)
                G.tensor_tensor(ssq, ssq, eps[:, 1, :], ALU.add).then_inc(rms_mid, 1)
                pool.wait_ge(rms_mid, 1)
                G.tensor_tensor(rms, ssq, half[:, :], ALU.pow).then_inc(rms_set, 1)

            def lost_part(x):
                pool.wait_ge(soft_exp, x + 1)
                pool.wait_ge(fix_mid, x + 1)
                pool.wait_ge(soft_ln, x + 1)
                G.tensor_tensor(u2, u2, one_w, ALU.subtract).then_inc(soft_fix, 1)

            def states(b, after, before):
                for j in range(NS):
                    n = b * NS + j
                    pool.wait_ge(st_set, n + 1)
                    pool.wait_ge(cc_set, n + 1)
                    if not isinstance(n, int) or n >= 4:
                        pool.wait_ge(y_sum, n - 3)
                    G.tensor_tensor(hc[j % 4], st[j % 2],
                                    cc[j % 2].unsqueeze(1).to_broadcast([P, EH, S]), ALU.mult).then_inc(hc_set, 1)
                    if j == 4 and after:
                        inverse_std(1, b - 1)
                    if j == 13 and before:
                        lost_part(b + 1)

            def state_space():
                inverse_rms()
                lost_part(0)
                states(0, False, True)
                with steps.loop(1, NB - 1, 1) as b:
                    states(b, True, True)
                states(NB - 1, True, False)
                inverse_std(1, NB - 1)

            def moe(l):
                pool.wait_ge(*rows_set[l].at(1))
                pool.wait_ge(*kept[l].at(NB))
                pool.wait_ge(xs_zeroed, 16)
                for t in range(NT):
                    for k in range(2):
                        G.indirect_dma_start(out=xs, out_offset=bass.IndirectOffsetOnAxis(ap=rows[k][:, t:t + 1], axis=0),
                                             in_=x_all[:, t * D:(t + 1) * D], in_offset=None).then_inc(scattered[l].sem, 16)
                if l == 0:
                    diagonals()
                for k in range(4):
                    pool.wait_ge(*ys_stored[l][k].at(16 * fills(k)))
                for t in range(NT):
                    if t >= 8:
                        pool.wait_ge(*combined[l].at(t // 4 - 1))
                    for k in range(2):
                        G.indirect_dma_start(out=y_k[k][t % 8], out_offset=None, in_=ys,
                                             in_offset=bass.IndirectOffsetOnAxis(ap=rows[k][:, t:t + 1], axis=0))\
                            .then_inc(gathered[l][t % 8].sem, 16)

            norm_attention()
            moe(0)
            state_space()
            moe(1)


def kernel(**inputs):
    import concourse.bacc as bacc
    from concourse.bass_utils import run_bass_kernel_spmd

    a = {k: np.asarray(v) for k, v in inputs.items()}
    put = {"x": a["L0_attn_x"].reshape(T, D)}
    qkv = a["L0_attn_W_qkv"].reshape(D, 3, D)
    put["wq"], put["wk"], put["wv"] = qkv[:, 0], qkv[:, 1], qkv[:, 2]
    put["woT"] = a["L0_attn_W_out"].T
    up = lambda w, shared: np.concatenate([w, shared[None]]).transpose(1, 0, 2).reshape(D, -1)
    down = lambda w, shared: (np.concatenate([w, shared[None]]).reshape(NE + 1, HB, P, D)
                              .transpose(2, 0, 1, 3).reshape(P, -1))
    put["gate0"] = a["L0_ffn_gate_w"].T
    put["w1"] = up(a["L0_ffn_experts_w1"].transpose(0, 2, 1), a["L0_ffn_shared_w1"].T)
    put["w2"] = down(a["L0_ffn_experts_w2"].transpose(0, 2, 1), a["L0_ffn_shared_w2"].T)
    put["gate1"] = a["L1_ffn_w_router"]
    put["wg"] = up(a["L1_ffn_w_gate"], a["L1_ffn_ws_gate"])
    put["wu"] = up(a["L1_ffn_w_up"], a["L1_ffn_ws_up"])
    put["wd"] = down(a["L1_ffn_w_down"], a["L1_ffn_ws_down"])
    halves = lambda w: w.reshape(EH, P, -1).transpose(1, 0, 2)
    put["norm_w"] = a["L1_attn_norm_w"].reshape(P, 1)
    put["w_in"] = a["L1_attn_W_in"]
    put["conv"] = halves(a["L1_attn_conv_w"])
    w_x = halves(a["L1_attn_W_x"])
    put["w_dtl"] = w_x[:, :, :DTR]
    put["w_bc3"] = np.concatenate([w_x[:, :, DTR:]] * 3, axis=2)
    put["w_dt"] = a["L1_attn_W_dt"]
    put["b_dt"] = halves(a["L1_attn_b_dt"]).reshape(P, EH)
    put["a_log"] = halves(a["L1_attn_A_log"]).reshape(P, EH * NS)
    put["d_par"] = halves(a["L1_attn_D_param"]).reshape(P, EH)
    put["w_out"] = halves(a["L1_attn_W_out"])
    put = {k: np.ascontiguousarray(v) for k, v in put.items()}

    nc = bacc.Bacc("TRN2", target_bir_lowering=False, num_devices=1)
    args = {k: nc.dram_tensor(f"in_{k}", v.shape, mybir.dt.from_np(v.dtype), kind="ExternalInput").ap()
            for k, v in put.items()}
    out = nc.dram_tensor("out", (T, D), F32, kind="ExternalOutput").ap()
    build(nc, args, out)
    r = run_bass_kernel_spmd(nc, [{f"in_{k}": v for k, v in put.items()}], core_ids=[0])
    return r.results[0]["out"].reshape(NB, S, D)
```

```python
import numpy as np
import concourse.bass as bass
from concourse import mybir
from contextlib import ExitStack, contextmanager

F32 = mybir.dt.float32
BF16 = mybir.dt.bfloat16
I32 = mybir.dt.int32
U32 = mybir.dt.uint32
ALU = mybir.AluOpType
ACT = mybir.ActivationFunctionType
AXX = mybir.AxisListType.X
ds = bass.ds

P = 128
D = 128
NB = 4
S = 512
QT = S // P
T = NB * S
NT = T // P
NE = 8
HID = 512
HB = HID // P
ROUTED = (2 * T + NE * (P - 1)) // P
SLOTS = NT + ROUTED
ROWS = ROUTED * P
CLEAR = 3
XW = D + 2
BACK = 4 * T
EI = 256
EH = EI // P
NS = 16
KC = 4
DTR = 64
BC = 2 * NS
LN_EPS = 1e-5
RMS_EPS = 1e-6
SCALE = float(D) ** -0.5
NEVER = -3.0e38


class Steps:

    def __init__(self, eng, sem):
        self.eng, self.sem, self.n, self.marks = eng, sem, 0, 0

    def mark(self, ins):
        ins.then_inc(self.sem, 1)
        self.n = self.n + 1
        self.marks += 1

    def link(self, ins):
        self.mark(ins)
        self.eng.wait_ge(self.sem, self.n)

    @contextmanager
    def loop(self, lo, hi, per):
        base, before = self.n, self.marks
        with self.eng.Fori(0, hi - lo) as i:
            self.n = base + i * per
            yield i + lo
            assert self.marks - before == per, (self.marks - before, per)
        self.n = base + (hi - lo) * per


class Share:

    def __init__(self, sem, base):
        self.sem, self.base = sem, base

    def at(self, n):
        return self.sem, n + self.base


def build(nc, a, out):
    ctx = ExitStack()
    with ctx:
        def sb(name, shape, dt=F32):
            return ctx.enter_context(nc.sbuf_tensor(name, shape, dt))

        def sem(name):
            return ctx.enter_context(nc.semaphore(name))

        xs = [nc.dram_tensor(f"xs{l}", (ROWS, XW), F32).ap() for l in range(2)]
        xn_rows = nc.dram_tensor("xn_rows", (T, D), F32).ap()
        y_shared = nc.dram_tensor("y_shared", (T, D), F32).ap()
        y_choice = nc.dram_tensor("y_choice", (2 * T, D), F32).ap()

        x_all = sb("x_all", [P, NT * XW])
        ident = sb("ident", [P, P])
        ones = sb("ones", [P, P])
        before = sb("before", [P, P])
        wq = sb("wq", [P, D]); wk = sb("wk", [P, D]); wv = sb("wv", [P, D]); woT = sb("woT", [P, D])
        wqk = sb("wqk", [P, D]); wvo = sb("wvo", [P, D])
        gate = [sb(f"gate{l}", [P, NE]) for l in range(2)]
        w1 = sb("w1", [P, (NE + 1) * HID])
        w2 = sb("w2", [P, (NE + 1) * HID])
        wg = sb("wg", [P, (NE + 1) * HID])
        wu = sb("wu", [P, (NE + 1) * HID])
        wd = sb("wd", [P, (NE + 1) * HID])
        norm_w = sb("norm_w", [P, 1])
        w_in = sb("w_in", [P, 2 * EI])
        conv = sb("conv", [P, EH, KC])
        w_dtl = sb("w_dtl", [P, EH, DTR])
        w_bc3 = sb("w_bc3", [P, EH, 3 * BC])
        w_dt = sb("w_dt", [DTR, EI])
        b_dt = sb("b_dt", [P, EH])
        a_log = sb("a_log", [P, EH * NS])
        a_neg = sb("a_neg", [P, EH * NS])
        d_par = sb("d_par", [P, EH])
        w_out = sb("w_out", [P, EH, D])
        diag = sb("diag", [P, EH * KC, P])
        sel = sb("sel", [3 * BC, BC * P], BF16)
        normed = sb("normed", [P, QT, D])
        normT = sb("normT", [P, S])
        pre = sb("pre", [P, QT, D])
        stats = sb("stats", [P, QT, 6])
        stats_n = sb("stats_n", [P, QT])
        mv = sb("mv", [P, QT, 2])
        rstd = sb("rstd", [P, QT])
        half = sb("half", [P, NT])
        eps = sb("eps", [P, 2, NT])
        logits = sb("logits", [P, NT, NE])
        rank8 = sb("rank8", [P, NE]); rank8i = sb("rank8i", [P, NE], I32)
        slot_row = sb("slot_row", [P, ROUTED]); slot_rowi = sb("slot_rowi", [P, ROUTED], I32)
        eq = sb("eq", [P, NT, NE]); sc = sb("sc", [P, NT, NE]); l2 = sb("l2", [P, NT, NE])
        oh = [sb(f"oh{k}", [P, NT, NE]) for k in range(2)]
        mm = [sb(f"mm{k}", [P, NT]) for k in range(2)]
        ms = [sb(f"ms{k}", [P, NT]) for k in range(2)]
        mask = sb("mask", [P, NT, NE])
        gap = sb("gap", [P, NT]); egap = sb("egap", [P, NT]); den = sb("den", [P, NT]); zsum = sb("zsum", [P, NT])
        gates = [sb(f"gates{k}", [P, NT]) for k in range(2)]
        carry = sb("carry", [P, NE, NT])
        tot = sb("tot", [P, NE, NT]); incl = sb("incl", [P, NE, NT])
        cnt_i = sb("cnt_i", [P, NE], I32); cnt = sb("cnt", [P, NE]); ends = sb("ends", [P, NE]); offs = sb("offs", [P, NE])
        pos = sb("pos", [P, NT, NE]); posk = sb("posk", [P, NT, NE]); posf = [sb(f"posf{k}", [P, NT]) for k in range(2)]
        rows = [sb(f"rows{k}", [P, NT], U32) for k in range(2)]
        slot_ef = sb("slot_ef", [P, ROUTED])
        slot_m = sb("slot_m", [P, SLOTS])
        token = sb("token", [P, NT]); tokeni = sb("tokeni", [P, NT], I32)
        dest = sb("dest", [P, SLOTS], U32); choice = sb("choice", [P, SLOTS])
        slot_e = sb("slot_e", [P, SLOTS], I32)
        xin = [sb(f"xin{k}", [P, XW]) for k in range(4)]
        xT = [sb(f"xT{k}", [P, P]) for k in range(2)]
        wide = sb("wide", [P, 8 * HID])
        th, ga, hs, hT = ([wide[:, (2 * j + k) * HID:(2 * j + k + 1) * HID] for k in range(2)] for j in range(4))
        yout = [sb(f"yout{k}", [P, D]) for k in range(4)]
        work = sb("work", [P, 12 * 1024])

        def area(at, *shape):
            n = int(np.prod(shape))
            v = work[:, at:at + n]
            if len(shape) == 2:
                v = v.rearrange("p (a b) -> p a b", a=shape[0])
            return v

        past = area(11792, ROUTED, NE)
        xb = area(0, QT, D)
        xbT = area(512, S)
        qmT = area(1024, S)
        v_all = area(1536, T)
        probs = area(3584, QT, S)
        pT = [area(5632 + 512 * k, S) for k in range(2)]
        mx = area(6656, QT); nmx = area(6660, QT); rs = area(6664, QT); rinv = area(6668, QT)
        zero = area(6720, ROUTED * XW)
        shared = wide[:, 0:T]
        y_k = [w1[:, k * T:(k + 1) * T] for k in range(2)]
        all_stats, all_mv, srt, inv = (wide[:, T + at:T + at + NT * n] for at, n in ((0, 6), (96, 2), (128, 1), (144, 1)))
        all_stats = all_stats.rearrange("p (t s) -> p t s", s=6); all_mv = all_mv.rearrange("p (t s) -> p t s", s=2)
        xn = area(0, QT, D); xnT = area(512, S)
        xi = area(1024, EH, S + KC - 1)
        xa = area(2304, EH, S); zs = area(3328, EH, S)
        u1 = area(4352, EH, S); u2 = area(5376, EH, S); u3 = area(6400, EH, S)
        delta = area(7424, EH, S); du = area(8448, EH, S)
        ssq = area(12032, NT); rms = area(12032 + NT, NT)
        res = area(9472, S)
        dA = [area(9984 + 1024 * k, EH, S) for k in range(2)]
        st, hc = ([wide[:, (2 * j + k) * EH * S:(2 * j + k + 1) * EH * S].rearrange("p (h t) -> p h t", h=EH)
                   for k in range(2)] for j in range(2))

        def halves_in(w, at):
            return w[:, at:at + EH * S].rearrange("p (h t) -> p h t", h=EH)

        dbu = [halves_in(w1, k * EH * S) for k in range(2)]
        yg = halves_in(w1, 2 * EH * S); one_w = halves_in(w1, 3 * EH * S)
        cc = [w2[:, k * S:(k + 1) * S] for k in range(2)]
        dts = w2[0:DTR, 2 * S:3 * S]
        hc += [halves_in(w2, (4 + k * EH) * S) for k in range(2)]
        d_diag = [wq, wk]
        hi = sb("hi", [3 * BC, S], BF16); mid = sb("mid", [3 * BC, S], BF16)
        parts = sb("parts", [3 * BC, S], BF16)
        ps = ctx.enter_context(nc.psum_tensor("ps", [P, 8, 512], F32))

        def bank(k, n=512):
            return ps[:, k, 0:n]

        def tile_of(ap, t):
            return ap[:, ds(t * D, D)]

        def x_tile(t):
            return x_all[:, ds(t * XW, D)]

        def x_seq(b):
            return x_all[:, ds(b * QT * XW, QT * XW)].rearrange("p (q w) -> p q w", w=XW)[:, :, 0:D]

        def tiles(ap):
            return ap.rearrange("p (q d) -> p q d", d=D)

        def layers(name, per_layer):
            s = sem(name)
            return [Share(s, l * per_layer) for l in range(2)]

        def fills(k):
            return (SLOTS - k + 3) // 4

        ld_x = sem("ld_x"); ld_gate = sem("ld_gate"); ld_att = sem("ld_att"); ld_f0 = sem("ld_f0"); ld_f1 = sem("ld_f1"); ld_ss = sem("ld_ss")
        zero_set = sem("zero_set"); xs_zeroed = sem("xs_zeroed")
        consts = sem("consts"); diag_set = sem("diag_set")
        w_ps = sem("w_ps"); w_set = sem("w_set")
        pool_step = sem("pool_step"); dve_step = sem("dve_step"); act_step = sem("act_step")
        xb_loaded = sem("xb_loaded"); xbT_ps = sem("xbT_ps"); xbT_set = sem("xbT_set")
        qm_ps = sem("qm_ps"); qmT_set = sem("qmT_set"); v_ps = sem("v_ps"); v_set = sem("v_set")
        scores_ps = sem("scores_ps"); nmax_set = sem("nmax_set"); probs_set = sem("probs_set")
        pT_ps = sem("pT_ps"); pT_set = sem("pT_set"); ctx_ps = sem("ctx_ps"); ctx_added = sem("ctx_added")
        stats_set = layers("stats_set", NB); rstd_set = layers("rstd_set", NB)
        normed_set = layers("normed_set", NB); kept = layers("kept", NB)
        xs_stored = layers("xs_stored", 16 * NB)
        nT_ps = layers("nT_ps", NB); nT_set = layers("nT_set", NB)
        logit_ps = layers("logit_ps", NB); logits_set = layers("logits_set", NB)
        mask_set = layers("mask_set", 1); count_ps = layers("count_ps", 1)
        counts_taken = layers("counts_taken", 1)
        gap_set = layers("gap_set", 1); egap_set = layers("egap_set", 1)
        rows_set = layers("rows_set", 2); scattered = layers("scattered", 16 * 2 * NT)
        xin_loaded_ = [layers(f"xin_loaded{k}", 16 * fills(k)) for k in range(4)]
        xin_loaded = [[r[l] for r in xin_loaded_] for l in range(2)]
        x_ps = layers("x_ps", SLOTS); xT_set = layers("xT_set", SLOTS)
        h_ps = layers("h_ps", SLOTS); th_set = layers("th_set", SLOTS)
        hs_set = layers("hs_set", SLOTS); hT_ps = layers("hT_ps", SLOTS)
        hT_set = layers("hT_set", SLOTS); y_ps = layers("y_ps", SLOTS)
        yout_set = layers("yout_set", SLOTS)
        ys_stored_ = [layers(f"ys_stored{k}", 16 * NT // 4) for k in range(4)]
        ys_sent_ = [layers(f"ys_sent{k}", 16 * (fills(k) - NT // 4)) for k in range(4)]
        ys_sent = [[r[l] for r in ys_sent_] for l in range(2)]
        ys_stored = [[r[l] for r in ys_stored_] for l in range(2)]
        gathered_ = [layers(f"gathered{k}", NB // 2 * 48) for k in range(2)]
        gathered = [[r[l] for r in gathered_] for l in range(2)]
        rms_mid = sem("rms_mid"); fix_mid = sem("fix_mid")
        var_set = layers("var_set", 2)
        std_set = layers("std_set", 2); layer_out = layers("layer_out", NB)
        out_stored = sem("out_stored")
        a_set = sem("a_set"); ssq_set = sem("ssq_set"); rms_set = sem("rms_set"); xn_set = sem("xn_set")
        xn_ps = sem("xn_ps"); xnT_set = sem("xnT_set"); xi_ps = sem("xi_ps"); z_ps = sem("z_ps"); xi_set = sem("xi_set")
        conv_ps = sem("conv_ps"); conv_th = sem("conv_th"); z_th = sem("z_th"); xa_set = sem("xa_set")
        zs_set = sem("zs_set"); dtl_ps = sem("dtl_ps"); bc_ps = sem("bc_ps"); dts_set = sem("dts_set"); hi_set = sem("hi_set")
        parts_set = sem("parts_set"); dl_ps = sem("dl_ps"); soft_abs = sem("soft_abs"); soft_exp = sem("soft_exp")
        soft_ln = sem("soft_ln"); soft_fix = sem("soft_fix"); delta_set = sem("delta_set")
        b_ps = sem("b_ps"); c_ps = sem("c_ps"); dA_set = sem("dA_set"); cc_set = sem("cc_set")
        dbu_set = sem("dbu_set"); st_set = sem("st_set"); hc_set = sem("hc_set"); y_sum = sem("y_sum")
        yg_set = sem("yg_set"); o_ps = sem("o_ps"); o_added = sem("o_added")

        block = ctx.enter_context(nc.Block())

        LOOP_LO = NT + 4 + 1
        LOOP_TRIPS = (SLOTS - 2 - LOOP_LO) // 4
        COUNT_STEP, EGAP_STEP = -1, 1

        def slot_steps(loop, step):
            for i in range(-2, LOOP_LO):
                step(0, i)
            with loop as m:
                for k in range(4):
                    step(m, LOOP_LO + k)
            for i in range(LOOP_LO + 4 * LOOP_TRIPS, SLOTS + 1):
                step(0, i)

        before_ps, tiles_ps = (ps[:, 0, P + k * NT * NE:P + (k + 1) * NT * NE] for k in range(2))

        GROUPS = (((0, 1), (1, NB)), ((0, NB // 2), (NB // 2, NB)))

        def valid(i, n=SLOTS):
            return not isinstance(i, int) or 0 <= i < n

        ROUTE_STEPS = 9

        def wait_pos(eng, s, value):
            if isinstance(value, int) and value <= 0:
                return
            eng.wait_ge(*s.at(value))

        @block.sync
        def _(sp):
            def load_seq(b):
                if not isinstance(b, int):
                    sp.wait_ge(xbT_ps, b)
                sp.dma_start(xb, a["x"][ds(b * S, S), :].rearrange("(q p) d -> p q d", p=P)).then_inc(xb_loaded, 16)

            def load_weights(done, *pairs):
                for dst, name in pairs:
                    sp.dma_start(dst[:], a[name]).then_inc(done, 16)

            load_seq(0)
            load_weights(ld_att, (wq, "wq"), (wk, "wk"), (wv, "wv"), (woT, "woT"))
            load_weights(ld_gate, (gate[0], "gate0"), (gate[1], "gate1"))
            sp.dma_start(x_all[:].rearrange("p (t w) -> p t w", w=XW)[:, :, 0:D],
                         a["x"].rearrange("(t p) d -> p t d", p=P)).then_inc(ld_x, 16)
            with sp.Fori(1, NB) as b:
                load_seq(b)
            load_weights(ld_ss, (norm_w, "norm_w"), (w_in, "w_in"), (conv, "conv"), (w_dtl, "w_dtl"), (w_bc3, "w_bc3"),
                         (w_dt, "w_dt"), (b_dt, "b_dt"), (a_log, "a_log"), (d_par, "d_par"), (w_out, "w_out"))

            def moe(l):
                def keep_rows(b):
                    sp.wait_ge(*normed_set[l].at(b + 1))
                    sp.dma_start(xn_rows[ds(b * S, S), :].rearrange("(q p) d -> p q d", p=P),
                                 normed[:, :, :]).then_inc(xs_stored[l].sem, 16)

                def load(i, k, rows, w):
                    if not isinstance(i, int) or i >= 4:
                        sp.wait_ge(*xT_set[l].at(i - 3))
                    sp.dma_start(xin[k % 4][:, 0:w], rows).then_inc(xin_loaded[l][k % 4].sem, 16)

                def load_own(i, k):
                    load(i, k, xn_rows[ds(i * P, P), :], D)

                def load_routed(i, k):
                    load(i, k, xs[l][ds((i - NT) * P, P), :], XW)

                with sp.Fori(0, NB - 1) as b:
                    keep_rows(b)
                sp.wait_ge(*xs_stored[l].at(16 * (NB - 1)))
                for i in range(4):
                    load_own(i, i)
                keep_rows(NB - 1)
                sp.wait_ge(*xs_stored[l].at(16 * NB))
                with sp.Fori(0, (NT - 4) // 4) as m:
                    for k in range(4):
                        load_own(m * 4 + (k + 4), k)
                sp.wait_ge(*scattered[l].at(16 * 2 * NT))
                trips = ROUTED // 4
                with sp.Fori(0, trips) as m:
                    for k in range(4):
                        load_routed(m * 4 + (NT + k), k)
                for i in range(NT + 4 * trips, SLOTS):
                    load_routed(i, i)
                for k in range(4):
                    sp.wait_ge(*ys_stored[l][k].at(16 * NT // 4))
                    sp.wait_ge(*ys_sent[l][k].at(16 * (fills(k) - NT // 4)))
                for b in range(NB):
                    if b >= 2:
                        sp.wait_ge(*gathered[l][b % 2].at(b // 2 * 48))
                    for dst, src in ((shared, y_shared[b * S:(b + 1) * S, :]), (y_k[0], y_choice[b * S:(b + 1) * S, :]),
                                     (y_k[1], y_choice[T + b * S:T + (b + 1) * S, :])):
                        sp.dma_start(tiles(dst[:, b * S:(b + 1) * S]), src.rearrange("(q p) d -> p q d", p=P))\
                            .then_inc(gathered[l][b % 2].sem, 16)

            moe(0)
            load_weights(ld_f1, (wg, "wg"), (wu, "wu"), (wd, "wd"))
            moe(1)
            with sp.Fori(0, NB) as b:
                sp.wait_ge(*layer_out[1].at(b + 1))
                sp.dma_start(out[ds(b * S, S), :].rearrange("(q p) d -> p q d", p=P),
                             x_seq(b)).then_inc(out_stored, 16)
            sp.wait_ge(out_stored, 16 * NB)

        @block.tensor
        def _(pe):
            mm_ = nc.tensor.matmul
            tr = nc.tensor.transpose
            pe.wait_ge(ld_att, 64)
            mm_(bank(5, P), wq[:, :], wk[:, :], start=True, stop=True).then_inc(w_ps, 1)
            mm_(bank(6, P), wv[:, :], woT[:, :], start=True, stop=True).then_inc(w_ps, 1)
            pe.wait_ge(consts, 4)
            pe.wait_ge(w_set, 2)

            def project(b):
                pe.wait_ge(xb_loaded, b * 16 + 16)
                for q in range(QT):
                    last = tr(ps[:, 6, q * P:(q + 1) * P], xb[:, q, :], ident[:, :])
                last.then_inc(xbT_ps, 1)
                pe.wait_ge(xbT_set, b + 1)
                mm_(bank(5), wqk[:, :], xbT, start=True, stop=True).then_inc(qm_ps, 1)
                for q in range(QT):
                    last = mm_(ps[:, 6, q * P:(q + 1) * P], xbT[:, q * P:(q + 1) * P], wvo[:, :], start=True, stop=True)
                last.then_inc(v_ps, 1)

            def router(l, b):
                pe.wait_ge(*normed_set[l].at(b + 1))
                for q in range(QT):
                    last = tr(ps[:, 5, q * P:(q + 1) * P], normed[:, q, :], ident[:, :])
                last.then_inc(nT_ps[l].sem, 1)
                pe.wait_ge(*nT_set[l].at(b + 1))
                for q in range(QT):
                    last = mm_(ps[:, 6, q * NE:(q + 1) * NE], normT[:, q * P:(q + 1) * P], gate[l][:, :],
                               start=True, stop=True)
                last.then_inc(logit_ps[l].sem, 1)
                pe.wait_ge(*logits_set[l].at(b + 1))

            def attend(b, first, final):
                pe.wait_ge(qmT_set, b + 1)
                for q in range(QT):
                    mm_(bank(q), qmT[:, q * P:(q + 1) * P], xbT, start=True, stop=True).then_inc(scores_ps, 1)
                pe.wait_ge(v_set, b + 1)
                if not final:
                    project(b + 1)

                def turn(q):
                    pe.wait_ge(probs_set, b * QT + (q + 1))
                    if q > 0 or not first:
                        pe.wait_ge(pT_set, b * QT + q)
                    for k in range(QT):
                        last = tr(ps[:, 7, k * P:(k + 1) * P], probs[:, q, k * P:(k + 1) * P], ident[:, :])
                    last.then_inc(pT_ps, 1)

                def context(q):
                    pe.wait_ge(pT_set, b * QT + (q + 1))
                    if q == 0 and not first:
                        pe.wait_ge(ctx_added, b)
                    for k in range(QT):
                        last = mm_(ps[:, 4, q * P:(q + 1) * P], pT[q % 2][:, k * P:(k + 1) * P],
                                   tile_of(v_all, b * QT + k), start=(k == 0), stop=(k == QT - 1))
                    last.then_inc(ctx_ps, 1)

                turn(0)
                for q in range(QT):
                    if q + 1 < QT:
                        turn(q + 1)
                    context(q)
                if not first:
                    router(0, b - 1)

            project(0)
            attend(0, True, False)
            pe.wait_ge(ld_gate, 32)
            with pe.Fori(1, NB - 1) as b:
                attend(b, False, False)
            attend(NB - 1, False, True)
            router(0, NB - 1)

            def moe(l):
                wa, wb, wc = ((w1, None, w2), (wg, wu, wd))[l]
                hbank = (4, 6)
                pe.wait_ge(*((ld_f0, 32), (ld_f1, 48))[l])

                def counts():
                    pe.wait_ge(*mask_set[l].at(1))
                    pe.wait_ge(*xT_set[l].at(COUNT_STEP + 2))
                    flat = mask[:, :, :].rearrange("p t e -> p (t e)")
                    mm_(before_ps, before[:, :], flat, start=True, stop=True)
                    mm_(tiles_ps, ones[:, :], flat, start=True, stop=True).then_inc(count_ps[l].sem, 1)
                    pe.wait_ge(*counts_taken[l].at(1))

                expert = {}

                def expert_of(i, k):
                    if isinstance(i, int):
                        expert.clear()
                        if i < NT:
                            return NE * HID
                        return pe.value_load(slot_e[0:1, i:i + 1], min_val=0, max_val=NE * HID)
                    if k not in expert:
                        expert[k] = pe.value_load(slot_e[0:1, ds(i, 1)], min_val=0, max_val=NE * HID)
                    return expert[k]

                def step(m, k):
                    i = m * 4 + k
                    x, h, t, y = i + 2, i + 1, i, i - 1
                    if isinstance(m, int) and i == COUNT_STEP:
                        counts()
                    if isinstance(m, int) and i == ROUTE_STEPS:
                        pe.wait_ge(*rows_set[l].at(2))
                    if valid(x):
                        q = (k + 2) % 4
                        pe.wait_ge(*xin_loaded[l][q].at((m + (k + 2) // 4 + 1) * 16))
                        wait_pos(pe, xT_set[l], x)
                        tr(bank(0, P), xin[q][:, 0:D], ident[:, :]).then_inc(x_ps[l].sem, 1)
                    if valid(h):
                        p = (k + 1) % 2
                        e = expert_of(h, k + 1)
                        pe.wait_ge(*xT_set[l].at(h + 1))
                        wait_pos(pe, hs_set[l], h - 1)
                        last = mm_(bank(hbank[0] + p), xT[p][:, :], wa[:, ds(e, HID)], start=True, stop=True)
                        if wb is not None:
                            last = mm_(bank(hbank[1] + p), xT[p][:, :], wb[:, ds(e, HID)], start=True, stop=True)
                        last.then_inc(h_ps[l].sem, 1)
                        if not isinstance(h, int) and k < LOOP_LO + 3:
                            expert_of(h + 1, k + 2)
                    if valid(t):
                        p = k % 2
                        pe.wait_ge(*hs_set[l].at(t + 1))
                        wait_pos(pe, hT_set[l], t - 1)
                        for j in range(HB):
                            last = tr(ps[:, 2 + p, j * P:(j + 1) * P], hs[p][:, j * P:(j + 1) * P], ident[:, :])
                        last.then_inc(hT_ps[l].sem, 1)
                    if valid(y):
                        p = (k - 1) % 2
                        e = expert_of(y, k - 1)
                        pe.wait_ge(*hT_set[l].at(y + 1))
                        wait_pos(pe, yout_set[l], y)
                        for j in range(HB):
                            last = mm_(bank(1, D), hT[p][:, j * P:(j + 1) * P], wc[:, ds(e + j * D, D)],
                                       start=(j == 0), stop=(j == HB - 1))
                        last.then_inc(y_ps[l].sem, 1)

                slot_steps(pe.Fori(0, LOOP_TRIPS), step)

            moe(0)

            pe.wait_ge(ld_ss, 160)
            pe.wait_ge(diag_set, EH * KC + EH)
            pe.wait_ge(consts, 5)
            pe.wait_ge(a_set, 2)

            def turn_xn(x):
                pe.wait_ge(xn_set, x + 1)
                for q in range(QT):
                    last = tr(ps[:, 5, q * P:(q + 1) * P], xn[:, q, :], ident[:, :])
                last.then_inc(xn_ps, 1)

            def project_x(x):
                pe.wait_ge(xnT_set, x + 1)
                for h in range(EH):
                    mm_(bank(5 - h), w_in[:, h * P:(h + 1) * P], xnT, start=True, stop=True).then_inc(xi_ps, 1)

            def convolve(x, h, taps):
                if taps[0] == 0:
                    pe.wait_ge(xi_set, x * EH + (h + 1))
                for k in taps:
                    last = mm_(bank(5 - h), diag[:, h * KC + k, :], xi[:, h, k:k + S], start=(k == 0), stop=(k == KC - 1))
                if taps[-1] == KC - 1:
                    last.then_inc(conv_ps, 1)

            def project_dt_low(x):
                pe.wait_ge(xa_set, x * EH + EH)
                for h in range(EH):
                    last = mm_(ps[0:DTR, 5, :], w_dtl[:, h, :], xa[:, h, :], start=(h == 0), stop=(h == EH - 1))
                last.then_inc(dtl_ps, 1)

            def project_dt(x):
                pe.wait_ge(dts_set, x + 1)
                for h in range(EH):
                    last = mm_(bank(4 + h), w_dt[:, h * P:(h + 1) * P], dts, start=True, stop=True)
                last.then_inc(dl_ps, 1)

            def project_bc(x):
                for h in range(EH):
                    last = mm_(ps[0:3 * BC, 3, :], w_bc3[:, h, :], xa[:, h, :], start=(h == 0), stop=(h == EH - 1))
                last.then_inc(bc_ps, 1)

            def project_z(b):
                pe.wait_ge(soft_abs, b + 1)
                for h in range(EH):
                    mm_(bank(3 + h), w_in[:, EI + h * P:EI + (h + 1) * P], xnT, start=True, stop=True).then_inc(z_ps, 1)

            def project_out(b):
                for q in range(QT):
                    for h in range(EH):
                        last = mm_(ps[:, 3, q * P:(q + 1) * P], yg[:, h, q * P:(q + 1) * P], w_out[:, h, :],
                                   start=(h == 0), stop=(h == EH - 1))
                last.then_inc(o_ps, 1)

            def turn_normed(b):
                pe.wait_ge(*normed_set[1].at(b + 1))
                for q in range(QT):
                    last = tr(ps[:, 3, q * P:(q + 1) * P], normed[:, q, :], ident[:, :])
                last.then_inc(nT_ps[1].sem, 1)

            def route_out(b):
                pe.wait_ge(*nT_set[1].at(b + 1))
                for q in range(QT):
                    last = mm_(ps[:, 3, q * NE:(q + 1) * NE], normT[:, q * P:(q + 1) * P], gate[1][:, :],
                               start=True, stop=True)
                last.then_inc(logit_ps[1].sem, 1)

            def spread_b(n, j):
                if not isinstance(n, int) or n >= 2:
                    pe.wait_ge(dbu_set, n - 1)
                mm_(bank(j % 2), sel[:, j * P:(j + 1) * P], parts[:, :], start=True, stop=True).then_inc(b_ps, 1)

            def spread_c(n, j):
                if not isinstance(n, int) or n >= 1:
                    pe.wait_ge(cc_set, n)
                mm_(bank(2), sel[:, (j + NS) * P:(j + NS + 1) * P], parts[:, :], start=True, stop=True).then_inc(c_ps, 1)

            def add_up(n, j):
                pe.wait_ge(hc_set, n + 1)
                for h in range(EH):
                    last = mm_(bank(6 + h), ident[:, :], hc[j % 4][:, h, :], start=False, stop=(j == NS - 1))
                last.then_inc(y_sum, 1)

            def states(b, after, before):
                pe.wait_ge(parts_set, b + 1)
                spread_b(b * NS, 0)
                if after:
                    add_up(b * NS - 2, NS - 2)
                for j in range(NS):
                    if j < NS - 1:
                        spread_b(b * NS + (j + 1), j + 1)
                    spread_c(b * NS + j, j)
                    if j == 0:
                        project_z(b)
                        if after:
                            add_up(b * NS - 1, NS - 1)
                    if j == 1 and before:
                        turn_xn(b + 1)
                    if j == 2:
                        if after:
                            pe.wait_ge(yg_set, b)
                        for h in range(EH):
                            mm_(bank(6 + h), d_diag[h][:, :], xa[:, h, :], start=True, stop=False)
                    if j == 3:
                        pe.wait_ge(zs_set, b * EH + EH)
                        if before:
                            project_x(b + 1)
                        if after:
                            project_out(b - 1)
                    if after:
                        if j == 8:
                            turn_normed(b - 1)
                        if j == 9:
                            route_out(b - 1)
                    if before:
                        if j in (4, 5):
                            convolve(b + 1, 0, ((0, 1), (2, 3))[j - 4])
                        if j in (6, 7):
                            convolve(b + 1, 1, ((0, 1), (2, 3))[j - 6])
                        if j == 9:
                            project_dt_low(b + 1)
                        if j == 10:
                            project_dt(b + 1)
                        if j == 11:
                            if after:
                                pe.wait_ge(*logits_set[1].at(b))
                            project_bc(b + 1)
                    if j >= 2:
                        add_up(b * NS + (j - 2), j - 2)

            turn_xn(0)
            project_x(0)
            for h in range(EH):
                convolve(0, h, range(KC))
            project_dt_low(0)
            project_dt(0)
            project_bc(0)
            states(0, False, True)
            with pe.Fori(1, NB - 1) as b:
                states(b, True, True)
            states(NB - 1, True, False)
            for k in (2, 1):
                add_up(NB * NS - k, NS - k)
            pe.wait_ge(yg_set, NB)
            project_out(NB - 1)
            turn_normed(NB - 1)
            route_out(NB - 1)
            moe(1)

        @block.scalar
        def _(act):
            A = nc.scalar.activation
            steps = Steps(act, act_step)

            def cp(dst, src, **kw):
                return A(dst, src, ACT.Copy, **kw)

            act.wait_ge(w_ps, 1)
            cp(wqk[:, :], bank(5, P)).then_inc(w_set, 1)
            act.wait_ge(w_ps, 2)
            cp(wvo[:, :], bank(6, P)).then_inc(w_set, 1)

            def project(b):
                act.wait_ge(xbT_ps, b + 1)
                cp(xbT, bank(6)).then_inc(xbT_set, 1)

            def values(b):
                act.wait_ge(v_ps, b + 1)
                cp(v_all[:, ds(b * S, S)], bank(6)).then_inc(v_set, 1)

            def router(l, b, k=5):
                act.wait_ge(*nT_ps[l].at(b + 1))
                cp(normT[:, :], bank(k)).then_inc(nT_set[l].sem, 1)

            def attend(b, first, final):
                def soften(q):
                    act.wait_ge(nmax_set, b * QT + (q + 1))
                    A(probs[:, q, :], bank(q), ACT.Exp, bias=nmx[:, q:q + 1], scale=SCALE,
                      accum_out=rs[:, q:q + 1]).then_inc(probs_set, 1)

                for q in range(QT - 1):
                    soften(q)
                if not final:
                    project(b + 1)
                soften(QT - 1)
                if not final:
                    values(b + 1)
                for q in range(QT):
                    act.wait_ge(pT_ps, b * QT + (q + 1))
                    cp(pT[q % 2], bank(7)).then_inc(pT_set, 1)
                if not first:
                    router(0, b - 1)

            project(0)
            values(0)
            attend(0, True, False)
            act.dma_start(w1[:], a["w1"]).then_inc(ld_f0, 16)
            with act.Fori(1, NB - 1) as b:
                attend(b, False, False)
            act.dma_start(w2[:], a["w2"]).then_inc(ld_f0, 16)
            attend(NB - 1, False, True)
            router(0, NB - 1)

            def moe(l):
                def exp_gaps():
                    act.wait_ge(*gap_set[l].at(1))
                    A(egap[:, :], gap[:, :], ACT.Exp).then_inc(egap_set[l].sem, 1)
                    if l:
                        act.wait_ge(*gap_set[l].at(2))
                        A(sc[:, :, :], l2[:, :, :], ACT.Exp).then_inc(egap_set[l].sem, 1)

                def step(m, k):
                    i = m * 4 + k
                    h, t, y = i + 1, i, i - 1
                    if isinstance(m, int) and i == EGAP_STEP:
                        exp_gaps()
                    if valid(h):
                        p = (k + 1) % 2
                        act.wait_ge(*h_ps[l].at(h + 1))
                        wait_pos(act, hs_set[l], h - 1)
                        A(th[p], bank(4 + p), ACT.Tanh, scale=0.5).then_inc(th_set[l].sem, 1)
                    if valid(t):
                        p = k % 2
                        act.wait_ge(*hT_ps[l].at(t + 1))
                        wait_pos(act, y_ps[l], t - 1)
                        cp(hT[p], bank(2 + p)).then_inc(hT_set[l].sem, 1)
                    if valid(y):
                        q = (k - 1) % 4
                        act.wait_ge(*y_ps[l].at(y + 1))
                        if isinstance(y, int) and y < NT + 4:
                            wait_pos(act, ys_stored[l][q], y // 4 * 16)
                        else:
                            wait_pos(act, ys_sent[l][q], (m + ((k - 1) // 4 - NT // 4)) * 16)
                        A(yout[q][:, :], bank(1, D), ACT.Copy, scale=0.5).then_inc(yout_set[l].sem, 1)
                        if isinstance(y, int) and y < NT:
                            act.wait_ge(*yout_set[l].at(y + 1))
                            act.dma_start(y_shared[y * P:(y + 1) * P, :], yout[q][:, :]).then_inc(ys_stored[l][q].sem, 16)

                slot_steps(act.Fori(0, LOOP_TRIPS), step)

                if l:
                    for g in range(2):
                        deviate(l, g)

            def deviate(l, g):
                first, end = GROUPS[l][g]
                act.wait_ge(*var_set[l].at(g + 1))
                A(srt[:, first * QT:end * QT], all_mv[:, first * QT:end * QT, 1], ACT.Sqrt).then_inc(std_set[l].sem, 1)

            def squares(b):
                act.wait_ge(*layer_out[0].at(b + 1))
                for q in range(QT):
                    last = A(tile_of(shared, b * QT + q), x_tile(b * QT + q), ACT.Square, scale=D ** -0.5,
                             accum_out=ssq[:, b * QT + q:b * QT + q + 1])
                last.then_inc(ssq_set, 1)

            moe(0)

            act.wait_ge(ld_ss, 160)
            A(a_neg[:, :], a_log[:, :], ACT.Exp).then_inc(a_set, 1)

            def scale_rows(x):
                for q in range(QT):
                    last = A(xn[:, q, :], x_tile(x * QT + q), ACT.Copy, scale=rms[:, ds(x * QT + q, 1)])
                last.then_inc(xn_set, 1)

            def take_xnT(x):
                act.wait_ge(xn_ps, x + 1)
                A(xnT, bank(5), ACT.Copy, scale=norm_w[:, 0:1]).then_inc(xnT_set, 1)

            def take_xi(x):
                for h in range(EH):
                    act.wait_ge(xi_ps, x * EH + (h + 1))
                    cp(xi[:, h, KC - 1:KC - 1 + S], bank(5 - h)).then_inc(xi_set, 1)

            def tanh_conv(x, h):
                act.wait_ge(conv_ps, x * EH + (h + 1))
                A(u1[:, h, :], bank(5 - h), ACT.Tanh).then_inc(conv_th, 1)

            def take_dt_low(x):
                act.wait_ge(dtl_ps, x + 1)
                cp(dts, ps[0:DTR, 5, :]).then_inc(dts_set, 1)

            def soft_parts(x):
                act.wait_ge(dl_ps, x + 1)
                act.wait_ge(xa_set, x * EH + EH)
                for h in range(EH):
                    steps.mark(A(u1[:, h, :], bank(4 + h), ACT.Abs, bias=b_dt[:, h:h + 1]))
                for h in range(EH):
                    last = A(u3[:, h, :], bank(4 + h), ACT.Relu, bias=b_dt[:, h:h + 1])
                last.then_inc(soft_abs, 1)
                act.wait_ge(act_step, steps.n)
                A(u2, u1, ACT.Exp, scale=-1.0).then_inc(soft_exp, 1)

            def take_hi(x):
                act.wait_ge(bc_ps, x + 1)
                cp(hi[:, :], ps[0:3 * BC, 3, :]).then_inc(hi_set, 1)

            def soft_log(x):
                act.wait_ge(soft_exp, x + 1)
                A(u1, u2, ACT.Ln, bias=1.0).then_inc(soft_ln, 1)

            def tanh_z(b):
                for h in range(EH):
                    act.wait_ge(z_ps, b * EH + (h + 1))
                    A(u2[:, h, :], bank(3 + h), ACT.Tanh, scale=0.5).then_inc(z_th, 1)

            def keep(b):
                act.wait_ge(*normed_set[1].at(b + 1))
                cp(x_seq(b), normed[:, :, :]).then_inc(kept[1].sem, 1)

            def decay(n, j):
                if not isinstance(n, int) or n >= 2:
                    act.wait_ge(st_set, n - 1)
                for h in range(EH):
                    lo = 1 if h else 0
                    last = A(dA[j % 2][:, h, lo:S], delta[:, h, lo:S], ACT.Exp, scale=a_neg[:, j + h * NS:j + h * NS + 1])
                last.then_inc(dA_set, 1)

            def take_c(n, j):
                act.wait_ge(c_ps, n + 1)
                if not isinstance(n, int) or n >= 2:
                    act.wait_ge(hc_set, n - 1)
                cp(cc[j % 2], bank(2)).then_inc(cc_set, 1)

            def states(b, after, before):
                act.wait_ge(delta_set, b + 1)
                decay(b * NS, 0)
                for j in range(NS):
                    if j < NS - 1:
                        decay(b * NS + (j + 1), j + 1)
                    take_c(b * NS + j, j)
                    if j == 0 and before:
                        scale_rows(b + 1)
                    if j == 1:
                        tanh_z(b)
                    if after:
                        if j == 7:
                            keep(b - 1)
                        if j == 8:
                            router(1, b - 1, 3)
                    if before:
                        if j == 1:
                            take_xnT(b + 1)
                        if j == 3:
                            take_xi(b + 1)
                        if j == 5:
                            tanh_conv(b + 1, 0)
                        if j == 7:
                            tanh_conv(b + 1, 1)
                        if j == 9:
                            take_dt_low(b + 1)
                        if j == 10:
                            soft_parts(b + 1)
                        if j == 12:
                            take_hi(b + 1)
                        if j == 12:
                            soft_log(b + 1)

            deviate(0, 0)
            squares(0)
            act.wait_ge(rms_set, 1)
            scale_rows(0)
            take_xnT(0)
            take_xi(0)
            deviate(0, 1)
            for h in range(EH):
                tanh_conv(0, h)
            take_dt_low(0)
            soft_parts(0)
            soft_log(0)
            take_hi(0)
            for b in range(1, NB):
                squares(b)
            act.wait_ge(rms_set, 2)
            states(0, False, True)
            with steps.loop(1, NB - 1, EH) as b:
                states(b, True, True)
            states(NB - 1, True, False)
            router(1, NB - 1, 3)
            keep(NB - 1)
            moe(1)

        @block.vector
        def _(dve):
            V = nc.vector
            steps = Steps(dve, dve_step)
            link = steps.link

            def take_qm(b):
                dve.wait_ge(qm_ps, b + 1)
                V.tensor_copy(qmT, bank(5)).then_inc(qmT_set, 1)

            def take_logits(l, b, k=6):
                dve.wait_ge(*logit_ps[l].at(b + 1))
                V.tensor_copy(logits[:].rearrange("p t e -> p (t e)")[:, ds(b * QT * NE, QT * NE)],
                              ps[:, k, 0:QT * NE]).then_inc(logits_set[l].sem, 1)

            def norm_stats(done):
                for q in range(QT):
                    steps.mark(V.bn_stats(stats[:, q, :], pre[:, q, :]))
                dve.wait_ge(dve_step, steps.n)
                V.tensor_copy(stats_n[:, :], stats[:, :, 0])
                for q in range(QT - 1):
                    V.bn_aggr(mv[:, q, :], stats[:, q, :])
                done(V.bn_aggr(mv[:, QT - 1, :], stats[:, QT - 1, :]))

            NORM_STEPS = QT

            def norm_apply(l, b):
                dve.wait_ge(*rstd_set[l].at(b + 1))
                for q in range(QT):
                    last = V.tensor_scalar(normed[:, q, :], pre[:, q, :], mv[:, q, 0:1], rstd[:, q:q + 1],
                                           ALU.subtract, ALU.mult)
                last.then_inc(normed_set[l].sem, 1)

            def reuse(l, b):
                dve.wait_ge(*xs_stored[l].at(b * 16 + 16))
                dve.wait_ge(*kept[l].at(b + 1))

            def attend_norm(b):
                dve.wait_ge(ctx_ps, b * QT + QT)
                for q in range(QT):
                    last = V.scalar_tensor_tensor(out=pre[:, q, :], in0=ps[:, 4, q * P:(q + 1) * P],
                                                  scalar=rinv[:, q:q + 1], in1=x_tile(b * QT + q),
                                                  op0=ALU.mult, op1=ALU.add)
                last.then_inc(ctx_added, 1)
                dve.wait_ge(ctx_added, b + 1)
                norm_stats(lambda ins: ins.then_inc(stats_set[0].sem, 1))
                norm_apply(0, b)

            ATT_NORM = NORM_STEPS

            def attend(b, first, final):
                for q in range(QT):
                    dve.wait_ge(scores_ps, b * QT + (q + 1))
                    link(V.reduce_max(mx[:, q:q + 1], bank(q), AXX))
                    V.tensor_scalar(nmx[:, q:q + 1], mx[:, q:q + 1], -SCALE, None, ALU.mult).then_inc(nmax_set, 1)
                if not final:
                    take_qm(b + 1)
                if not first:
                    attend_norm(b - 1)
                    take_logits(0, b - 1)
                    reuse(0, b - 1)
                dve.wait_ge(probs_set, b * QT + QT)
                link(V.reciprocal(rinv, rs))

            take_qm(0)
            dve.wait_ge(ld_x, 16)
            attend(0, True, False)
            with steps.loop(1, NB - 1, QT + 1 + ATT_NORM) as b:
                attend(b, False, False)
            attend(NB - 1, False, True)
            attend_norm(NB - 1)
            take_logits(0, NB - 1)

            dve.wait_ge(consts, 8)
            link(V.tensor_copy(rank8[:, :], rank8i[:, :]))
            link(V.tensor_copy(slot_row[:, :], slot_rowi[:, :]))
            link(V.memset(carry[:, :, :], 1.0))
            link(V.memset(carry[:, :, 0:1], 0.0))
            link(V.memset(slot_e[:, 0:NT], NE * HID))
            link(V.tensor_copy(token[:, :], tokeni[:, :]))
            link(V.tensor_scalar(token[:, :], token[:, :], -1.0 / T, float(BACK // T), ALU.mult, ALU.add))

            x_words = x_all[:].rearrange("p (t w) -> p t w", w=XW)[:, :, D:XW]

            def moe(l):
                tok_exp = [P, NT, NE]

                def over_e(ap):
                    return ap.unsqueeze(2).to_broadcast(tok_exp)

                def over_t(ap):
                    return ap.unsqueeze(1).to_broadcast(tok_exp)

                def routing():
                    dve.wait_ge(*logits_set[l].at(NB))
                    src = logits
                    for k in range(2):
                        link(V.reduce_max(mm[k][:, :], src[:, :, :], AXX))
                        link(V.tensor_tensor(eq[:, :, :], src[:, :, :], over_e(mm[k][:, :]), ALU.is_equal))
                        link(V.tensor_tensor(sc[:, :, :], eq[:, :, :], over_t(rank8[:, :]), ALU.mult))
                        link(V.reduce_max(ms[k][:, :], sc[:, :, :], AXX))
                        link(V.tensor_tensor(oh[k][:, :, :], sc[:, :, :], over_e(ms[k][:, :]), ALU.is_equal))
                        if k == 0:
                            link(V.scalar_tensor_tensor(out=l2[:, :, :].rearrange("p t e -> p (t e)"),
                                                        in0=oh[0][:, :, :].rearrange("p t e -> p (t e)"), scalar=NEVER,
                                                        in1=logits[:, :, :].rearrange("p t e -> p (t e)"),
                                                        op0=ALU.mult, op1=ALU.add))
                            src = l2
                        yield
                    V.tensor_tensor(mask[:, :, :], oh[0][:, :, :], oh[1][:, :, :], ALU.add).then_inc(mask_set[l].sem, 1)
                    V.tensor_tensor(gap[:, :], mm[1][:, :], mm[0][:, :], ALU.subtract).then_inc(gap_set[l].sem, 1)
                    if l:
                        V.tensor_tensor(l2[:, :, :], logits[:, :, :], over_e(mm[0][:, :]),
                                        ALU.subtract).then_inc(gap_set[l].sem, 1)
                    yield
                    dve.wait_ge(*count_ps[l].at(1))
                    link(V.tensor_copy(tot[:, :, :], tiles_ps.rearrange("p (t e) -> p e t", e=NE)))
                    V.tensor_copy(pos[:, :, :].rearrange("p t e -> p (t e)"), before_ps).then_inc(counts_taken[l].sem, 1)
                    yield
                    dve.wait_ge(*counts_taken[l].at(1))
                    flat = "p e t -> p (e t)"
                    link(V.tensor_tensor_scan(incl[:, :, :].rearrange(flat), carry[:, :, :].rearrange(flat),
                                              tot[:, :, :].rearrange(flat), 0.0, ALU.mult, ALU.add))
                    link(V.tensor_scalar(cnt_i[:, :], incl[:, :, NT - 1], float(P - 1), None, ALU.add))
                    link(V.tensor_scalar(cnt_i[:, :], cnt_i[:, :], 7, None, ALU.arith_shift_right))
                    yield
                    link(V.tensor_scalar(cnt[:, :], cnt_i[:, :], float(P), None, ALU.mult))
                    link(V.tensor_tensor_scan(ends[:, :], ones[:, 0:NE], cnt[:, :], 0.0, ALU.mult, ALU.add))
                    link(V.tensor_tensor(offs[:, :], ends[:, :], cnt[:, :], ALU.subtract))
                    link(V.tensor_tensor(incl[:, :, :], incl[:, :, :], tot[:, :, :], ALU.subtract))
                    link(V.tensor_tensor(pos[:, :, :], incl[:, :, :].rearrange("p e t -> p t e"),
                                         pos[:, :, :], ALU.add))
                    yield
                    link(V.tensor_tensor(pos[:, :, :], pos[:, :, :], over_t(offs[:, :]), ALU.add))
                    V.tensor_copy(x_words[:, :, 0], token[:, :])
                    V.tensor_copy(x_words[:, :, 1], ms[0][:, :])
                    for k in range(2):
                        link(V.tensor_tensor(posk[:, :, :], pos[:, :, :], oh[k][:, :, :], ALU.mult))
                        link(V.reduce_sum(posf[k][:, :], posk[:, :, :], AXX))
                        last = V.tensor_copy(rows[k][:, :], posf[k][:, :])
                        if k == 0:
                            link(last)
                    last.then_inc(rows_set[l].sem, 1)
                    yield
                    shp = [P, ROUTED, NE]
                    link(V.tensor_tensor(past[:, :, :], slot_row[:, :].unsqueeze(2).to_broadcast(shp),
                                         ends[:, :].unsqueeze(1).to_broadcast(shp), ALU.is_ge))
                    link(V.reduce_sum(slot_ef[:, :], past[:, :, :], AXX))
                    V.tensor_scalar(slot_m[:, NT:SLOTS], slot_ef[:, :], -1.0, float(NE), ALU.mult, ALU.add)
                    V.tensor_scalar(slot_e[:, NT:SLOTS], slot_ef[:, :], float(NE - 1), float(HID),
                                    ALU.min, ALU.mult).then_inc(rows_set[l].sem, 1)
                    yield
                    dve.wait_ge(*egap_set[l].at(1))
                    if l:
                        dve.wait_ge(*egap_set[l].at(2))
                        link(V.reduce_sum(zsum[:, :], sc[:, :, :], AXX))
                        link(V.tensor_scalar(zsum[:, :], zsum[:, :], 1e-8, 1.0, ALU.mult, ALU.add))
                        link(V.tensor_tensor(den[:, :], zsum[:, :], egap[:, :], ALU.add))
                    else:
                        link(V.tensor_scalar(den[:, :], egap[:, :], 1.0, None, ALU.add))
                    link(V.reciprocal(gates[0][:, :], den[:, :]))
                    link(V.tensor_tensor(gates[1][:, :], gates[0][:, :], egap[:, :], ALU.mult))
                    yield

                route = routing()

                def step(m, k):
                    i = m * 4 + k
                    x, h = i + 2, i + 1
                    if isinstance(m, int):
                        for _ in range({-2: 3, -1: 1, 0: 3}.get(i, 1)):
                            next(route, None)
                    if valid(x) and (not isinstance(x, int) or x >= NT):
                        q = (k + 2) % 4
                        dve.wait_ge(*xin_loaded[l][q].at((m + (k + 2) // 4 + 1) * 16))
                        link(V.scalar_tensor_tensor(out=choice[:, ds(x, 1)], in0=xin[q][:, D + 1:XW],
                                                    scalar=slot_m[:, ds(x, 1)], in1=xin[q][:, D:D + 1],
                                                    op0=ALU.is_equal, op1=ALU.add))
                        V.tensor_scalar(dest[:, ds(x, 1)], choice[:, ds(x, 1)], -float(T), float(BACK + T),
                                        ALU.mult, ALU.add)
                    if valid(x):
                        p = k % 2
                        dve.wait_ge(*x_ps[l].at(x + 1))
                        wait_pos(dve, h_ps[l], x - 1)
                        V.tensor_copy(xT[p][:, :], bank(0, P)).then_inc(xT_set[l].sem, 1)
                    if valid(h):
                        p = (k + 1) % 2
                        dve.wait_ge(*th_set[l].at(h + 1))
                        wait_pos(dve, hT_ps[l], h - 1)
                        if l:
                            link(V.scalar_tensor_tensor(out=ga[p], in0=th[p], scalar=1.0, in1=bank(4 + p),
                                                        op0=ALU.add, op1=ALU.mult))
                            V.tensor_tensor(hs[p], ga[p], bank(6 + p), ALU.mult).then_inc(hs_set[l].sem, 1)
                        else:
                            V.scalar_tensor_tensor(out=hs[p], in0=th[p], scalar=1.0, in1=bank(4 + p),
                                                   op0=ALU.add, op1=ALU.mult).then_inc(hs_set[l].sem, 1)

                slot_steps(steps.loop(0, LOOP_TRIPS, 4 * l + 4), step)

                if l:
                    for b in range(NB):
                        combine(l, b)
                        if b == NB // 2 - 1:
                            variances(l, 0)
                        if b == NB // 2:
                            norm_group(l, 0)
                    variances(l, 1)
                    norm_group(l, 1)

            def combine(l, b):
                own = [tile_of(shared, b * QT + q) for q in range(QT)]
                dve.wait_ge(*gathered[l][b % 2].at((b // 2 + 1) * 48))
                link(V.tensor_tensor(tiles(shared[:, b * S:(b + 1) * S]), x_seq(b),
                                     tiles(shared[:, b * S:(b + 1) * S]), ALU.add))
                for k in range(2):
                    for q in range(QT):
                        t = b * QT + q
                        steps.mark(V.scalar_tensor_tensor(out=own[q], in0=tile_of(y_k[k], t), scalar=gates[k][:, t:t + 1],
                                                          in1=own[q], op0=ALU.mult, op1=ALU.add))
                    dve.wait_ge(dve_step, steps.n)
                for q in range(QT):
                    steps.mark(V.bn_stats(all_stats[:, b * QT + q, :], own[q]))
                dve.wait_ge(dve_step, steps.n)
                for t in range(b * QT, b * QT + QT):
                    steps.mark(V.bn_aggr(all_mv[:, t, :], all_stats[:, t, :]))

            def variances(l, g):
                first, end = GROUPS[l][g]
                dve.wait_ge(dve_step, steps.n)
                v = all_mv[:, first * QT:end * QT, 1]
                V.tensor_scalar(v, v, LN_EPS, None, ALU.add).then_inc(var_set[l].sem, 1)

            def norm_group(l, g):
                first, end = GROUPS[l][g]
                dve.wait_ge(*std_set[l].at(g + 1))
                link(V.reciprocal(inv[:, first * QT:end * QT], srt[:, first * QT:end * QT]))
                for b in range(first, end):
                    for t in range(b * QT, b * QT + QT):
                        last = V.tensor_scalar(x_tile(t), tile_of(shared, t), all_mv[:, t, 0:1], inv[:, t:t + 1],
                                               ALU.subtract, ALU.mult)
                    last.then_inc(layer_out[l].sem, 1)

            moe(0)
            reuse(0, NB - 1)

            dve.wait_ge(a_set, 1)
            dve.wait_ge(xs_zeroed, 16 * (1 + ROUTED // CLEAR))
            link(V.tensor_scalar(a_neg[:, :], a_neg[:, :], -1.0, None, ALU.mult))
            link(V.memset(xi[:, :, 0:KC - 1], 0.0))
            link(V.memset(dA[0][:, 1, 0:1], 0.0))
            V.memset(dA[1][:, 1, 0:1], 0.0).then_inc(a_set, 1)

            def activate(x, h):
                dve.wait_ge(conv_th, x * EH + (h + 1))
                V.scalar_tensor_tensor(out=xa[:, h, :], in0=u1[:, h, :], scalar=1.0, in1=bank(5 - h),
                                       op0=ALU.add, op1=ALU.mult).then_inc(xa_set, 1)

            def one_plus(x):
                dve.wait_ge(soft_exp, x + 1)
                V.tensor_scalar(one_w, u2, 1.0, -1.0, ALU.add, ALU.add).then_inc(fix_mid, 1)

            def split_bc(x):
                dve.wait_ge(hi_set, x + 1)
                link(V.tensor_tensor(res[0:3 * BC, :], ps[0:3 * BC, 3, :], hi[:, :], ALU.subtract))
                link(V.tensor_copy(mid[:, :], res[0:3 * BC, :]))

            def soft_sum(x):
                dve.wait_ge(soft_ln, x + 1)
                link(V.tensor_tensor(u3, u3, u1, ALU.add))

            def hand_over(x):
                if not isinstance(x, int) or x > 0:
                    dve.wait_ge(c_ps, x * NS)
                V.tensor_copy(parts[0:BC, :], hi[0:BC, :])
                V.tensor_copy(parts[BC:2 * BC, :], mid[BC:2 * BC, :])
                V.tensor_tensor(parts[2 * BC:3 * BC, :], res[2 * BC:3 * BC, :], mid[2 * BC:3 * BC, :],
                                ALU.subtract).then_inc(parts_set, 1)
                dve.wait_ge(soft_fix, x + 1)
                if not isinstance(x, int) or x > 0:
                    dve.wait_ge(dA_set, x * NS)
                V.tensor_tensor(delta, u3, u2, ALU.add).then_inc(delta_set, 1)

            def weigh_input(x):
                dve.wait_ge(delta_set, x + 1)
                link(V.tensor_tensor(du, delta, xa, ALU.mult))

            def activate_z(b):
                if not isinstance(b, int) or b > 0:
                    dve.wait_ge(yg_set, b)
                for h in range(EH):
                    dve.wait_ge(z_th, b * EH + (h + 1))
                    V.scalar_tensor_tensor(out=zs[:, h, :], in0=u2[:, h, :], scalar=1.0, in1=bank(3 + h),
                                           op0=ALU.add, op1=ALU.mult).then_inc(zs_set, 1)

            def gate_sum(b):
                dve.wait_ge(y_sum, b * NS + NS)
                dve.wait_ge(zs_set, b * EH + EH)
                V.scalar_tensor_tensor(out=yg, in0=ps[:, 6:8, :], scalar=0.5, in1=zs,
                                       op0=ALU.mult, op1=ALU.mult).then_inc(yg_set, 1)

            def add_residual(b):
                dve.wait_ge(o_ps, b + 1)
                V.scalar_tensor_tensor(out=pre[:, :, :], in0=x_seq(b), scalar=2.0,
                                       in1=tiles(bank(3)), op0=ALU.mult, op1=ALU.add).then_inc(o_added, 1)
                dve.wait_ge(o_added, b + 1)
                norm_stats(lambda ins: ins.then_inc(stats_set[1].sem, 1))

            def state(n, j, between):
                dve.wait_ge(b_ps, n + 1)
                if not isinstance(n, int) or n >= 2:
                    dve.wait_ge(st_set, n - 1)
                V.tensor_tensor(dbu[j % 2], du, bank(j % 2).unsqueeze(1).to_broadcast([P, EH, S]), ALU.mult)\
                    .then_inc(dbu_set, 1)
                between()
                dve.wait_ge(dbu_set, n + 1)
                dve.wait_ge(dA_set, n + 1)
                if not isinstance(n, int) or n >= 2:
                    dve.wait_ge(hc_set, n - 1)
                V.tensor_tensor_scan(st[j % 2].rearrange("p h t -> p (h t)"),
                                     dA[j % 2].rearrange("p h t -> p (h t)"),
                                     dbu[j % 2].rearrange("p h t -> p (h t)"), 0.0,
                                     ALU.mult, ALU.add).then_inc(st_set, 1)

            def states(b, after, before):
                for j in range(NS):
                    def between():
                        if after:
                            if j == 1:
                                gate_sum(b - 1)
                            if j == 4:
                                add_residual(b - 1)
                            if j == 6:
                                if not isinstance(b, int) or b > 1:
                                    reuse(1, b - 2)
                                norm_apply(1, b - 1)
                            if j == 10:
                                take_logits(1, b - 1, 3)
                        if j == 2:
                            activate_z(b)
                        if before:
                            if j in (7, 9):
                                activate(b + 1, (j - 7) // 2)
                            if j == 12:
                                one_plus(b + 1)
                            if j == 13:
                                split_bc(b + 1)
                            if j == 14:
                                soft_sum(b + 1)
                            if j == 15:
                                hand_over(b + 1)

                    state(b * NS + j, j, between)
                if before:
                    weigh_input(b + 1)

            combine(0, 0)
            variances(0, 0)
            norm_group(0, 0)
            for b in range(1, NB):
                combine(0, b)
            variances(0, 1)
            for h in range(EH):
                activate(0, h)
            norm_group(0, 1)
            one_plus(0)
            split_bc(0)
            soft_sum(0)
            hand_over(0)
            weigh_input(0)
            states(0, False, True)
            states(1, True, True)
            with steps.loop(2, NB - 1, NORM_STEPS + 4) as b:
                states(b, True, True)
            states(NB - 1, True, False)
            gate_sum(NB - 1)
            add_residual(NB - 1)
            reuse(1, NB - 2)
            norm_apply(1, NB - 1)
            take_logits(1, NB - 1, 3)
            moe(1)

        @block.gpsimd
        def _(pool):
            G = nc.gpsimd
            steps = Steps(pool, pool_step)
            link = steps.link

            link(G.memset(ident[:, :], 0.0))
            G.affine_select(out=ident[:, :], in_=ident[:, :], compare_op=ALU.not_equal, fill=1.0, base=0,
                            pattern=[[-1, P]], channel_multiplier=1).then_inc(consts, 1)
            G.memset(ones[:, :], 1.0).then_inc(consts, 1)
            pool.wait_ge(consts, 2)
            G.affine_select(out=before[:, :], in_=ones[:, :], compare_op=ALU.is_gt, fill=0.0, base=0,
                            pattern=[[1, P]], channel_multiplier=-1).then_inc(consts, 1)
            link(G.memset(half[:, :], -0.5))
            link(G.memset(eps[:, 0, :], LN_EPS))
            G.memset(eps[:, 1, :], RMS_EPS).then_inc(consts, 1)
            G.memset(zero, 0.0).then_inc(zero_set, 1)
            sel3 = sel[:].rearrange("r (j m) -> r j m", m=P)
            link(G.memset(sel[:], 0.0))
            for g in range(2):
                link(G.affine_select(out=sel3, in_=sel3, compare_op=ALU.not_equal, fill=1.0,
                                     base=-g * BC, pattern=[[-1, BC], [0, P]], channel_multiplier=1))
            G.affine_select(out=sel3, in_=sel3, compare_op=ALU.not_equal, fill=1.0,
                            base=-2 * BC, pattern=[[-1, BC], [0, P]], channel_multiplier=1).then_inc(consts, 1)
            G.iota(rank8i[:, :], pattern=[[-1, NE]], base=NE, channel_multiplier=0).then_inc(consts, 1)
            G.iota(tokeni[:, :], pattern=[[P, NT]], base=0, channel_multiplier=1).then_inc(consts, 1)
            G.iota(slot_rowi[:, :], pattern=[[P, ROUTED]], base=0, channel_multiplier=0).then_inc(consts, 1)
            def diagonals():
                pool.wait_ge(ld_ss, 160)
                link(G.tensor_scalar(conv[:, :, :], conv[:, :, :], 0.5, None, ALU.mult))
                for h in range(EH):
                    for k in range(KC):
                        G.tensor_scalar(diag[:, h * KC + k, :], ident[:, :], conv[:, h, k:k + 1], None, ALU.mult)\
                            .then_inc(diag_set, 1)
                    G.tensor_scalar(d_diag[h][:, :], ident[:, :], d_par[:, h:h + 1], None, ALU.mult)\
                        .then_inc(diag_set, 1)

            def inverse_std(l, b):
                pool.wait_ge(*stats_set[l].at(b + 1))
                link(G.tensor_tensor(mv[:, :, 1], mv[:, :, 1], eps[:, 0, 0:QT], ALU.add))
                G.tensor_tensor(rstd[:, :], mv[:, :, 1], half[:, 0:QT], ALU.pow).then_inc(rstd_set[l].sem, 1)

            def clear_rows(l, lo, hi):
                pool.dma_start(xs[l].rearrange("(p c) w -> p (c w)", p=P)[:, lo * XW:hi * XW],
                               zero[:, lo * XW:hi * XW]).then_inc(xs_zeroed, 16)

            def norm_attention():
                def one(b):
                    inverse_std(0, b)
                    pool.wait_ge(*normed_set[0].at(b + 1))
                    G.tensor_copy(x_seq(b), normed[:, :, :]).then_inc(kept[0].sem, 1)

                one(0)
                pool.wait_ge(zero_set, 1)
                clear_rows(0, 0, ROUTED)
                with steps.loop(1, NB, 1) as b:
                    one(b)

            def inverse_rms(g):
                first, end = GROUPS[0][g]
                own = slice(first * QT, end * QT)
                pool.wait_ge(ssq_set, end)
                G.tensor_tensor(ssq[:, own], ssq[:, own], eps[:, 1, own], ALU.add).then_inc(rms_mid, 1)
                pool.wait_ge(rms_mid, g + 1)
                G.tensor_tensor(rms[:, own], ssq[:, own], half[:, own], ALU.pow).then_inc(rms_set, 1)

            def lost_part(x):
                pool.wait_ge(soft_exp, x + 1)
                pool.wait_ge(fix_mid, x + 1)
                pool.wait_ge(soft_ln, x + 1)
                G.tensor_tensor(u2, u2, one_w, ALU.subtract).then_inc(soft_fix, 1)

            def states(b, after, before):
                for j in range(NS):
                    n = b * NS + j
                    pool.wait_ge(st_set, n + 1)
                    pool.wait_ge(cc_set, n + 1)
                    if not isinstance(n, int) or n >= 4:
                        pool.wait_ge(y_sum, n - 3)
                    G.tensor_tensor(hc[j % 4], st[j % 2],
                                    cc[j % 2].unsqueeze(1).to_broadcast([P, EH, S]), ALU.mult).then_inc(hc_set, 1)
                    if j == 4 and after:
                        inverse_std(1, b - 1)
                    if j == 13 and before:
                        lost_part(b + 1)

            def state_space():
                inverse_rms(0)
                lost_part(0)
                inverse_rms(1)
                states(0, False, True)
                with steps.loop(1, NB - 1, 1) as b:
                    states(b, True, True)
                states(NB - 1, True, False)
                inverse_std(1, NB - 1)

            def moe(l):
                pool.wait_ge(*rows_set[l].at(1))
                pool.wait_ge(*kept[l].at(NB))
                pool.wait_ge(xs_zeroed, 16 * (1 + l * ROUTED // CLEAR))
                for t in range(NT):
                    for k in range(2):
                        G.indirect_dma_start(out=xs[l], out_offset=bass.IndirectOffsetOnAxis(ap=rows[k][:, t:t + 1], axis=0),
                                             in_=x_all[:, t * XW:(t + 1) * XW], in_offset=None).then_inc(scattered[l].sem, 16)
                if l == 0:
                    diagonals()
                for y in range(NT, SLOTS):
                    if l == 0 and (y - NT) % CLEAR == 0:
                        clear_rows(1, y - NT, y - NT + CLEAR)
                    pool.wait_ge(*yout_set[l].at(y + 1))
                    G.indirect_dma_start(out=y_choice, out_offset=bass.IndirectOffsetOnAxis(ap=dest[:, y:y + 1], axis=0),
                                         in_=yout[y % 4][:, :], in_offset=None, bounds_check=2 * T - 1,
                                         oob_is_err=False).then_inc(ys_sent[l][y % 4].sem, 16)

            norm_attention()
            moe(0)
            state_space()
            moe(1)


def kernel(**inputs):
    import concourse.bacc as bacc
    from concourse.bass_utils import run_bass_kernel_spmd

    a = {k: np.asarray(v) for k, v in inputs.items()}
    put = {"x": a["L0_attn_x"].reshape(T, D)}
    qkv = a["L0_attn_W_qkv"].reshape(D, 3, D)
    put["wq"], put["wk"], put["wv"] = qkv[:, 0], qkv[:, 1], qkv[:, 2]
    put["woT"] = a["L0_attn_W_out"].T
    up = lambda w, shared: np.concatenate([w, shared[None]]).transpose(1, 0, 2).reshape(D, -1)
    down = lambda w, shared: (np.concatenate([w, shared[None]]).reshape(NE + 1, HB, P, D)
                              .transpose(2, 0, 1, 3).reshape(P, -1))
    put["gate0"] = a["L0_ffn_gate_w"].T
    put["w1"] = up(a["L0_ffn_experts_w1"].transpose(0, 2, 1), a["L0_ffn_shared_w1"].T)
    put["w2"] = down(a["L0_ffn_experts_w2"].transpose(0, 2, 1), a["L0_ffn_shared_w2"].T)
    put["gate1"] = a["L1_ffn_w_router"]
    put["wg"] = up(a["L1_ffn_w_gate"], a["L1_ffn_ws_gate"])
    put["wu"] = up(a["L1_ffn_w_up"], a["L1_ffn_ws_up"])
    put["wd"] = down(a["L1_ffn_w_down"], a["L1_ffn_ws_down"])
    halves = lambda w: w.reshape(EH, P, -1).transpose(1, 0, 2)
    put["norm_w"] = a["L1_attn_norm_w"].reshape(P, 1)
    put["w_in"] = a["L1_attn_W_in"]
    put["conv"] = halves(a["L1_attn_conv_w"])
    w_x = halves(a["L1_attn_W_x"])
    put["w_dtl"] = w_x[:, :, :DTR]
    put["w_bc3"] = np.concatenate([w_x[:, :, DTR:]] * 3, axis=2)
    put["w_dt"] = a["L1_attn_W_dt"]
    put["b_dt"] = halves(a["L1_attn_b_dt"]).reshape(P, EH)
    put["a_log"] = halves(a["L1_attn_A_log"]).reshape(P, EH * NS)
    put["d_par"] = halves(a["L1_attn_D_param"]).reshape(P, EH)
    put["w_out"] = halves(a["L1_attn_W_out"])
    put = {k: np.ascontiguousarray(v) for k, v in put.items()}

    nc = bacc.Bacc("TRN2", target_bir_lowering=False, num_devices=1)
    args = {k: nc.dram_tensor(f"in_{k}", v.shape, mybir.dt.from_np(v.dtype), kind="ExternalInput").ap()
            for k, v in put.items()}
    out = nc.dram_tensor("out", (T, D), F32, kind="ExternalOutput").ap()
    build(nc, args, out)
    r = run_bass_kernel_spmd(nc, [{f"in_{k}": v for k, v in put.items()}], core_ids=[0])
    return r.results[0]["out"].reshape(NB, S, D)
```
